# Optimizing a Trainium2 kernel written in Bass

```python
import numpy as np
import jax
import jax.numpy as jnp

def _softmax(x, axis=-1):
    return jax.nn.softmax(x, axis=axis)

def _gelu(x):
    return jax.nn.gelu(x, approximate=True)

def _silu(x):
    return jax.nn.silu(x)

def _sigmoid(x):
    return jax.nn.sigmoid(x)

def _layernorm(x, axis=-1, eps=1e-05):
    m = jnp.mean(x, axis=axis, keepdims=True)
    v = jnp.var(x, axis=axis, keepdims=True)
    return (x - m) / jnp.sqrt(v + eps)

def _scatter_add(tgt, idx, src, axis=0):
    return tgt.at[idx].add(src)

def _segment_sum(src, seg, n):
    return jax.ops.segment_sum(src, seg, n)
kernel_name = 'mk_vit_tower_postln_d4_tok_img256_r4_f0d338'

def setup_inputs(seed: int=0):
    np.random.seed(seed)
    _w = jnp.asarray

    def _rec_inputs():
        import jax
        import jax.numpy as jnp
        _rk = jax.random.key(seed)
        x = -0.0003702 + 0.999946 * jax.random.normal(jax.random.fold_in(_rk, 1), (64, 1, 224, 224), jnp.float32)
        return x
    x = _rec_inputs()

    def _L0_tok_setup():
        import jax, jax.numpy as jnp
        import numpy as np
        PH, PW = (64, 25)
        SH, SW = (64, 12)

        def _unfold(x, ph, pw, sh, sw):
            B, C, H, W = x.shape
            nh = (H - ph) // sh + 1
            nw = (W - pw) // sw + 1
            rows = jnp.arange(nh)[:, None] * sh + jnp.arange(ph)[None, :]
            cols = jnp.arange(nw)[:, None] * sw + jnp.arange(pw)[None, :]
            p = x[:, :, rows, :]
            p = p[:, :, :, :, cols]
            p = jnp.transpose(p, (0, 2, 4, 1, 3, 5))
            return p.reshape(B, nh * nw, C * ph * pw)
        key = jax.random.key(seed)
        kx, kw = jax.random.split(key, 2)
        x = jax.random.normal(kx, (64, 1, 64, 1000), dtype=jnp.float32)
        in_dim = 1 * PH * PW
        weight = jax.random.normal(kw, (in_dim, 64), dtype=jnp.float32) / np.sqrt(in_dim).astype(np.float32)
        bias = jnp.zeros((64,), dtype=jnp.float32)
        return {'x': x, 'weight': weight, 'bias': bias}
    _L0_tok_all = _L0_tok_setup()
    _L0_tok_in = {k: v for k, v in _L0_tok_all.items() if k in ('weight', 'bias')}
    del _L0_tok_all

    def _L0_attn_setup():
        import jax, jax.numpy as jnp
        import numpy as np
        import math
        B, S, D = (4, 1024, 64)
        key = jax.random.key(seed)
        ks = jax.random.split(key, 9)
        s = 1.0 / math.sqrt(D)
        return {'src': jax.random.normal(ks[0], (B, S, D), dtype=jnp.float32), 'Wq': jax.random.normal(ks[1], (D, D), dtype=jnp.float32) * s, 'bq': jax.random.normal(ks[2], (D,), dtype=jnp.float32) * s, 'Wk': jax.random.normal(ks[3], (D, D), dtype=jnp.float32) * s, 'bk': jax.random.normal(ks[4], (D,), dtype=jnp.float32) * s, 'Wv': jax.random.normal(ks[5], (D, D), dtype=jnp.float32) * s, 'bv': jax.random.normal(ks[6], (D,), dtype=jnp.float32) * s, 'Wo': jax.random.normal(ks[7], (D, D), dtype=jnp.float32) * s, 'bo': jax.random.normal(ks[8], (D,), dtype=jnp.float32) * s}
    _L0_attn_all = _L0_attn_setup()
    _L0_attn_in = {k: v for k, v in _L0_attn_all.items() if k in ('Wq', 'bq', 'Wk', 'bk', 'Wv', 'bv', 'Wo', 'bo')}
    del _L0_attn_all

    def _L0_ffn_setup():
        import jax, jax.numpy as jnp
        import numpy as np
        B, N, D = (16, 1024, 64)
        NUM_EXPERTS, TOP_K, HEADS = (4, 2, 4)
        N_EDGES = 262144
        LN_EPS = 1e-05

        def _layernorm(x, g, b):
            mu = x.mean(-1, keepdims=True)
            var = ((x - mu) ** 2).mean(-1, keepdims=True)
            return (x - mu) * jax.lax.rsqrt(var + LN_EPS) * g + b

        def _forward(x, edge_index, W_gat, att_src, att_dst, b_gat, ln_gamma, ln_beta, W1, b1, W2, b2):
            Bc, Nc, Dc = x.shape
            M = Bc * Nc
            x_flat = x.reshape(M, Dc)
            h = (x_flat @ W_gat).reshape(M, HEADS, NUM_EXPERTS)
            loops = jnp.arange(M, dtype=edge_index.dtype)
            src = jnp.concatenate([edge_index[0], loops])
            dst = jnp.concatenate([edge_index[1], loops])
            a_src = (h * att_src).sum(-1)
            a_dst = (h * att_dst).sum(-1)
            e = jax.nn.leaky_relu(a_src[src] + a_dst[dst], negative_slope=0.2)
            e_max = jax.ops.segment_max(e, dst, num_segments=M)
            ee = jnp.exp(e - e_max[dst])
            denom = jax.ops.segment_sum(ee, dst, num_segments=M)
            alpha = ee / (denom[dst] + 1e-16)
            msg = h[src] * alpha[:, :, None]
            agg = jax.ops.segment_sum(msg, dst, num_segments=M).reshape(M, HEADS * NUM_EXPERTS) + b_gat
            scores = _layernorm(agg, ln_gamma, ln_beta).reshape(M, HEADS, NUM_EXPERTS).mean(1)
            scores = scores.reshape(Bc, Nc, NUM_EXPERTS)
            topk_s, topk_i = jax.lax.top_k(scores, TOP_K)
            w = jax.nn.softmax(topk_s, axis=-1)
            out = jnp.zeros_like(x)
            for ei in range(NUM_EXPERTS):
                g = jnp.where(topk_i == ei, w, 0.0).sum(-1)
                hh = jax.nn.gelu(x @ W1[ei] + b1[ei], approximate=False)
                out = out + g[..., None] * (hh @ W2[ei] + b2[ei])
            return out
        key = jax.random.key(seed)
        ks = jax.random.split(key, 8)
        s = 0.05
        return {'x': jax.random.normal(ks[0], (B, N, D), jnp.float32), 'W_gat': jax.random.normal(ks[1], (D, HEADS * NUM_EXPERTS), jnp.float32) * s, 'att_src': jax.random.normal(ks[2], (HEADS, NUM_EXPERTS), jnp.float32) * s, 'att_dst': jax.random.normal(ks[3], (HEADS, NUM_EXPERTS), jnp.float32) * s, 'b_gat': jnp.zeros((HEADS * NUM_EXPERTS,), jnp.float32), 'ln_gamma': jnp.ones((HEADS * NUM_EXPERTS,), jnp.float32), 'ln_beta': jnp.zeros((HEADS * NUM_EXPERTS,), jnp.float32), 'W1': jax.random.normal(ks[4], (NUM_EXPERTS, D, 2 * D), jnp.float32) * s, 'b1': jnp.zeros((NUM_EXPERTS, 2 * D), jnp.float32), 'W2': jax.random.normal(ks[5], (NUM_EXPERTS, 2 * D, D), jnp.float32) * s, 'b2': jnp.zeros((NUM_EXPERTS, D), jnp.float32), 'edge_index': jax.random.randint(ks[6], (2, N_EDGES), 0, B * N, jnp.int32)}
    _L0_ffn_all = _L0_ffn_setup()
    _L0_ffn_in = {k: v for k, v in _L0_ffn_all.items() if k in ('W_gat', 'att_src', 'att_dst', 'b_gat', 'ln_gamma', 'ln_beta', 'W1', 'b1', 'W2', 'b2', 'edge_index')}
    del _L0_ffn_all

    def _L1_attn_setup():
        import jax, jax.numpy as jnp
        import numpy as np
        B_SZ, T, N, H = (8, 1024, 64, 128)
        RMAX, RMIN = (0.99, 0.4)

        def _glorot_half(k, shape):
            fan_avg = (shape[0] + shape[1]) / 2.0
            limit = float(np.sqrt(3.0 * 0.5 / fan_avg))
            return jax.random.uniform(k, shape, jnp.float32, -limit, limit)

        def _binary_op(qi, qj):
            A_i, b_i = qi
            A_j, b_j = qj
            return (A_j * A_i, A_j * b_i + b_j)
        key = jax.random.key(seed)
        ks = jax.random.split(key, 8)
        x = jax.random.normal(ks[0], (B_SZ, T, N), jnp.float32)
        C_re = _glorot_half(ks[1], (H, N))
        C_im = _glorot_half(ks[2], (H, N))
        B_re = _glorot_half(ks[3], (N, H))
        B_im = _glorot_half(ks[4], (N, H))
        D = jax.random.normal(ks[5], (N,), jnp.float32)
        numin = float(np.log(-np.log(RMAX)))
        numax = float(np.log(-np.log(RMIN)))
        nu = jax.random.uniform(ks[6], (H,), jnp.float32, numin, numax)
        theta = jax.random.uniform(ks[7], (H,), jnp.float32, 0.0, 3.14 / 10)
        lam_abs = jnp.exp(-jnp.exp(nu))
        gamma_log = jnp.log(jnp.sqrt(1.0 - lam_abs ** 2))
        return dict(x=x, B_re=B_re, B_im=B_im, C_re=C_re, C_im=C_im, D=D, nu=nu, theta=theta, gamma_log=gamma_log)
    _L1_attn_all = _L1_attn_setup()
    _L1_attn_in = {k: v for k, v in _L1_attn_all.items() if k in ('B_re', 'B_im', 'C_re', 'C_im', 'D', 'nu', 'theta', 'gamma_log')}
    del _L1_attn_all

    def _L1_ffn_setup():
        import jax, jax.numpy as jnp
        import numpy as np
        C = 64
        HID = 256
        E = 8
        TEMP = 1.0
        key = jax.random.key(seed)
        ks = jax.random.split(key, 7)
        x = jax.random.normal(ks[0], (8, 4096, C), dtype=jnp.float32)
        W1 = jax.random.normal(ks[1], (C, HID), dtype=jnp.float32) * 0.02
        b1 = jnp.zeros((HID,), dtype=jnp.float32)
        Wg = jax.random.normal(ks[2], (HID, E), dtype=jnp.float32) * 0.02
        bg = jnp.zeros((E,), dtype=jnp.float32)
        Wd = jax.random.normal(ks[3], (E, HID, C), dtype=jnp.float32) * 0.02
        bd = jnp.zeros((E, C), dtype=jnp.float32)
        return {'x': x, 'W1': W1, 'b1': b1, 'Wg': Wg, 'bg': bg, 'Wd': Wd, 'bd': bd}
    _L1_ffn_all = _L1_ffn_setup()
    _L1_ffn_in = {k: v for k, v in _L1_ffn_all.items() if k in ('W1', 'b1', 'Wg', 'bg', 'Wd', 'bd')}
    del _L1_ffn_all

    def _L2_attn_setup():
        import jax, jax.numpy as jnp
        import numpy as np
        NUM_HEADS = 8

        def _to_heads(y, R, C, H, hd):
            y = y.reshape(R, C, H, hd).transpose(0, 2, 1, 3)
            y = jnp.transpose(y, (2, 1, 0, 3)).reshape(1, H, C, R * hd)
            return y

        def _reference_tuple_inner(x, Wq, bq, Wk, bk, Wv, bv):
            R, C, E = x.shape
            H = NUM_HEADS
            hd = E // H
            q = _to_heads(x @ Wq.T + bq, R, C, H, hd)
            k = _to_heads(x @ Wk.T + bk, R, C, H, hd)
            v = _to_heads(x @ Wv.T + bv, R, C, H, hd)
            d = q.shape[-1]
            q = jax.nn.softmax(q, axis=-1)
            k = jax.nn.softmax(k, axis=-2)
            q = q * jnp.asarray(float(d) ** 0.5, dtype=q.dtype)
            attn_weights = jnp.einsum('bhnd,bhmd->bhnm', q, k).sum(0)
            context = jnp.einsum('bhnd,bhne->bhde', k, v)
            out = jnp.einsum('bhnd,bhde->hbne', q, context)
            out = out.reshape(H, C, R, hd)
            out = jnp.transpose(out, (2, 1, 0, 3)).reshape(R, C, E)
            return (out, attn_weights)
        key = jax.random.key(seed)
        ks = jax.random.split(key, 7)
        R, C, E = (16, 512, 64)
        x = jax.random.normal(ks[0], (R, C, E), dtype=jnp.float32)
        s = 0.02
        Wq = jax.random.normal(ks[1], (E, E), dtype=jnp.float32) * s
        bq = jax.random.normal(ks[2], (E,), dtype=jnp.float32) * s
        Wk = jax.random.normal(ks[3], (E, E), dtype=jnp.float32) * s
        bk = jax.random.normal(ks[4], (E,), dtype=jnp.float32) * s
        Wv = jax.random.normal(ks[5], (E, E), dtype=jnp.float32) * s
        bv = jax.random.normal(ks[6], (E,), dtype=jnp.float32) * s
        return {'x': x, 'Wq': Wq, 'bq': bq, 'Wk': Wk, 'bk': bk, 'Wv': Wv, 'bv': bv}
    _L2_attn_all = _L2_attn_setup()
    _L2_attn_in = {k: v for k, v in _L2_attn_all.items() if k in ('Wq', 'bq', 'Wk', 'bk', 'Wv', 'bv')}
    del _L2_attn_all

    def _L2_ffn_setup():
        import jax, jax.numpy as jnp
        import numpy as np
        B, T, IN_DIM = (64, 64, 64)
        HID, OUT_DIM = (128, 64)
        N_LAYERS, N_EXPERTS, N_SHARED = (2, 16, 1)
        key = jax.random.key(seed)
        ks = jax.random.split(key, 10)
        s = 0.02
        x = jax.random.normal(ks[0], (B, T, IN_DIM), dtype=jnp.float32)
        route_id = jax.random.randint(ks[1], (B,), 0, N_EXPERTS)
        Wi = jax.random.normal(ks[2], (HID, IN_DIM), dtype=jnp.float32) * s
        bi = jnp.zeros((HID,), dtype=jnp.float32)
        Wr = jax.random.normal(ks[3], (N_LAYERS, N_EXPERTS, HID, HID), dtype=jnp.float32) * s
        br = jax.random.normal(ks[4], (N_LAYERS, N_EXPERTS, HID), dtype=jnp.float32) * s
        Ws = jax.random.normal(ks[5], (N_LAYERS, N_SHARED, HID, HID), dtype=jnp.float32) * s
        bs = jax.random.normal(ks[6], (N_LAYERS, N_SHARED, HID), dtype=jnp.float32) * s
        Wo = jax.random.normal(ks[7], (OUT_DIM, HID), dtype=jnp.float32) * s
        bo = jnp.zeros((OUT_DIM,), dtype=jnp.float32)
        return {'x': x, 'route_id': route_id, 'Wi': Wi, 'bi': bi, 'Wr': Wr, 'br': br, 'Ws': Ws, 'bs': bs, 'Wo': Wo, 'bo': bo}
    _L2_ffn_all = _L2_ffn_setup()
    _L2_ffn_in = {k: v for k, v in _L2_ffn_all.items() if k in ('route_id', 'Wi', 'bi', 'Wr', 'br', 'Ws', 'bs', 'Wo', 'bo')}
    del _L2_ffn_all

    def _L3_attn_setup():
        import jax, jax.numpy as jnp
        import numpy as np
        B, S, D, H = (8, 256, 64, 8)
        key = jax.random.key(seed)
        k1, k2, k3, k4, k5 = jax.random.split(key, 5)
        return {'x': jax.random.normal(k1, (B, S, D), dtype=jnp.float32), 'wq': jax.random.normal(k2, (H, D, D), dtype=jnp.float32), 'wk': jax.random.normal(k3, (H, D, D), dtype=jnp.float32), 'wv': jax.random.normal(k4, (H, D, D), dtype=jnp.float32), 'wo': jax.random.normal(k5, (H * D, D), dtype=jnp.float32)}
    _L3_attn_all = _L3_attn_setup()
    _L3_attn_in = {k: v for k, v in _L3_attn_all.items() if k in ('wq', 'wk', 'wv', 'wo')}
    del _L3_attn_all

    def _L3_ffn_setup():
        import jax, jax.numpy as jnp
        import numpy as np
        TOP_K = 2
        key = jax.random.key(seed)
        ks = jax.random.split(key, 4)
        B, L, D, H, E = (8, 1024, 64, 256, 8)
        s = 0.02
        return {'x': jax.random.normal(ks[0], (B, L, D), jnp.float32), 'Wg': jax.random.normal(ks[1], (D, E), jnp.float32) * s, 'bg': jnp.zeros((E,), jnp.float32), 'W1': jax.random.normal(ks[2], (E, D, H), jnp.float32) * s, 'b1': jnp.zeros((E, H), jnp.float32), 'W2': jax.random.normal(ks[3], (E, H, D), jnp.float32) * s, 'b2': jnp.zeros((E, D), jnp.float32)}
    _L3_ffn_all = _L3_ffn_setup()
    _L3_ffn_in = {k: v for k, v in _L3_ffn_all.items() if k in ('Wg', 'bg', 'W1', 'b1', 'W2', 'b2')}
    del _L3_ffn_all
    return {'x': x, 'L0_tok_weight': _L0_tok_in['weight'], 'L0_tok_bias': _L0_tok_in['bias'], 'L0_attn_Wq': _L0_attn_in['Wq'], 'L0_attn_bq': _L0_attn_in['bq'], 'L0_attn_Wk': _L0_attn_in['Wk'], 'L0_attn_bk': _L0_attn_in['bk'], 'L0_attn_Wv': _L0_attn_in['Wv'], 'L0_attn_bv': _L0_attn_in['bv'], 'L0_attn_Wo': _L0_attn_in['Wo'], 'L0_attn_bo': _L0_attn_in['bo'], 'L0_ffn_W_gat': _L0_ffn_in['W_gat'], 'L0_ffn_att_src': _L0_ffn_in['att_src'], 'L0_ffn_att_dst': _L0_ffn_in['att_dst'], 'L0_ffn_b_gat': _L0_ffn_in['b_gat'], 'L0_ffn_ln_gamma': _L0_ffn_in['ln_gamma'], 'L0_ffn_ln_beta': _L0_ffn_in['ln_beta'], 'L0_ffn_W1': _L0_ffn_in['W1'], 'L0_ffn_b1': _L0_ffn_in['b1'], 'L0_ffn_W2': _L0_ffn_in['W2'], 'L0_ffn_b2': _L0_ffn_in['b2'], 'L0_ffn_edge_index': _L0_ffn_in['edge_index'], 'L1_attn_B_re': _L1_attn_in['B_re'], 'L1_attn_B_im': _L1_attn_in['B_im'], 'L1_attn_C_re': _L1_attn_in['C_re'], 'L1_attn_C_im': _L1_attn_in['C_im'], 'L1_attn_D': _L1_attn_in['D'], 'L1_attn_nu': _L1_attn_in['nu'], 'L1_attn_theta': _L1_attn_in['theta'], 'L1_attn_gamma_log': _L1_attn_in['gamma_log'], 'L1_ffn_W1': _L1_ffn_in['W1'], 'L1_ffn_b1': _L1_ffn_in['b1'], 'L1_ffn_Wg': _L1_ffn_in['Wg'], 'L1_ffn_bg': _L1_ffn_in['bg'], 'L1_ffn_Wd': _L1_ffn_in['Wd'], 'L1_ffn_bd': _L1_ffn_in['bd'], 'L2_attn_Wq': _L2_attn_in['Wq'], 'L2_attn_bq': _L2_attn_in['bq'], 'L2_attn_Wk': _L2_attn_in['Wk'], 'L2_attn_bk': _L2_attn_in['bk'], 'L2_attn_Wv': _L2_attn_in['Wv'], 'L2_attn_bv': _L2_attn_in['bv'], 'L2_ffn_route_id': _L2_ffn_in['route_id'], 'L2_ffn_Wi': _L2_ffn_in['Wi'], 'L2_ffn_bi': _L2_ffn_in['bi'], 'L2_ffn_Wr': _L2_ffn_in['Wr'], 'L2_ffn_br': _L2_ffn_in['br'], 'L2_ffn_Ws': _L2_ffn_in['Ws'], 'L2_ffn_bs': _L2_ffn_in['bs'], 'L2_ffn_Wo': _L2_ffn_in['Wo'], 'L2_ffn_bo': _L2_ffn_in['bo'], 'L3_attn_wq': _L3_attn_in['wq'], 'L3_attn_wk': _L3_attn_in['wk'], 'L3_attn_wv': _L3_attn_in['wv'], 'L3_attn_wo': _L3_attn_in['wo'], 'L3_ffn_Wg': _L3_ffn_in['Wg'], 'L3_ffn_bg': _L3_ffn_in['bg'], 'L3_ffn_W1': _L3_ffn_in['W1'], 'L3_ffn_b1': _L3_ffn_in['b1'], 'L3_ffn_W2': _L3_ffn_in['W2'], 'L3_ffn_b2': _L3_ffn_in['b2']}

def reference(x, L0_tok_weight, L0_tok_bias, L0_attn_Wq, L0_attn_bq, L0_attn_Wk, L0_attn_bk, L0_attn_Wv, L0_attn_bv, L0_attn_Wo, L0_attn_bo, L0_ffn_W_gat, L0_ffn_att_src, L0_ffn_att_dst, L0_ffn_b_gat, L0_ffn_ln_gamma, L0_ffn_ln_beta, L0_ffn_W1, L0_ffn_b1, L0_ffn_W2, L0_ffn_b2, L0_ffn_edge_index, L1_attn_B_re, L1_attn_B_im, L1_attn_C_re, L1_attn_C_im, L1_attn_D, L1_attn_nu, L1_attn_theta, L1_attn_gamma_log, L1_ffn_W1, L1_ffn_b1, L1_ffn_Wg, L1_ffn_bg, L1_ffn_Wd, L1_ffn_bd, L2_attn_Wq, L2_attn_bq, L2_attn_Wk, L2_attn_bk, L2_attn_Wv, L2_attn_bv, L2_ffn_route_id, L2_ffn_Wi, L2_ffn_bi, L2_ffn_Wr, L2_ffn_br, L2_ffn_Ws, L2_ffn_bs, L2_ffn_Wo, L2_ffn_bo, L3_attn_wq, L3_attn_wk, L3_attn_wv, L3_attn_wo, L3_ffn_Wg, L3_ffn_bg, L3_ffn_W1, L3_ffn_b1, L3_ffn_W2, L3_ffn_b2):
    import jax
    import jax.numpy as jnp

    def _L0_tok_ref(x, weight, bias):
        import jax, jax.numpy as jnp
        import numpy as np
        PH, PW = (64, 25)
        SH, SW = (64, 12)

        def _unfold(x, ph, pw, sh, sw):
            B, C, H, W = x.shape
            nh = (H - ph) // sh + 1
            nw = (W - pw) // sw + 1
            rows = jnp.arange(nh)[:, None] * sh + jnp.arange(ph)[None, :]
            cols = jnp.arange(nw)[:, None] * sw + jnp.arange(pw)[None, :]
            p = x[:, :, rows, :]
            p = p[:, :, :, :, cols]
            p = jnp.transpose(p, (0, 2, 4, 1, 3, 5))
            return p.reshape(B, nh * nw, C * ph * pw)
        p = _unfold(x, PH, PW, SH, SW)
        return jax.nn.gelu(jnp.einsum('bnk,kd->bnd', p, weight) + bias, approximate=False)

    def _L0_attn_ref(src, Wq, bq, Wk, bk, Wv, bv, Wo, bo):
        import jax, jax.numpy as jnp
        import numpy as np
        import math
        B, S, D = (4, 1024, 64)
        q = src @ Wq.T + bq
        k = src @ Wk.T + bk
        v = src @ Wv.T + bv
        row_mask = (q[:, :, 0] != 0) & (k[:, :, 0] != 0)
        mask = row_mask[:, :, None]
        scale = 1.0 / math.sqrt(D)
        scores = jnp.einsum('bid,bjd->bij', q, k) * scale
        scores = jnp.where(mask, scores, jnp.float32(-1000000000.0))
        prob = jax.nn.softmax(scores, axis=-1)
        prob = jnp.where(mask, prob, 0.0)
        out = jnp.einsum('bij,bjd->bid', prob, v)
        return out @ Wo.T + bo

    def _L0_ffn_ref(x, W_gat, att_src, att_dst, b_gat, ln_gamma, ln_beta, W1, b1, W2, b2, edge_index):
        import jax, jax.numpy as jnp
        import numpy as np
        B, N, D = (16, 1024, 64)
        NUM_EXPERTS, TOP_K, HEADS = (4, 2, 4)
        N_EDGES = 262144
        LN_EPS = 1e-05

        def _layernorm(x, g, b):
            mu = x.mean(-1, keepdims=True)
            var = ((x - mu) ** 2).mean(-1, keepdims=True)
            return (x - mu) * jax.lax.rsqrt(var + LN_EPS) * g + b

        def _forward(x, edge_index, W_gat, att_src, att_dst, b_gat, ln_gamma, ln_beta, W1, b1, W2, b2):
            Bc, Nc, Dc = x.shape
            M = Bc * Nc
            x_flat = x.reshape(M, Dc)
            h = (x_flat @ W_gat).reshape(M, HEADS, NUM_EXPERTS)
            loops = jnp.arange(M, dtype=edge_index.dtype)
            src = jnp.concatenate([edge_index[0], loops])
            dst = jnp.concatenate([edge_index[1], loops])
            a_src = (h * att_src).sum(-1)
            a_dst = (h * att_dst).sum(-1)
            e = jax.nn.leaky_relu(a_src[src] + a_dst[dst], negative_slope=0.2)
            e_max = jax.ops.segment_max(e, dst, num_segments=M)
            ee = jnp.exp(e - e_max[dst])
            denom = jax.ops.segment_sum(ee, dst, num_segments=M)
            alpha = ee / (denom[dst] + 1e-16)
            msg = h[src] * alpha[:, :, None]
            agg = jax.ops.segment_sum(msg, dst, num_segments=M).reshape(M, HEADS * NUM_EXPERTS) + b_gat
            scores = _layernorm(agg, ln_gamma, ln_beta).reshape(M, HEADS, NUM_EXPERTS).mean(1)
            scores = scores.reshape(Bc, Nc, NUM_EXPERTS)
            topk_s, topk_i = jax.lax.top_k(scores, TOP_K)
            w = jax.nn.softmax(topk_s, axis=-1)
            out = jnp.zeros_like(x)
            for ei in range(NUM_EXPERTS):
                g = jnp.where(topk_i == ei, w, 0.0).sum(-1)
                hh = jax.nn.gelu(x @ W1[ei] + b1[ei], approximate=False)
                out = out + g[..., None] * (hh @ W2[ei] + b2[ei])
            return out
        return _forward(x, edge_index, W_gat, att_src, att_dst, b_gat, ln_gamma, ln_beta, W1, b1, W2, b2)

    def _L1_attn_ref(x, B_re, B_im, C_re, C_im, D, nu, theta, gamma_log):
        import jax, jax.numpy as jnp
        import numpy as np
        B_SZ, T, N, H = (8, 1024, 64, 128)
        RMAX, RMIN = (0.99, 0.4)

        def _glorot_half(k, shape):
            fan_avg = (shape[0] + shape[1]) / 2.0
            limit = float(np.sqrt(3.0 * 0.5 / fan_avg))
            return jax.random.uniform(k, shape, jnp.float32, -limit, limit)

        def _binary_op(qi, qj):
            A_i, b_i = qi
            A_j, b_j = qj
            return (A_j * A_i, A_j * b_i + b_j)
        u = x
        lam_log = jax.lax.complex(-jnp.exp(nu), theta)
        lam = jnp.exp(lam_log)
        gamma = jnp.exp(gamma_log).astype(jnp.complex64)
        Bm = jax.lax.complex(B_re, B_im)
        Cm = jax.lax.complex(C_re, C_im)
        u_c = u.astype(jnp.complex64)
        bu = gamma * (u_c @ Bm)
        A = jnp.broadcast_to(lam, (1, u.shape[1], lam.shape[0]))
        _, xs = jax.lax.associative_scan(_binary_op, (A, bu), axis=1)
        y = jnp.real(xs @ Cm) + D * u
        return y

    def _L1_ffn_ref(x, W1, b1, Wg, bg, Wd, bd):
        import jax, jax.numpy as jnp
        import numpy as np
        C = 64
        HID = 256
        E = 8
        TEMP = 1.0
        orig_shape = x.shape
        xf = x.reshape(-1, orig_shape[-1])
        H = jax.nn.gelu(xf @ W1 + b1, approximate=False)
        probs = jax.nn.softmax((H @ Wg + bg) / TEMP, axis=-1)
        assign = jnp.argmax(probs, axis=-1)
        out = jnp.zeros_like(xf)
        for e in range(Wd.shape[0]):
            y = H @ Wd[e] + bd[e]
            sel = (assign == e)[:, None]
            out = out + jnp.where(sel, probs[:, e:e + 1] * y, 0.0)
        return out.reshape(orig_shape)

    def _L2_attn_ref(x, Wq, bq, Wk, bk, Wv, bv):
        import jax, jax.numpy as jnp
        import numpy as np
        NUM_HEADS = 8

        def _to_heads(y, R, C, H, hd):
            y = y.reshape(R, C, H, hd).transpose(0, 2, 1, 3)
            y = jnp.transpose(y, (2, 1, 0, 3)).reshape(1, H, C, R * hd)
            return y

        def _reference_tuple_inner(x, Wq, bq, Wk, bk, Wv, bv):
            R, C, E = x.shape
            H = NUM_HEADS
            hd = E // H
            q = _to_heads(x @ Wq.T + bq, R, C, H, hd)
            k = _to_heads(x @ Wk.T + bk, R, C, H, hd)
            v = _to_heads(x @ Wv.T + bv, R, C, H, hd)
            d = q.shape[-1]
            q = jax.nn.softmax(q, axis=-1)
            k = jax.nn.softmax(k, axis=-2)
            q = q * jnp.asarray(float(d) ** 0.5, dtype=q.dtype)
            attn_weights = jnp.einsum('bhnd,bhmd->bhnm', q, k).sum(0)
            context = jnp.einsum('bhnd,bhne->bhde', k, v)
            out = jnp.einsum('bhnd,bhde->hbne', q, context)
            out = out.reshape(H, C, R, hd)
            out = jnp.transpose(out, (2, 1, 0, 3)).reshape(R, C, E)
            return (out, attn_weights)
        return _reference_tuple_inner(x, Wq, bq, Wk, bk, Wv, bv)[0]

    def _L2_ffn_ref(x, route_id, Wi, bi, Wr, br, Ws, bs, Wo, bo):
        import jax, jax.numpy as jnp
        import numpy as np
        B, T, IN_DIM = (64, 64, 64)
        HID, OUT_DIM = (128, 64)
        N_LAYERS, N_EXPERTS, N_SHARED = (2, 16, 1)
        flat = x.reshape(-1, x.shape[-1])
        n_tok = flat.shape[0]
        route = jnp.repeat(route_id, n_tok // route_id.shape[0])
        h = jax.nn.relu(flat @ Wi.T + bi)
        n_layers, n_experts = (Wr.shape[0], Wr.shape[1])
        for l in range(n_layers):
            shared = (jnp.einsum('nd,shd->snh', h, Ws[l]) + bs[l][:, None, :]).mean(axis=0)
            routed = jnp.zeros_like(h)
            for e in range(n_experts):
                ye = h @ Wr[l, e].T + br[l, e]
                routed = routed + jnp.where((route == e)[:, None], ye, 0.0)
            h = jax.nn.relu(shared + routed + h)
        out = h @ Wo.T + bo
        return out.reshape(*x.shape[:-1], out.shape[-1])

    def _L3_attn_ref(x, wq, wk, wv, wo):
        import jax, jax.numpy as jnp
        import numpy as np
        B, S, D, H = (8, 256, 64, 8)
        scale = jnp.asarray(D ** 0.5, x.dtype)
        Q = jnp.einsum('bsd,hde->bhse', x, wq)
        K = jnp.einsum('bsd,hde->bhse', x, wk)
        V = jnp.einsum('bsd,hde->bhse', x, wk)
        Sc = jnp.einsum('bhse,bhte->bhst', Q, K) / scale
        P = jax.nn.softmax(Sc, axis=-1)
        O = jnp.einsum('bhst,bhte->bhse', P, V)
        out = jnp.transpose(O, (0, 2, 1, 3)).reshape(x.shape[0], x.shape[1], -1)
        return jnp.einsum('bsf,fd->bsd', out, wo)

    def _L3_ffn_ref(x, Wg, bg, W1, b1, W2, b2):
        import jax, jax.numpy as jnp
        import numpy as np
        TOP_K = 2
        B, L, D = x.shape
        E = W1.shape[0]
        xf = x.reshape(-1, D)
        gate_logits = xf @ Wg + bg
        top_w, top_i = jax.lax.top_k(gate_logits, TOP_K)
        top_w = jax.nn.softmax(top_w, axis=-1)
        w_dense = jnp.sum(jax.nn.one_hot(top_i, E, dtype=xf.dtype) * top_w[..., None], axis=1)
        out = jnp.zeros_like(xf)
        for e in range(E):
            h = jax.nn.gelu(xf @ W1[e] + b1[e], approximate=False)
            out = out + w_dense[:, e:e + 1] * (h @ W2[e] + b2[e])
        return out.reshape(B, L, D)
    h = _L0_tok_ref(x, L0_tok_weight, L0_tok_bias)
    h = _layernorm(h + _L0_attn_ref(h, L0_attn_Wq, L0_attn_bq, L0_attn_Wk, L0_attn_bk, L0_attn_Wv, L0_attn_bv, L0_attn_Wo, L0_attn_bo), axis=-1)
    h = _layernorm(h + _L0_ffn_ref(h, L0_ffn_W_gat, L0_ffn_att_src, L0_ffn_att_dst, L0_ffn_b_gat, L0_ffn_ln_gamma, L0_ffn_ln_beta, L0_ffn_W1, L0_ffn_b1, L0_ffn_W2, L0_ffn_b2, L0_ffn_edge_index), axis=-1)
    h = _layernorm(h + _L1_attn_ref(h, L1_attn_B_re, L1_attn_B_im, L1_attn_C_re, L1_attn_C_im, L1_attn_D, L1_attn_nu, L1_attn_theta, L1_attn_gamma_log), axis=-1)
    h = _layernorm(h + _L1_ffn_ref(h, L1_ffn_W1, L1_ffn_b1, L1_ffn_Wg, L1_ffn_bg, L1_ffn_Wd, L1_ffn_bd), axis=-1)
    h = _layernorm(h + _L2_attn_ref(h, L2_attn_Wq, L2_attn_bq, L2_attn_Wk, L2_attn_bk, L2_attn_Wv, L2_attn_bv), axis=-1)
    h = _layernorm(h + _L2_ffn_ref(h, L2_ffn_route_id, L2_ffn_Wi, L2_ffn_bi, L2_ffn_Wr, L2_ffn_br, L2_ffn_Ws, L2_ffn_bs, L2_ffn_Wo, L2_ffn_bo), axis=-1)
    h = _layernorm(h + _L3_attn_ref(h, L3_attn_wq, L3_attn_wk, L3_attn_wv, L3_attn_wo), axis=-1)
    h = _layernorm(h + _L3_ffn_ref(h, L3_ffn_Wg, L3_ffn_bg, L3_ffn_W1, L3_ffn_b1, L3_ffn_W2, L3_ffn_b2), axis=-1)
    return h

_drawn_inputs = setup_inputs


def setup_inputs(seed=0):
    import zlib

    import numpy as np

    out = dict(_drawn_inputs(seed))
    spreads = {'L0_tok_bias': (0.0, 0.1),
     'L0_ffn_b_gat': (0.0, 0.1),
     'L0_ffn_ln_gamma': (1.0, 0.548),
     'L0_ffn_ln_beta': (0.0, 0.366),
     'L0_ffn_b1': (0.0, 0.1),
     'L0_ffn_b2': (0.0, 0.1),
     'L1_ffn_b1': (0.0, 0.269),
     'L1_ffn_bg': (0.0, 0.1),
     'L1_ffn_bd': (0.0, 0.1),
     'L2_ffn_bi': (0.0, 0.1),
     'L2_ffn_bo': (0.0, 0.1),
     'L3_ffn_bg': (0.0, 0.1),
     'L3_ffn_b1': (0.0, 0.697),
     'L3_ffn_b2': (0.0, 0.1)}
    factors = {'L0_attn_bk': 8.0,
     'L0_ffn_att_src': 8.0,
     'L0_ffn_att_dst': 8.0,
     'L1_ffn_Wd': 4.069,
     'L2_attn_Wq': 6.022,
     'L2_attn_bq': 8.0,
     'L2_attn_bk': 6.67,
     'L2_ffn_br': 3.58,
     'L2_ffn_bs': 3.931,
     'L3_ffn_W1': 3.076}
    for name, (base, spread) in spreads.items():
        noise = np.random.default_rng([zlib.crc32(name.encode()), seed]).standard_normal(out[name].shape)
        drawn = base * np.exp(spread * noise) if base else spread * noise
        out[name] = jnp.asarray(drawn.astype(out[name].dtype))
    for name, factor in factors.items():
        out[name] = (out[name] * factor).astype(out[name].dtype)
    return out
```

```python
class Chain:

    def __init__(self, engine, done):
        self.engine, self.done, self.count = engine, done, 0

    def step(self, instruction):
        self.count += 1
        instruction.then_inc(self.done, 1)
        self.engine.wait_ge(self.done, self.count)


def vit_tower(nc, A, out, stop):
    import concourse.bass as bass
    from concourse import mybir
    from contextlib import ExitStack

    F32, BF16, I32, U32 = mybir.dt.float32, mybir.dt.bfloat16, mybir.dt.int32, mybir.dt.uint32
    ALU, ACT, AX = mybir.AluOpType, mybir.ActivationFunctionType, mybir.AxisListType
    ts, ds = bass.ts, bass.ds

    P = 128
    IMAGES, S, D = 64, 51, 64
    T = IMAGES * S
    TILES = (T + P - 1) // P
    TP = TILES * P
    BANK = 512
    PATCH_COLS, STRIDE_COLS, PATCH_ROWS, NH, NW = 25, 12, 64, 3, 17
    GROUP = 8
    GCOLS = GROUP * S
    GROUPS = IMAGES // GROUP
    CHUNKS = [(c, min(BANK, TP - c)) for c in range(0, TP, BANK)]
    EDGES = A["L0_ffn_edge_index"].shape[1]
    EC = EDGES // P
    LN_EPS = 1e-5

    top = ExitStack()
    sb = lambda name, shape, dt=F32, ctx=top: ctx.enter_context(nc.sbuf_tensor(name, shape, dt))
    stage_semaphores, serial = [], [0]

    def sem(name, ctx=top):
        if ctx is top:
            return ctx.enter_context(nc.semaphore(name))
        serial[0] += 1
        stage_semaphores.append(nc.alloc_semaphore("%s_%d" % (name, serial[0])))
        return stage_semaphores[-1]

    psum = top.enter_context(nc.psum_tensor("psum", [P, 8 * BANK], F32))

    def bank(k, n=1):
        return psum[:, k * BANK:(k + n) * BANK]

    tok = sb("tok", [P, TILES, D])
    feat = sb("feat", [D, TP])
    ident = sb("ident", [P, P])
    ones_row = sb("ones_row", [1, P])
    ones_col = sb("ones_col", [P, 1])
    table = nc.dram_tensor("node_table", (TP, 20), F32, kind="Internal").ap()

    W, loads = {}, {}

    def weight(part, name, shape, src):
        W[name] = sb("w_" + name, shape)
        loads.setdefault(part, []).append((W[name], src))

    def row(ap):
        return ap.rearrange("(a n) -> a n", a=1)

    def column(ap):
        return ap.rearrange("(n a) -> n a", a=1)

    def spread(ap, n):
        return ap.rearrange("(a n) -> a n", a=1).broadcast_to([n, ap.shape[0]])

    tw = A["L0_tok_weight"].rearrange("(r c) o -> r c o", c=PATCH_COLS)
    W["tok"] = sb("w_tok", [P, 13, D])
    loads["tok"] = [(W["tok"][0:64], tw[:, 0::2, :]), (W["tok"][64:128, 0:12], tw[:, 1::2, :])]
    weight("tok", "tok_b", [D, 1], column(A["L0_tok_bias"]))
    for n in "qkv":
        weight("attn0", "a0" + n, [D, D], A["L0_attn_W" + n])
    for n in "qk":
        weight("attn0", "a0b" + n, [D, 1], column(A["L0_attn_b" + n]))
    W["a0bm"] = sb("w_a0bm", [S, 2])
    W["a0o"] = sb("w_a0o", [D + 1, D])
    loads["attn0"] += [(W["a0bm"][:, 0:1], spread(A["L0_attn_bq"][0:1], S)),
                       (W["a0bm"][:, 1:2], spread(A["L0_attn_bk"][0:1], S)),
                       (W["a0o"][0:D], A["L0_attn_Wo"]), (W["a0o"][D:D + 1], row(A["L0_attn_bo"]))]
    weight("attn0", "a0bv", [S, D], spread(A["L0_attn_bv"], S))
    weight("gat", "gat", [D, 16], A["L0_ffn_W_gat"])
    for n in ("att_src", "att_dst", "b_gat", "ln_gamma", "ln_beta"):
        weight("gat", n, [P, 16], spread(A["L0_ffn_" + n], P))
    weight("ffn0", "f0w1", [D, 4, 128], A["L0_ffn_W1"].rearrange("e d h -> d e h"))
    weight("ffn0", "f0b1", [P, 4], A["L0_ffn_b1"])
    weight("ffn0", "f0w2", [P, 4, D], A["L0_ffn_W2"].rearrange("e h d -> h e d"))
    weight("ffn0", "f0b2", [1, 4 * D], A["L0_ffn_b2"].rearrange("(a e) d -> a (e d)", a=1))
    for n in ("B_re", "B_im"):
        weight("attn1", n, [D, P], A["L1_attn_" + n])
    for n in ("C_re", "C_im"):
        weight("attn1", n, [P, D], A["L1_attn_" + n])
    weight("attn1", "D", [D, 1], column(A["L1_attn_D"]))
    for n in ("nu", "theta", "gamma_log"):
        weight("attn1", n, [P, 1], column(A["L1_attn_" + n]))
    weight("ffn1", "f1w1", [D, 256], A["L1_ffn_W1"])
    weight("ffn1", "f1b1", [P, 2], A["L1_ffn_b1"])
    weight("ffn1", "f1wg", [P, 2, 8], A["L1_ffn_Wg"].rearrange("(c p) e -> p c e", p=P))
    weight("ffn1", "f1bg", [1, 8], row(A["L1_ffn_bg"]))
    W["f1wd"] = sb("w_f1wd", [P, 2, 8, D])
    for c in range(2):
        loads["ffn1"].append((W["f1wd"][:, c], A["L1_ffn_Wd"][:, c * P:(c + 1) * P, :].rearrange("e p d -> p e d")))
    weight("ffn1", "f1bd", [1, 8 * D], A["L1_ffn_bd"].rearrange("(a e) d -> a (e d)", a=1))
    W["a2"] = sb("w_a2", [D, 3, D])
    W["a2b"] = sb("w_a2b", [D, 3, D])
    loads["attn2"] = []
    for i, n in enumerate("qkv"):
        loads["attn2"] += [(W["a2"][:, i], A["L2_attn_W" + n]), (W["a2b"][:, i], spread(A["L2_attn_b" + n], D))]
    weight("ffn2", "f2wi", [D, P], A["L2_ffn_Wi"])
    weight("ffn2", "f2bi", [P, 1], column(A["L2_ffn_bi"]))
    W["f2w"] = sb("w_f2w", [P, 2, 16, P + 1])
    weight("ffn2", "f2ws", [P, 2, P], A["L2_ffn_Ws"].rearrange("l i o -> i l o"))
    weight("ffn2", "f2bs", [P, 2], A["L2_ffn_bs"])
    weight("ffn2", "f2br", [P, 2, 16], A["L2_ffn_br"])
    weight("ffn2", "f2wo", [P, D], A["L2_ffn_Wo"])
    weight("ffn2", "f2bo", [1, D], row(A["L2_ffn_bo"]))
    for layer in range(2):
        loads["ffn2"].append((W["f2w"][:, layer, :, 0:P], A["L2_ffn_Wr"][layer].rearrange("e i o -> i e o")))
    route = sb("route", [1, IMAGES], I32)
    loads["ffn2"].append((route, row(A["L2_ffn_route_id"])))
    weight("attn3", "a3q", [D, 8, D], A["L3_attn_wq"].rearrange("h e d -> e h d"))
    weight("attn3", "a3k", [D, 8, D], A["L3_attn_wk"].rearrange("h e d -> e h d"))
    weight("attn3", "a3o", [D, 8, D], A["L3_attn_wo"].rearrange("(h e) d -> e h d", e=D))
    weight("ffn3", "f3wg", [D, 8], A["L3_ffn_Wg"])
    weight("ffn3", "f3bg", [1, 8], row(A["L3_ffn_bg"]))
    W["f3w1"] = sb("w_f3w1", [D, 16, P])
    W["f3w2"] = sb("w_f3w2", [P, 16, D])
    for e in range(8):
        loads["ffn3"] += [(W["f3w1"][:, 2 * e:2 * e + 2], A["L3_ffn_W1"][e].rearrange("d (c h) -> d c h", c=2)),
                          (W["f3w2"][:, 2 * e:2 * e + 2], A["L3_ffn_W2"][e].rearrange("(c h) d -> h c d", c=2))]
    weight("ffn3", "f3b1", [P, 16], A["L3_ffn_b1"])
    weight("ffn3", "f3b2", [1, 8 * D], A["L3_ffn_b2"].rearrange("(a e) d -> a (e d)", a=1))
    loaded = {part: sem("loaded_" + part) for part in loads}

    def load(engine, *parts):
        for part in parts:
            for tile, src in loads[part]:
                engine.dma_start(tile if isinstance(tile, bass.AP) else tile[:], src).then_inc(loaded[part], 16)

    def wait_weights(engine, part):
        engine.wait_ge(loaded[part], 16 * len(loads[part]))

    def ap(x):
        return x if isinstance(x, bass.AP) else x[:]

    edge_src = sb("edge_src", [P, EC], U32)
    edge_dlo = sb("edge_dlo", [P, EC])
    edge_dhi = sb("edge_dhi", [P, EC])
    trips = sb("trips", [P, 1], I32)

    def tokens_and_keys():
        ctx = ExitStack()
        local = lambda name, shape, dt=F32: sb(name, shape, dt, ctx)
        mark = lambda name: sem(name, ctx)
        rows = local("rows", [P, 2, GROUP * NH, 224])
        e_src, e_dst = local("e_src", [P, EC], I32), local("e_dst", [P, EC], I32)
        key, valid, order = local("key", [P, EC]), local("valid", [P, EC]), local("order", [P, EC])
        top8, spare = local("top8", [P, 2, 8]), local("spare", [1, 2])
        count, most = local("count", [P, 1]), local("most", [P, 1])
        rows_in = [mark("rows_in0"), mark("rows_in1")]
        edges_in, patches_done, gelu_done, counted, most_known = (
            mark(n) for n in ("edges_in", "patches_done", "gelu_done", "counted", "most_known"))
        dve_done, sort_done, consts_done, pool_done = mark("dve_done"), mark("sort_done"), mark("consts_done"), mark("pool_done")

        block = ctx.enter_context(nc.Block())

        @block.sync
        def _(sp):
            load(sp, "tok")
            for h, t in enumerate((e_src, e_dst)):
                sp.dma_start(t[:], A["L0_ffn_edge_index"][h].rearrange("(p c) -> p c", p=P)).then_inc(edges_in, 16)
            for g in range(GROUPS):
                if g >= 2:
                    sp.wait_ge(patches_done, g - 1)
                for half in range(2):
                    img = A["x"][g * GROUP:(g + 1) * GROUP, 0, 0:NH * PATCH_ROWS, half:224]
                    for n in range(NH):
                        sp.dma_start(
                            rows[64 * half:64 * half + 64, g % 2, n::NH, 0:224 - half],
                            img[:, n * PATCH_ROWS:(n + 1) * PATCH_ROWS, :].rearrange("b r c -> r b c"),
                        ).then_inc(rows_in[g % 2], 16)
            load(sp, *[p for p in loads if p != "tok"])

        @block.gpsimd
        def _(pool):
            chain = Chain(pool, pool_done)
            nc.gpsimd.memset(ones_row[:], 1.0).then_inc(consts_done, 1)
            nc.gpsimd.memset(ones_col[:], 1.0).then_inc(consts_done, 1)
            nc.gpsimd.memset(feat[:, T:TP], 0.0).then_inc(consts_done, 1)
            chain.step(nc.gpsimd.memset(ident[:], 0.0))
            nc.gpsimd.affine_select(out=ident[:], in_=ident[:], compare_op=ALU.not_equal, fill=1.0, base=0,
                                    pattern=[[-1, P]], channel_multiplier=1).then_inc(consts_done, 1)
            pool.wait_ge(counted, 1)
            nc.gpsimd.partition_all_reduce(most[:], count[:], P, bass.bass_isa.ReduceOp.max).then_inc(most_known, 1)

        @block.tensor
        def _(pe):
            wait_weights(pe, "tok")
            for g in range(GROUPS):
                pe.wait_ge(rows_in[g % 2], 16 * 2 * NH * (g // 2 + 1))
                if g >= 2:
                    pe.wait_ge(gelu_done, g - 1)
                for k in range(13):
                    K = P if k < 12 else PATCH_ROWS
                    mm = nc.tensor.matmul(bank(g % 2)[0:D, 0:GCOLS], W["tok"][0:K, k, :],
                                          rows[0:K, g % 2, :, 2 * k:2 * k + STRIDE_COLS * (NW - 1) + 1:STRIDE_COLS],
                                          start=(k == 0), stop=(k == 12))
                mm.then_inc(patches_done, 1)

        @block.scalar
        def _(act):
            wait_weights(act, "tok")
            for g in range(GROUPS):
                act.wait_ge(patches_done, g + 1)
                nc.scalar.activation(feat[:, g * GCOLS:(g + 1) * GCOLS], bank(g % 2)[0:D, 0:GCOLS], ACT.Gelu,
                                     bias=W["tok_b"][:, 0:1]).then_inc(gelu_done, 1)
            act.wait_ge(consts_done, 4)

        @block.vector
        def _(dve):
            chain = Chain(dve, dve_done)
            dve.wait_ge(edges_in, 32)
            nc.vector.tensor_scalar(order[:], e_src[:], float(T - 1), None, ALU.min)
            chain.step(nc.vector.tensor_scalar(valid[:], e_dst[:], float(T), None, ALU.is_lt))
            nc.vector.tensor_reduce(count[:], valid[:], AX.X, ALU.add).then_inc(counted, 1)
            chain.step(nc.vector.scalar_tensor_tensor(key[:], e_dst[:], 4096.0, order[:], ALU.mult, ALU.add))
            chain.step(nc.vector.scalar_tensor_tensor(key[:], key[:], 1.0, valid[:], ALU.add, ALU.mult))
            chain.step(nc.vector.tensor_scalar(key[:], key[:], -1.0, None, ALU.add))
            chain.step(nc.vector.memset(order[:], -1.0))
            dve.wait_ge(most_known, 1)
            chain.step(nc.vector.tensor_scalar(trips[:], most[:], 15.0, 16.0, ALU.add, ALU.max))
            chain.step(nc.vector.tensor_scalar(trips[:], trips[:], 4, None, ALU.arith_shift_right))
            n_trips = dve.value_load(trips[0:1, 0:1], min_val=1, max_val=EC // 16)
            with dve.Fori(0, n_trips) as i:
                for q in range(2):
                    nc.vector.max(top8[:, q], key[:]).then_inc(sort_done, 1)
                    dve.wait_ge(sort_done, i * 4 + (2 * q + 1))
                    nc.vector.memset(spare[:, 0:1], 0.0)
                    nc.vector.tensor_copy(order[:, ds(i * 16 + 8 * q, 8)], top8[:, q])
                    nc.vector.match_replace(key[:], top8[:, q], key[:], -1.0).then_inc(sort_done, 1)
                    dve.wait_ge(sort_done, i * 4 + (2 * q + 2))
                    nc.vector.memset(spare[:, 1:2], 0.0)
            as_int, field = e_src, e_dst
            chain.step(nc.vector.tensor_copy(as_int[:], order[:]))
            chain.step(nc.vector.tensor_scalar(field[:], as_int[:], 4095, None, ALU.bitwise_and))
            chain.step(nc.vector.tensor_scalar(edge_src[:], field[:], float(T - 1), None, ALU.min))
            chain.step(nc.vector.tensor_scalar(field[:], as_int[:], 12, 127, ALU.arith_shift_right, ALU.bitwise_and))
            chain.step(nc.vector.tensor_copy(edge_dlo[:], field[:]))
            chain.step(nc.vector.tensor_scalar(field[:], as_int[:], 19, None, ALU.arith_shift_right))
            chain.step(nc.vector.tensor_copy(edge_dhi[:], field[:]))

        ctx.close()

    def norm(name, z):
        ctx = ExitStack()
        mark = lambda n: sem(name + n, ctx)
        mean = sb(name + "mean", [P, TILES], F32, ctx)
        var = sb(name + "var", [P, TILES], F32, ctx)
        eps = sb(name + "eps", [P, 1], F32, ctx)
        squares = sb(name + "squares", [P, TILES, D], F32, ctx)
        dve_done, var_done, std_done, tok_done, turned, copied = (
            mark(n) for n in ("dve_done", "var_done", "std_done", "tok_done", "turned", "copied"))
        z3 = z.rearrange("p (t f) -> p t f", f=D)
        block = ctx.enter_context(nc.Block())

        def wide(x):
            return x[:].rearrange("p (t a) -> p t a", a=1).broadcast_to([P, TILES, D])

        @block.vector
        def _(dve):
            chain = Chain(dve, dve_done)
            nc.vector.memset(eps[:], LN_EPS)
            chain.step(nc.vector.tensor_reduce(mean[:], z3, AX.X, ALU.add))
            chain.step(nc.vector.tensor_scalar(mean[:], mean[:], 1.0 / D, None, ALU.mult))
            chain.step(nc.vector.tensor_tensor(tok[:], z3, wide(mean), ALU.subtract))
            chain.step(nc.vector.tensor_tensor(squares[:], tok[:], tok[:], ALU.mult))
            nc.vector.tensor_reduce(var[:], squares[:], AX.X, ALU.add).then_inc(var_done, 1)
            dve.wait_ge(std_done, 1)
            chain.step(nc.vector.reciprocal(mean[:], var[:]))
            nc.vector.tensor_tensor(tok[:], tok[:], wide(mean), ALU.mult).then_inc(tok_done, 1)

        @block.scalar
        def _(act):
            act.wait_ge(var_done, 1)
            nc.scalar.activation(var[:], var[:], ACT.Sqrt, bias=eps[:, 0:1], scale=1.0 / D).then_inc(std_done, 1)
            for c, (start, n) in enumerate(CHUNKS):
                act.wait_ge(turned, c + 1)
                nc.scalar.copy(feat[:, start:start + n], bank(c)[0:D, 0:n]).then_inc(copied, 1)

        @block.tensor
        def _(pe):
            pe.wait_ge(tok_done, 1)
            for c, (start, n) in enumerate(CHUNKS):
                for j in range(n // P):
                    mm = nc.tensor.transpose(bank(c)[0:D, j * P:(j + 1) * P], tok[:, start // P + j, :], ident[:])
                mm.then_inc(turned, 1)

        ctx.close()

    def close_block(pe, z, branch, bias=None, done=None):
        for t in range(TILES):
            pairs = list(branch(t)) + [(feat[:, t * P:(t + 1) * P], ident[0:D, 0:D])]
            if bias is not None:
                pairs.append((ones_row[:], bias))
            for i, (l, r) in enumerate(pairs):
                mm = nc.tensor.matmul(z[:, t * D:(t + 1) * D], l, r, start=(i == 0), stop=(i == len(pairs) - 1))
        return mm

    def attention0():
        ctx = ExitStack()
        local = lambda name, shape, dt=F32: sb(name, shape, dt, ctx)
        mark = lambda name: sem(name, ctx)
        qT, kT = local("qT", [D, T]), local("kT", [D, T])
        v = local("v", [S, IMAGES, D])
        mask2, mask = local("mask2", [S, IMAGES, 2]), local("mask", [S, IMAGES])
        prob = local("prob", [S, 2, GROUP, S])
        probT = local("probT", [S, 2, GROUP, S])
        high, total = local("high", [S, 2, GROUP]), local("total", [S, 2, GROUP])
        mixT = local("mixT", [D + 1, TP])
        proj_done, proj_copied, v_done, v_copied, m_done = (mark(n) for n in ("proj_done", "proj_copied", "v_done", "v_copied", "m_done"))
        s_done, s_read, exp_in, exp_done, p_done, pT_done, pT_copied, mix_done, mix_copied, dve_done, mixT_set, z_done = (
            mark(n) for n in ("s_done", "s_read", "exp_in", "exp_done", "p_done", "pT_done", "pT_copied", "mix_done",
                              "mix_copied", "dve_done", "mixT_set", "z_done"))
        z = psum[:, 0:TILES * D]
        block = ctx.enter_context(nc.Block())
        PCH = [(c, min(BANK, T - c)) for c in range(0, T, BANK)]

        @block.tensor
        def _(pe):
            wait_weights(pe, "attn0")
            n_proj = 0
            for c, (start, n) in enumerate(PCH):
                for w in ("a0q", "a0k"):
                    if n_proj >= 2:
                        pe.wait_ge(proj_copied, n_proj - 1)
                    nc.tensor.matmul(bank(n_proj % 2)[0:D, 0:n], W[w][:], feat[:, start:start + n],
                                     start=True, stop=True).then_inc(proj_done, 1)
                    n_proj += 1
            for g in range(GROUPS):
                if g >= 2:
                    pe.wait_ge(v_copied, g - 1)
                for j in range(GROUP):
                    b = g * GROUP + j
                    x_b = feat[:, b * S:(b + 1) * S]
                    for i, w in enumerate(("a0q", "a0k")):
                        nc.tensor.matmul(bank(4)[0:S, 2 * b + i:2 * b + i + 1], x_b, W[w][:, 0:1], start=True, stop=True)
                    mm = nc.tensor.matmul(bank(2 + g % 2)[0:S, j * D:(j + 1) * D], x_b, W["a0v"][:], start=True, stop=True)
                mm.then_inc(v_done, 1)
            pe.wait_ge(proj_copied, n_proj)

            def scores(g):
                if g >= 2:
                    pe.wait_ge(s_read, g - 1)
                for j in range(GROUP):
                    b = g * GROUP + j
                    mm = nc.tensor.matmul(bank(g % 2)[0:S, j * S:(j + 1) * S], qT[:, b * S:(b + 1) * S],
                                          kT[:, b * S:(b + 1) * S], start=True, stop=True)
                mm.then_inc(s_done, 1)

            def mix(g):
                pe.wait_ge(p_done, g + 1)
                pe.wait_ge(v_copied, g + 1)
                if g >= 1:
                    pe.wait_ge(pT_copied, g)
                for j in range(GROUP):
                    mm = nc.tensor.transpose(bank(5)[0:S, j * S:(j + 1) * S], prob[:, g % 2, j, :], ident[0:S, 0:S])
                mm.then_inc(pT_done, 1)
                pe.wait_ge(pT_copied, g + 1)
                if g >= 2:
                    pe.wait_ge(mix_copied, g - 1)
                for j in range(GROUP):
                    mm = nc.tensor.matmul(bank(6 + g % 2)[0:D, j * S:(j + 1) * S], v[:, g * GROUP + j, :],
                                          probT[:, g % 2, j, :], start=True, stop=True)
                mm.then_inc(mix_done, 1)

            for g in range(GROUPS + 1):
                if g < GROUPS:
                    scores(g)
                if g >= 1:
                    mix(g - 1)
            pe.wait_ge(mix_copied, GROUPS)
            pe.wait_ge(mixT_set, 2)
            close_block(pe, z, lambda t: [(mixT[:, t * P:(t + 1) * P], W["a0o"][:])]).then_inc(z_done, 1)

        @block.scalar
        def _(act):
            wait_weights(act, "attn0")
            n_proj = 0
            for c, (start, n) in enumerate(PCH):
                for dst, b in ((qT, "a0bq"), (kT, "a0bk")):
                    act.wait_ge(proj_done, n_proj + 1)
                    nc.scalar.activation(dst[:, start:start + n], bank(n_proj % 2)[0:D, 0:n], ACT.Identity,
                                         bias=W[b][:, 0:1]).then_inc(proj_copied, 1)
                    n_proj += 1
            for g in range(GROUPS):
                act.wait_ge(exp_in, g + 1)
                nc.scalar.activation(prob[:, g % 2], prob[:, g % 2], ACT.Exp, scale=D ** -0.5).then_inc(exp_done, 1)
                act.wait_ge(pT_done, g + 1)
                nc.scalar.copy(probT[:, g % 2].rearrange("p a b -> p (a b)"), bank(5)[0:S, 0:GCOLS]).then_inc(pT_copied, 1)
                act.wait_ge(mix_done, g + 1)
                nc.scalar.copy(mixT[0:D, g * GCOLS:(g + 1) * GCOLS], bank(6 + g % 2)[0:D, 0:GCOLS]).then_inc(mix_copied, 1)

        @block.gpsimd
        def _(pool):
            nc.gpsimd.memset(mixT[0:D, T:TP], 0.0).then_inc(mixT_set, 1)
            nc.gpsimd.memset(mixT[D:D + 1, :], 1.0).then_inc(mixT_set, 1)

        @block.vector
        def _(dve):
            chain = Chain(dve, dve_done)
            wait_weights(dve, "attn0")
            for g in range(GROUPS):
                dve.wait_ge(v_done, g + 1)
                nc.vector.tensor_tensor(v[:, g * GROUP:(g + 1) * GROUP, :],
                                        bank(2 + g % 2)[0:S].rearrange("p (b f) -> p b f", f=D),
                                        W["a0bv"][:].rearrange("p (a f) -> p a f", a=1).broadcast_to([S, GROUP, D]),
                                        ALU.add).then_inc(v_copied, 1)
            chain.step(nc.vector.tensor_tensor(
                mask2[:], bank(4)[0:S, 0:2 * IMAGES].rearrange("p (b f) -> p b f", f=2),
                W["a0bm"][:].rearrange("p (a f) -> p a f", a=1).broadcast_to([S, IMAGES, 2]), ALU.add))
            chain.step(nc.vector.tensor_scalar(mask2[:], mask2[:], 0.0, None, ALU.not_equal))
            chain.step(nc.vector.tensor_tensor(mask[:], mask2[:, :, 0], mask2[:, :, 1], ALU.mult))
            for g in range(GROUPS):
                s3 = bank(g % 2)[0:S, 0:GCOLS].rearrange("p (b j) -> p b j", j=S)
                wide = lambda x: x[:, g % 2].rearrange("p (b a) -> p b a", a=1).broadcast_to([S, GROUP, S])
                dve.wait_ge(s_done, g + 1)
                if g >= 2:
                    dve.wait_ge(pT_done, g - 1)
                chain.step(nc.vector.tensor_reduce(high[:, g % 2], s3, AX.X, ALU.max))
                ins = nc.vector.tensor_tensor(prob[:, g % 2], s3, wide(high), ALU.subtract)
                ins.then_inc(exp_in, 1)
                dve.wait_ge(exp_in, g + 1)
                nc.vector.memset(total[:, g % 2], 0.0).then_inc(s_read, 1)
                dve.wait_ge(exp_done, g + 1)
                dve.wait_ge(s_read, g + 1)
                chain.step(nc.vector.tensor_reduce(total[:, g % 2], prob[:, g % 2], AX.X, ALU.add))
                chain.step(nc.vector.reciprocal(high[:, g % 2], total[:, g % 2]))
                chain.step(nc.vector.tensor_tensor(total[:, g % 2], high[:, g % 2], mask[:, g * GROUP:(g + 1) * GROUP], ALU.mult))
                nc.vector.tensor_tensor(prob[:, g % 2], prob[:, g % 2], wide(total), ALU.mult).then_inc(p_done, 1)

        ctx.close()
        norm("n0a_", z)

    def per(x, n):
        return x.rearrange("p (t a) -> p t a", a=1).broadcast_to([P, TILES, n])

    def first_largest(chain, chosen, scores, high, index, E):
        lanes = index[:, 0:E].rearrange("p (a e) -> p a e", a=1).broadcast_to([P, TILES, E])
        chain.step(nc.vector.tensor_reduce(high, scores, AX.X, ALU.max))
        chain.step(nc.vector.tensor_tensor(chosen, scores, per(high, E), ALU.is_equal))
        chain.step(nc.vector.scalar_tensor_tensor(chosen, chosen, -float(E), lanes, ALU.mult, ALU.add))
        first = spare_col[:]
        chain.step(nc.vector.tensor_reduce(first, chosen, AX.X, ALU.min))
        chain.step(nc.vector.tensor_tensor(chosen, chosen, per(first, E), ALU.is_equal))

    spare_col = sb("spare_col", [P, TILES])
    lane_index = sb("lane_index", [P, P])
    gates = sb("gates", [P, TILES, 8])

    def top_two(chain, name, ctx, scores, E, exp_wanted, exp_given):
        one, two = sb(name + "one", [P, TILES, E], F32, ctx), sb(name + "two", [P, TILES, E], F32, ctx)
        m1, m2 = sb(name + "m1", [P, TILES], F32, ctx), sb(name + "m2", [P, TILES], F32, ctx)
        first_largest(chain, one[:], scores, m1[:], lane_index, E)
        chain.step(nc.vector.scalar_tensor_tensor(scores, one[:], -1e30, scores, ALU.mult, ALU.add))
        first_largest(chain, two[:], scores, m2[:], lane_index, E)
        nc.vector.tensor_tensor(m2[:], m2[:], m1[:], ALU.subtract).then_inc(exp_wanted, 1)

        def finish():
            chain.engine.wait_ge(exp_given, 1)
            chain.step(nc.vector.tensor_scalar(m1[:], m2[:], 1.0, None, ALU.add))
            chain.step(nc.vector.reciprocal(m1[:], m1[:]))
            chain.step(nc.vector.tensor_tensor(m2[:], m2[:], m1[:], ALU.mult))
            chain.step(nc.vector.tensor_tensor(one[:], one[:], per(m1[:], E), ALU.mult))
            chain.step(nc.vector.tensor_tensor(two[:], two[:], per(m2[:], E), ALU.mult))
            return nc.vector.tensor_tensor(gates[:, :, 0:E], one[:], two[:], ALU.add)

        return m2, finish

    HEADS, SLOTS, FIELDS = 4, 8, 20

    def graph_gates():
        ctx = ExitStack()
        local = lambda name, shape, dt=F32: sb(name, shape, dt, ctx)
        mark = lambda name: sem(name, ctx)
        nodes = local("nodes", [P, TILES, FIELDS])
        a_dst = local("a_dst", [P, TILES, HEADS])
        dst_parts = local("dst_parts", [P, 3, TILES * HEADS], BF16)
        rest = local("rest", [P, TILES * HEADS])
        work = local("work", [P, TILES, 16])
        high, high_all = local("high_src", [P, HEADS]), local("high_all", [P, HEADS])
        zeros = local("zeros", [P, 260])

        inner = ExitStack()
        mark1 = lambda name: sem(name, inner)
        h_done, nodes_ready, table_ready, high_ready, high_known, dve_done1 = (
            mark1(n) for n in ("h_done", "nodes_ready", "table_ready", "high_ready", "high_known", "dve_done1"))
        block = inner.enter_context(nc.Block())

        @block.tensor
        def _(pe):
            wait_weights(pe, "gat")
            for t in range(TILES):
                mm = nc.tensor.matmul(bank(0)[:, 16 * t:16 * t + 16], feat[:, t * P:(t + 1) * P], W["gat"][:],
                                      start=True, stop=True)
            mm.then_inc(h_done, 1)

        @block.vector
        def _(dve):
            chain = Chain(dve, dve_done1)
            wait_weights(dve, "gat")
            nc.vector.memset(zeros[:], 0.0)
            dve.wait_ge(h_done, 1)
            chain.step(nc.vector.tensor_copy(nodes[:, :, 0:16], bank(0)[:, 0:16 * TILES].rearrange("p (t f) -> p t f", f=16)))
            for w, dst in (("att_src", nodes[:, :, 16:20]), ("att_dst", a_dst[:])):
                att = W[w][:].rearrange("p (a f) -> p a f", a=1).broadcast_to([P, TILES, 16])
                chain.step(nc.vector.tensor_tensor(work[:], nodes[:, :, 0:16], att, ALU.mult))
                ins = nc.vector.tensor_reduce(dst, work[:].rearrange("p t (h k) -> p t h k", k=4), AX.X, ALU.add)
                chain.step(ins)
            nc.vector.tensor_reduce(high[:], nodes[:, :, 16:20].rearrange("p t h -> p h t"), AX.X,
                                    ALU.max).then_inc(nodes_ready, 1)
            flat = a_dst[:].rearrange("p t h -> p (t h)")
            chain.step(nc.vector.tensor_copy(dst_parts[:, 0], flat))
            chain.step(nc.vector.tensor_tensor(rest[:], flat, dst_parts[:, 0], ALU.subtract))
            chain.step(nc.vector.tensor_copy(dst_parts[:, 1], rest[:]))
            chain.step(nc.vector.tensor_tensor(rest[:], rest[:], dst_parts[:, 1], ALU.subtract))
            chain.step(nc.vector.tensor_copy(dst_parts[:, 2], rest[:]))

        @block.gpsimd
        def _(pool):
            nc.gpsimd.iota(lane_index[:], [[1, P]], base=0, channel_multiplier=0,
                           allow_small_or_imprecise_dtypes=True).then_inc(high_known, 1)
            pool.wait_ge(nodes_ready, 1)
            nc.gpsimd.partition_all_reduce(high_all[:], high[:], P, bass.bass_isa.ReduceOp.max).then_inc(high_known, 1)
            pool.wait_ge(high_known, 2)

        @block.sync
        def _(sp):
            sp.wait_ge(nodes_ready, 1)
            sp.dma_start(table.rearrange("(t p) f -> p t f", p=P), nodes[:]).then_inc(table_ready, 16)
            sp.wait_ge(table_ready, 16)

        inner.close()

        inner = ExitStack()
        local2 = lambda name, shape, dt=F32: sb(name, shape, dt, inner)
        mark2 = lambda name: sem(name, inner)
        idx = [local2("idx%d" % q, [P, SLOTS], U32) for q in range(2)]
        got = [local2("got%d" % q, [P, SLOTS, FIELDS]) for q in range(2)]
        is_lo = [local2("is_lo%d" % q, [P, SLOTS, P]) for q in range(2)]
        is_loT = [local2("is_loT%d" % q, [P, SLOTS, P], BF16) for q in range(2)]
        is_hi = [local2("is_hi%d" % q, [P, SLOTS, TILES]) for q in range(2)]
        picked = local2("picked", [P, SLOTS, HEADS, TILES])
        dst_term = local2("dst_term", [P, SLOTS, HEADS])
        logit = local2("logit", [P, 2, SLOTS, HEADS])
        message = [local2("message%d" % q, [P, SLOTS, FIELDS]) for q in range(2)]
        placed = [local2("placed%d" % q, [P, SLOTS, TILES, FIELDS]) for q in range(2)]
        gathered = [mark2("gathered0"), mark2("gathered1")]
        (idx_ready, got_free, hot_ready, turned, turned_copied, picks_done, picks_read, exp_wanted, exp_given,
         placed_ready, summed, sums_started, pool_passed, dve_done2, dve_passed, act_passed) = (mark2(n) for n in (
             "idx_ready", "got_free", "hot_ready", "turned", "turned_copied", "picks_done", "picks_read", "exp_wanted",
             "exp_given", "placed_ready", "summed", "sums_started", "pool_passed", "dve_done2", "dve_passed", "act_passed"))
        HALF = TILES // 2
        block = inner.enter_context(nc.Block())

        def n_trips(engine):
            return engine.value_load(trips[0:1, 0:1], min_val=1, max_val=EC // 16)

        @block.gpsimd
        def _(pool):
            n = n_trips(pool)
            with pool.Fori(0, n) as i:
                for q in range(2):
                    pool.wait_ge(got_free, i * 2 + (q + 1))
                    pool.sem_inc(pool_passed, 1)
                    nc.gpsimd.tensor_copy(idx[q][:], edge_src[:, ds(i * 16 + 8 * q, SLOTS)]).then_inc(idx_ready, 1)
                    pool.wait_ge(idx_ready, i * 2 + (q + 1))
                    pool.sem_inc(pool_passed, 1)
                    for j in range(SLOTS):
                        nc.gpsimd.indirect_dma_start(
                            got[q][:, j, :], None, table,
                            bass.IndirectOffsetOnAxis(ap=idx[q][:, j:j + 1], axis=0)).then_inc(gathered[q], 16)

        @block.tensor
        def _(pe):
            for k in range(2):
                mm = nc.tensor.matmul(bank(4 + k)[:, 0:260], zeros[:, 0:P], zeros[:], start=True, stop=False)
            mm.then_inc(summed, 2)
            n = n_trips(pe)
            with pe.Fori(0, n) as i:
                for q in range(2):
                    pe.wait_ge(hot_ready, i * 2 + (q + 1))
                    for j in range(SLOTS):
                        mm = nc.tensor.transpose(bank(j // 4)[:, (j % 4) * P:(j % 4 + 1) * P], is_lo[q][:, j, :], ident[:])
                    mm.then_inc(turned, 1)
                    pe.wait_ge(turned_copied, i * 2 + (q + 1))
                    pe.wait_ge(picks_read, i * 2 + (q + 1))
                    for j in range(SLOTS):
                        for part in range(3):
                            mm = nc.tensor.matmul(bank(2 + j // 4)[:, (j % 4) * P:(j % 4) * P + TILES * HEADS],
                                                  is_loT[q][:, j, :], dst_parts[:, part, :], start=(part == 0), stop=(part == 2))
                    mm.then_inc(picks_done, 1)
                    pe.wait_ge(placed_ready, i * 2 + (q + 1))
                    for j in range(SLOTS):
                        for k in range(2):
                            mm = nc.tensor.matmul(
                                bank(4 + k)[:, 0:260], is_lo[q][:, j, :],
                                placed[q][:, j, k * HALF:(k + 1) * HALF, :].rearrange("p t f -> p (t f)"),
                                start=False, stop=False)
                    mm.then_inc(summed, 1)
            for k in range(2):
                nc.tensor.matmul(bank(4 + k)[:, 0:260], zeros[:, 0:P], zeros[:], start=False, stop=True)

        @block.scalar
        def _(act):
            n = n_trips(act)
            with act.Fori(0, n) as i:
                for q in range(2):
                    act.wait_ge(turned, i * 2 + (q + 1))
                    nc.scalar.copy(is_loT[q][:].rearrange("p a b -> p (a b)"), bank(0, 2)).then_inc(turned_copied, 1)
                    act.wait_ge(exp_wanted, i * 2 + (q + 1))
                    nc.scalar.activation(message[q][:, :, 16:20], logit[:, 0], ACT.Exp).then_inc(exp_given, 1)

        @block.vector
        def _(dve):
            dve.sem_inc(got_free, 2)
            dve.sem_inc(picks_read, 1)
            n = n_trips(dve)
            STEPS = 4
            lanes = lambda k: lane_index[:, 0:k].rearrange("p (a e) -> p a e", a=1).broadcast_to([P, SLOTS, k])

            with dve.Fori(0, n) as i:
                for q in range(2):
                    g1 = i * 2 + (q + 1)
                    steps = [0]

                    def step(ins):
                        steps[0] += 1
                        ins.then_inc(dve_done2, 1)
                        dve.wait_ge(dve_done2, i * (2 * STEPS) + (q * STEPS + steps[0]))

                    def slots(x, k):
                        return x[:, ds(i * 16 + 8 * q, SLOTS)].rearrange("p (t a) -> p t a", a=1).broadcast_to([P, SLOTS, k])

                    dve.wait_ge(summed, g1)
                    nc.vector.tensor_tensor(is_lo[q][:], lanes(P), slots(edge_dlo, P), ALU.is_equal)
                    nc.vector.tensor_tensor(is_hi[q][:], lanes(TILES), slots(edge_dhi, TILES), ALU.is_equal).then_inc(hot_ready, 1)
                    dve.wait_ge(picks_done, g1)
                    dve.wait_ge(hot_ready, g1)
                    picks = bank(2, 2).rearrange("p (j c) -> p j c", c=P)[:, :, 0:TILES * HEADS].rearrange(
                        "p j (t h) -> p j h t", h=HEADS)
                    hi = is_hi[q][:].rearrange("p j (a t) -> p j a t", a=1).broadcast_to([P, SLOTS, HEADS, TILES])
                    ins = nc.vector.tensor_tensor(picked[:], picks, hi, ALU.mult)
                    ins.then_inc(picks_read, 1)
                    dve.wait_ge(picks_read, i * 2 + (q + 2))
                    step(nc.vector.tensor_reduce(dst_term[:], picked[:], AX.X, ALU.add))
                    dve.wait_ge(gathered[q], i * 128 + 128)
                    nc.vector.tensor_tensor(logit[:, 0], got[q][:, :, 16:20], dst_term[:], ALU.add)
                    step(nc.vector.tensor_tensor(
                        logit[:, 1], dst_term[:],
                        high_all[:].rearrange("p (a h) -> p a h", a=1).broadcast_to([P, SLOTS, HEADS]), ALU.add))
                    step(nc.vector.scalar_tensor_tensor(logit[:], logit[:], 0.2, logit[:], ALU.mult, ALU.max))
                    nc.vector.tensor_tensor(logit[:, 0], logit[:, 0], logit[:, 1], ALU.subtract).then_inc(exp_wanted, 1)
                    dve.wait_ge(exp_given, g1)
                    weight4 = message[q][:, :, 16:20].rearrange("p j (h a) -> p j h a", a=1).broadcast_to([P, SLOTS, HEADS, 4])
                    step(nc.vector.tensor_tensor(
                        message[q][:, :, 0:16].rearrange("p j (h k) -> p j h k", k=4),
                        got[q][:, :, 0:16].rearrange("p j (h k) -> p j h k", k=4), weight4, ALU.mult))
                    dve.sem_inc(got_free, 1)
                    ins = nc.vector.tensor_tensor(
                        placed[q][:],
                        is_hi[q][:].rearrange("p j (t a) -> p j t a", a=1).broadcast_to([P, SLOTS, TILES, FIELDS]),
                        message[q][:].rearrange("p j (a f) -> p j a f", a=1).broadcast_to([P, SLOTS, TILES, FIELDS]), ALU.mult)
                    ins.then_inc(placed_ready, 1)

        inner.close()

        inner = ExitStack()
        local3 = lambda name, shape, dt=F32: sb(name, shape, dt, inner)
        mark3 = lambda name: sem(name, inner)
        sums = local3("sums", [P, TILES, FIELDS])
        own = local3("own", [P, 2, TILES, HEADS])
        mixed = local3("mixed", [P, TILES, 16])
        mean, var, eps = local3("mean", [P, TILES]), local3("var", [P, TILES]), local3("eps", [P, 1])
        scores = local3("scores", [P, TILES, HEADS])
        dve_done3, own_wanted, own_given, std_wanted, std_given, pair_wanted, pair_given = (mark3(n) for n in (
            "dve_done3", "own_wanted", "own_given", "std_wanted", "std_given", "pair_wanted", "pair_given"))
        block = inner.enter_context(nc.Block())
        shared = {}

        @block.vector
        def _(dve):
            chain = Chain(dve, dve_done3)
            nc.vector.memset(eps[:], LN_EPS)
            high4 = high_all[:].rearrange("p (a h) -> p a h", a=1).broadcast_to([P, TILES, HEADS])
            nc.vector.tensor_tensor(own[:, 0], nodes[:, :, 16:20], a_dst[:], ALU.add)
            chain.step(nc.vector.tensor_tensor(own[:, 1], a_dst[:], high4, ALU.add))
            chain.step(nc.vector.scalar_tensor_tensor(own[:], own[:], 0.2, own[:], ALU.mult, ALU.max))
            nc.vector.tensor_tensor(own[:, 0], own[:, 0], own[:, 1], ALU.subtract).then_inc(own_wanted, 1)
            dve.wait_ge(own_given, 1)
            grouped = lambda x: x.rearrange("p t (h k) -> p t h k", k=4)
            each4 = lambda x: x.rearrange("p t (h a) -> p t h a", a=1).broadcast_to([P, TILES, HEADS, 4])
            chain.step(nc.vector.tensor_tensor(grouped(sums[:, :, 0:16]), grouped(nodes[:, :, 0:16]), each4(own[:, 0]), ALU.mult))
            chain.step(nc.vector.tensor_copy(sums[:, :, 16:20], own[:, 0]))
            for k in range(2):
                part = sums[:, k * HALF:(k + 1) * HALF, :]
                chain.step(nc.vector.tensor_tensor(part, part, bank(4 + k)[:, 0:260].rearrange("p (t f) -> p t f", f=FIELDS), ALU.add))
            chain.step(nc.vector.tensor_scalar(own[:, 0], sums[:, :, 16:20], 1e-16, None, ALU.add))
            chain.step(nc.vector.reciprocal(own[:, 0], own[:, 0]))
            chain.step(nc.vector.tensor_tensor(grouped(mixed[:]), grouped(sums[:, :, 0:16]), each4(own[:, 0]), ALU.mult))
            each = lambda w: W[w][:].rearrange("p (a f) -> p a f", a=1).broadcast_to([P, TILES, 16])
            chain.step(nc.vector.tensor_tensor(mixed[:], mixed[:], each("b_gat"), ALU.add))
            chain.step(nc.vector.tensor_reduce(mean[:], mixed[:], AX.X, ALU.add))
            chain.step(nc.vector.tensor_scalar(mean[:], mean[:], 1.0 / 16, None, ALU.mult))
            chain.step(nc.vector.tensor_tensor(mixed[:], mixed[:], per(mean[:], 16), ALU.subtract))
            chain.step(nc.vector.tensor_tensor(work[:], mixed[:], mixed[:], ALU.mult))
            nc.vector.tensor_reduce(var[:], work[:], AX.X, ALU.add).then_inc(std_wanted, 1)
            dve.wait_ge(std_given, 1)
            chain.step(nc.vector.reciprocal(var[:], var[:]))
            chain.step(nc.vector.tensor_tensor(mixed[:], mixed[:], per(var[:], 16), ALU.mult))
            chain.step(nc.vector.tensor_tensor(mixed[:], mixed[:], each("ln_gamma"), ALU.mult))
            chain.step(nc.vector.tensor_tensor(mixed[:], mixed[:], each("ln_beta"), ALU.add))
            chain.step(nc.vector.tensor_reduce(scores[:], mixed[:].rearrange("p t (h k) -> p t k h", k=4), AX.X, ALU.add))
            chain.step(nc.vector.tensor_scalar(scores[:], scores[:], 1.0 / HEADS, None, ALU.mult))
            gap, finish = top_two(chain, "g0", inner, scores[:], 4, pair_wanted, pair_given)
            shared["gap"] = gap
            chain.step(finish())

        @block.scalar
        def _(act):
            act.wait_ge(own_wanted, 1)
            nc.scalar.activation(own[:, 0], own[:, 0], ACT.Exp).then_inc(own_given, 1)
            act.wait_ge(std_wanted, 1)
            nc.scalar.activation(var[:], var[:], ACT.Sqrt, bias=eps[:, 0:1], scale=1.0 / 16).then_inc(std_given, 1)
            act.wait_ge(pair_wanted, 1)
            nc.scalar.activation(shared["gap"][:], shared["gap"][:], ACT.Exp).then_inc(pair_given, 1)

        inner.close()
        ctx.close()

    def experts(name, part, E, HC, w1, b1, w2, b2, z):
        ctx = ExitStack()
        mark = lambda n: sem(name + n, ctx)
        hidden = sb(name + "hidden", [P, 2, E * HC, BANK], F32, ctx)
        weighed = sb(name + "weighed", [P, 2, E, D], F32, ctx)
        h_done, gelu_done, y_done, y_read, z_part, dve_done = (
            mark(n) for n in ("h_done", "gelu_done", "y_done", "y_read", "z_part", "dve_done"))
        block = ctx.enter_context(nc.Block())
        M = E * HC

        @block.tensor
        def _(pe):
            wait_weights(pe, part)
            done_tiles = 0

            def up(c):
                start, n = CHUNKS[c]
                for m in range(M):
                    k = c * M + m
                    if k >= 4:
                        pe.wait_ge(gelu_done, k - 3)
                    nc.tensor.matmul(bank(k % 4)[:, 0:n], w1[:, m, :], feat[:, start:start + n],
                                     start=True, stop=True).then_inc(h_done, 1)

            def down(c):
                start, n = CHUNKS[c]
                pe.wait_ge(gelu_done, (c + 1) * M)
                for j in range(n // P):
                    t = start // P + j
                    if t >= 2:
                        pe.wait_ge(y_read, t - 1)
                    y = bank(4 + t % 2)
                    nc.tensor.matmul(y[:, 0:E * D], ones_row[:], b2[:], start=True, stop=False)
                    for e in range(E):
                        for h in range(HC):
                            mm = nc.tensor.matmul(y[:, e * D:(e + 1) * D], hidden[:, c % 2, e * HC + h, j * P:(j + 1) * P],
                                                  w2[:, e * HC + h, :], start=False, stop=(e == E - 1 and h == HC - 1))
                    mm.then_inc(y_done, 1)

            up(0)
            for c in range(1, len(CHUNKS)):
                up(c)
                down(c - 1)
            down(len(CHUNKS) - 1)

        @block.scalar
        def _(act):
            wait_weights(act, part)
            for c, (start, n) in enumerate(CHUNKS):
                if c >= 2:
                    act.wait_ge(y_done, CHUNKS[c - 1][0] // P)
                for m in range(M):
                    k = c * M + m
                    act.wait_ge(h_done, k + 1)
                    nc.scalar.activation(hidden[:, c % 2, m, 0:n], bank(k % 4)[:, 0:n], ACT.Gelu,
                                         bias=b1[:, m:m + 1]).then_inc(gelu_done, 1)

        @block.vector
        def _(dve):
            chain = Chain(dve, dve_done)
            for t in range(TILES):
                dve.wait_ge(y_done, t + 1)
                g = gates[:, t, 0:E].rearrange("p (e a) -> p e a", a=1).broadcast_to([P, E, D])
                nc.vector.tensor_tensor(weighed[:, t % 2], bank(4 + t % 2)[:, 0:E * D].rearrange("p (e f) -> p e f", f=D),
                                        g, ALU.mult).then_inc(y_read, 1)
                dve.wait_ge(y_read, t + 1)
                nc.vector.tensor_reduce(z[:, t], weighed[:, t % 2].rearrange("p e f -> p f e"), AX.X,
                                        ALU.add).then_inc(z_part, 1)
            dve.wait_ge(z_part, TILES)
            chain.step(nc.vector.tensor_tensor(z[:], z[:], tok[:], ALU.add))

        ctx.close()

    def experts0():
        ctx = ExitStack()
        z = sb("z0", [P, TILES, D], F32, ctx)
        experts("e0_", "ffn0", 4, 1, W["f0w1"], W["f0b1"], W["f0w2"], W["f0b2"], z)
        norm("n0f_", z[:].rearrange("p t f -> p (t f)"))
        ctx.close()

    def recurrent1():
        ctx = ExitStack()
        local = lambda name, shape, dt=F32: sb(name, shape, dt, ctx)
        mark = lambda name: sem(name, ctx)
        TWO_PI = 6.283185307179586
        step_no = local("step_no", [P, S])
        angle = local("angle", [P, 2, S])
        turns_i, turns = local("turns_i", [P, 2, S], I32), local("turns", [P, 2, S])
        over = local("over", [P, 2, S])
        wave = local("wave", [P, 2, S])
        wave_in = local("wave_in", [P, 2, S])
        decay = local("decay", [P, 1])
        gamma = local("gamma", [P, 1])
        decays = local("decays", [P, GROUP, S])
        c_minus = local("c_minus", [P, D])
        keep = local("keep", [D, D])
        u4 = local("u4", [P, 4, GROUP, S])
        drive = local("drive", [P, 2, GROUP, S])
        state = local("state", [P, 2, GROUP, S])
        x_re, x_im = local("x_re", [P, TP]), local("x_im", [P, TP])
        (bu_done, bu_read, dve_done, pool_done, exps, sines, angles_ready, x_set, z_done, x_done) = (mark(n) for n in (
            "bu_done", "bu_read", "dve_done", "pool_done", "exps", "sines", "angles_ready", "x_set", "z_done", "x_done"))
        z = psum[:, 4 * BANK:4 * BANK + TILES * D]
        block = ctx.enter_context(nc.Block())

        @block.gpsimd
        def _(pool):
            nc.gpsimd.iota(step_no[:], [[1, S]], base=0, channel_multiplier=0,
                           allow_small_or_imprecise_dtypes=True).then_inc(pool_done, 1)
            nc.gpsimd.memset(x_re[:, T:TP], 0.0).then_inc(x_set, 1)
            nc.gpsimd.memset(x_im[:, T:TP], 0.0).then_inc(x_set, 1)

        @block.tensor
        def _(pe):
            wait_weights(pe, "attn1")
            for g in range(GROUPS):
                if g >= 2:
                    pe.wait_ge(bu_read, g - 1)
                for k, w in enumerate(("B_re", "B_im")):
                    mm = nc.tensor.matmul(bank(2 * (g % 2) + k)[:, 0:GCOLS], W[w][:], feat[:, g * GCOLS:(g + 1) * GCOLS],
                                          start=True, stop=True)
                mm.then_inc(bu_done, 1)
            pe.wait_ge(x_done, GROUPS)
            pe.wait_ge(x_set, 2)
            for t in range(TILES):
                cols = slice(t * P, (t + 1) * P)
                nc.tensor.matmul(z[:, t * D:(t + 1) * D], x_re[:, cols], W["C_re"][:], start=True, stop=False)
                nc.tensor.matmul(z[:, t * D:(t + 1) * D], x_im[:, cols], c_minus[:], start=False, stop=False)
                mm = nc.tensor.matmul(z[:, t * D:(t + 1) * D], feat[:, cols], keep[:], start=False, stop=True)
            mm.then_inc(z_done, 1)

        @block.scalar
        def _(act):
            wait_weights(act, "attn1")
            nc.scalar.activation(decay[:], W["nu"][:], ACT.Exp).then_inc(exps, 1)
            nc.scalar.activation(gamma[:], W["gamma_log"][:], ACT.Exp).then_inc(exps, 1)
            act.wait_ge(exps, 2)
            nc.scalar.activation(decay[:], decay[:], ACT.Exp, scale=-1.0).then_inc(exps, 1)
            act.wait_ge(angles_ready, 1)
            nc.scalar.activation(wave[:], angle[:], ACT.Sin).then_inc(sines, 1)

        @block.vector
        def _(dve):
            chain = Chain(dve, dve_done)
            wait_weights(dve, "attn1")
            dve.wait_ge(pool_done, 1)
            chain.step(nc.vector.tensor_scalar(angle[:, 1], step_no[:], W["theta"][:, 0:1], None, ALU.mult))
            chain.step(nc.vector.tensor_scalar(angle[:, 0], angle[:, 1], TWO_PI / 4, None, ALU.add))
            chain.step(nc.vector.tensor_scalar(turns_i[:], angle[:], 1.0 / TWO_PI, None, ALU.mult))
            chain.step(nc.vector.tensor_copy(turns[:], turns_i[:]))
            for piece in (6.28125, TWO_PI - 6.28125):
                chain.step(nc.vector.scalar_tensor_tensor(angle[:], turns[:], -piece, angle[:], ALU.mult, ALU.add))
            for compare, sign in ((ALU.is_gt, 1.0), (ALU.is_lt, -1.0)):
                chain.step(nc.vector.tensor_scalar(over[:], angle[:], sign * TWO_PI / 2, -sign * TWO_PI, compare, ALU.mult))
                chain.step(nc.vector.tensor_tensor(angle[:], angle[:], over[:], ALU.add))
            nc.vector.tensor_scalar(angle[:], angle[:], 3.1415925, -3.1415925, ALU.min, ALU.max).then_inc(angles_ready, 1)
            nc.vector.tensor_scalar(c_minus[:], W["C_im"][:], -1.0, None, ALU.mult)
            chain.step(nc.vector.tensor_scalar(keep[:], ident[0:D, 0:D], W["D"][:, 0:1], None, ALU.mult))
            chain.step(nc.vector.tensor_tensor(keep[:], keep[:], ident[0:D, 0:D], ALU.add))
            dve.wait_ge(exps, 3)
            nc.vector.memset(decays[:], 0.0)
            chain.step(nc.vector.memset(drive[:], 0.0))
            chain.step(nc.vector.tensor_scalar(decays[:, :, 1:S], decays[:, :, 1:S], decay[:, 0:1], None, ALU.add))
            dve.wait_ge(sines, 1)
            chain.step(nc.vector.tensor_scalar(wave_in[:], wave[:], gamma[:, 0:1], None, ALU.mult))

            def over_group(x, k):
                return x[:, k].rearrange("p (a s) -> p a s", a=1).broadcast_to([P, GROUP, S])

            for g in range(GROUPS):
                dve.wait_ge(bu_done, g + 1)
                re, im = (bank(2 * (g % 2) + k)[:, 0:GCOLS].rearrange("p (b s) -> p b s", s=S) for k in range(2))
                nc.vector.tensor_tensor(u4[:, 0], re, over_group(wave_in, 0), ALU.mult)
                nc.vector.tensor_tensor(u4[:, 1], im, over_group(wave_in, 1), ALU.mult)
                nc.vector.tensor_tensor(u4[:, 2], im, over_group(wave_in, 0), ALU.mult)
                ins = nc.vector.tensor_tensor(u4[:, 3], re, over_group(wave_in, 1), ALU.mult)
                ins.then_inc(bu_read, 1)
                dve.wait_ge(bu_read, g + 1)
                nc.vector.tensor_tensor(drive[:, 0], u4[:, 0], u4[:, 1], ALU.add)
                chain.step(nc.vector.tensor_tensor(drive[:, 1], u4[:, 2], u4[:, 3], ALU.subtract))
                flat = lambda x: x.rearrange("p b s -> p (b s)")
                nc.vector.tensor_tensor_scan(flat(state[:, 0]), flat(decays[:]), flat(drive[:, 0]), 0.0, ALU.mult, ALU.add)
                chain.step(nc.vector.tensor_tensor_scan(flat(state[:, 1]), flat(decays[:]), flat(drive[:, 1]), 0.0, ALU.mult, ALU.add))
                nc.vector.tensor_tensor(u4[:, 0], state[:, 0], over_group(wave, 0), ALU.mult)
                nc.vector.tensor_tensor(u4[:, 1], state[:, 1], over_group(wave, 1), ALU.mult)
                nc.vector.tensor_tensor(u4[:, 2], state[:, 1], over_group(wave, 0), ALU.mult)
                chain.step(nc.vector.tensor_tensor(u4[:, 3], state[:, 0], over_group(wave, 1), ALU.mult))
                cols = slice(g * GCOLS, (g + 1) * GCOLS)
                nc.vector.tensor_tensor(x_re[:, cols], flat(u4[:, 0]), flat(u4[:, 1]), ALU.subtract)
                nc.vector.tensor_tensor(x_im[:, cols], flat(u4[:, 2]), flat(u4[:, 3]), ALU.add).then_inc(x_done, 1)
                dve.wait_ge(x_done, g + 1)

        ctx.close()
        norm("n1a_", z)

    def single_expert1():
        ctx = ExitStack()
        local = lambda name, shape, dt=F32: sb(name, shape, dt, ctx)
        mark = lambda name: sem(name, ctx)
        E = 8
        z = local("z1", [P, TILES, D])
        inner = ExitStack()
        local1 = lambda name, shape, dt=F32: sb(name, shape, dt, inner)
        mark1 = lambda name: sem(name, inner)
        hidden = local1("hidden1", [P, 2, TP])
        score = local1("score1", [P, TILES, E])
        high, total = local1("high1", [P, TILES]), local1("total1", [P, TILES])
        weighed = local1("weighed1", [P, 2, E, D])
        (h_done, gelu_done, g_done, exp_wanted, exp_given, y_done, y_read, z_part, dve_done) = (mark1(n) for n in (
            "h_done", "gelu_done", "g_done", "exp_wanted", "exp_given", "y_done", "y_read", "z_part", "dve_done"))
        block = inner.enter_context(nc.Block())

        @block.tensor
        def _(pe):
            wait_weights(pe, "ffn1")
            k = 0
            for start, n in CHUNKS:
                for c in range(2):
                    if k >= 4:
                        pe.wait_ge(gelu_done, k - 3)
                    nc.tensor.matmul(bank(k % 4)[:, 0:n], W["f1w1"][:, c * P:(c + 1) * P], feat[:, start:start + n],
                                     start=True, stop=True).then_inc(h_done, 1)
                    k += 1
            pe.wait_ge(gelu_done, k)
            for t in range(TILES):
                cols = slice(t * P, (t + 1) * P)
                g = bank(6)[:, t * E:(t + 1) * E]
                nc.tensor.matmul(g, hidden[:, 0, cols], W["f1wg"][:, 0], start=True, stop=False)
                nc.tensor.matmul(g, hidden[:, 1, cols], W["f1wg"][:, 1], start=False, stop=False)
                mm = nc.tensor.matmul(g, ones_row[:], W["f1bg"][:], start=False, stop=True)
            mm.then_inc(g_done, 1)
            for t in range(TILES):
                cols = slice(t * P, (t + 1) * P)
                if t >= 2:
                    pe.wait_ge(y_read, t - 1)
                y = bank(4 + t % 2)
                for c in range(2):
                    nc.tensor.matmul(y, hidden[:, c, cols], W["f1wd"][:, c].rearrange("p e d -> p (e d)"),
                                     start=(c == 0), stop=False)
                nc.tensor.matmul(y, ones_row[:], W["f1bd"][:], start=False, stop=True).then_inc(y_done, 1)

        @block.scalar
        def _(act):
            wait_weights(act, "ffn1")
            k = 0
            for start, n in CHUNKS:
                for c in range(2):
                    act.wait_ge(h_done, k + 1)
                    nc.scalar.activation(hidden[:, c, start:start + n], bank(k % 4)[:, 0:n], ACT.Gelu,
                                         bias=W["f1b1"][:, c:c + 1]).then_inc(gelu_done, 1)
                    k += 1
            act.wait_ge(exp_wanted, 1)
            nc.scalar.activation(score[:], score[:], ACT.Exp).then_inc(exp_given, 1)

        @block.vector
        def _(dve):
            chain = Chain(dve, dve_done)
            dve.wait_ge(g_done, 1)
            logits = bank(6)[:, 0:TILES * E].rearrange("p (t e) -> p t e", e=E)
            chain.step(nc.vector.tensor_reduce(high[:], logits, AX.X, ALU.max))
            nc.vector.tensor_tensor(score[:], logits, per(high[:], E), ALU.subtract).then_inc(exp_wanted, 1)
            dve.wait_ge(exp_given, 1)
            chain.step(nc.vector.tensor_reduce(total[:], score[:], AX.X, ALU.add))
            chain.step(nc.vector.reciprocal(total[:], total[:]))
            chain.step(nc.vector.tensor_tensor(score[:], score[:], per(total[:], E), ALU.mult))
            first_largest(chain, gates[:], score[:], high[:], lane_index, E)
            chain.step(nc.vector.tensor_tensor(gates[:], gates[:], score[:], ALU.mult))
            for t in range(TILES):
                dve.wait_ge(y_done, t + 1)
                g = gates[:, t].rearrange("p (e a) -> p e a", a=1).broadcast_to([P, E, D])
                nc.vector.tensor_tensor(weighed[:, t % 2], bank(4 + t % 2).rearrange("p (e f) -> p e f", f=D), g,
                                        ALU.mult).then_inc(y_read, 1)
                dve.wait_ge(y_read, t + 1)
                nc.vector.tensor_reduce(z[:, t], weighed[:, t % 2].rearrange("p e f -> p f e"), AX.X,
                                        ALU.add).then_inc(z_part, 1)
            dve.wait_ge(z_part, TILES)
            chain.step(nc.vector.tensor_tensor(z[:], z[:], tok[:], ALU.add))

        inner.close()
        norm("n1f_", z[:].rearrange("p t f -> p (t f)"))
        ctx.close()

    def regrouped2():
        ctx = ExitStack()
        local = lambda name, shape, dt=F32: sb(name, shape, dt, ctx)
        mark = lambda name: sem(name, ctx)
        H, HD, R = 8, 8, IMAGES
        ROWS = S * H
        QUARTER = ROWS // 4
        qkv = local("qkv", [R, 3, S * D])
        q_high = local("q_high", [R, ROWS])
        q_turn = local("q_turn", [QUARTER, 4, R])
        q_top, q_wide = local("q_top", [QUARTER, 4]), local("q_wide", [QUARTER, 4, R])
        q_sum = local("q_sum", [R, ROWS])
        q_scale = local("q_scale", [S, H])
        k_high, k_sum = local("k_high", [R, H, HD]), local("k_sum", [R, H, HD])
        weights = local("weights", [S, H, S])
        v_turn = local("v_turn", [S, H, HD * R])
        mixed = local("mixed2", [S, D, R])
        mixT = local("mixT2", [D, TP])
        (p_done, p_read, dve_done, qh_done, qt_done, qw_done, qb_done, q_wanted, k_wanted, q_given, k_given, k_ready, qs_ready,
         qs_done, w_done, w_read, v_done, v_copied, o_done, o_read, t_done, t_copied, pad_set, z_done) = (mark(n) for n in (
             "p_done", "p_read", "dve_done", "qh_done", "qt_done", "qw_done", "qb_done", "q_wanted", "k_wanted", "q_given", "k_given",
             "k_ready", "qs_ready", "qs_done", "w_done", "w_read", "v_done", "v_copied", "o_done", "o_read", "t_done", "t_copied",
             "pad_set", "z_done"))
        z = psum[:, 0:TILES * D]
        PAIRS = (S + 1) // 2
        q3 = qkv[:, 0].rearrange("r (x d) -> r x d", d=HD)
        k4 = qkv[:, 1].rearrange("r (h n d) -> r h n d", h=H, d=HD)
        head = lambda i, h: qkv[:, i].rearrange("r (h n d) -> r h n d", h=H, d=HD)[:, h]
        block = ctx.enter_context(nc.Block())

        @block.gpsimd
        def _(pool):
            nc.gpsimd.memset(mixT[:, T:TP], 0.0).then_inc(pad_set, 1)

        @block.tensor
        def _(pe):
            wait_weights(pe, "attn2")
            w = W["a2"][:].rearrange("p i d -> p (i d)")
            for pair in range(PAIRS):
                if pair >= 4:
                    pe.wait_ge(p_read, pair - 3)
                for j in range(min(2, S - 2 * pair)):
                    mm = nc.tensor.matmul(bank(pair % 4)[0:R, j * 192:(j + 1) * 192],
                                          feat[:, 2 * pair + j:T:S], w, start=True, stop=True)
                mm.then_inc(p_done, 1)
            pe.wait_ge(qh_done, 1)
            for c in range(4):
                mm = nc.tensor.transpose(bank(4)[0:QUARTER, c * R:(c + 1) * R], q_high[:, c * QUARTER:(c + 1) * QUARTER],
                                         ident[0:R, 0:R])
            mm.then_inc(qt_done, 1)
            pe.wait_ge(qw_done, 1)
            for c in range(4):
                mm = nc.tensor.transpose(bank(5)[0:R, c * QUARTER:(c + 1) * QUARTER], q_wide[:, c, :],
                                         ident[0:QUARTER, 0:QUARTER])
            mm.then_inc(qb_done, 1)
            pe.wait_ge(p_read, PAIRS)
            for h in range(H):
                if h >= 2:
                    pe.wait_ge(v_copied, h - 1)
                for d in range(HD):
                    mm = nc.tensor.transpose(bank(6 + h % 2)[0:S, d * R:(d + 1) * R], head(2, h)[:, :, d], ident[0:R, 0:R])
                mm.then_inc(v_done, 1)
            pe.wait_ge(q_given, 1)
            pe.wait_ge(k_ready, 1)
            for h in range(H):
                for d in range(HD):
                    mm = nc.tensor.matmul(bank(0)[0:S, h * S:(h + 1) * S], head(1, h)[:, :, d], head(0, h)[:, :, d],
                                          start=(d == 0), stop=(d == HD - 1))
            mm.then_inc(w_done, 1)
            pe.wait_ge(qs_ready, 1)
            for h in range(H):
                mm = nc.tensor.matmul(bank(1)[0:S, h:h + 1], q_sum[:, h * S:(h + 1) * S], ones_col[0:R, 0:1],
                                      start=True, stop=True)
            mm.then_inc(qs_done, 1)
            pe.wait_ge(w_read, 1)
            for h in range(H):
                pe.wait_ge(v_copied, h + 1)
                if h >= 2:
                    pe.wait_ge(o_read, h - 1)
                nc.tensor.matmul(bank(2 + h % 2)[0:S, :], weights[:, h, :], v_turn[:, h, :],
                                 start=True, stop=True).then_inc(o_done, 1)
            pe.wait_ge(o_read, H)
            for g in range(GROUPS):
                if g >= 2:
                    pe.wait_ge(t_copied, g - 1)
                for j in range(GROUP):
                    mm = nc.tensor.transpose(bank(4 + g % 2)[0:D, j * S:(j + 1) * S], mixed[:, :, g * GROUP + j],
                                             ident[0:S, 0:S])
                mm.then_inc(t_done, 1)
            pe.wait_ge(t_copied, GROUPS)
            pe.wait_ge(pad_set, 1)
            close_block(pe, z, lambda t: [(mixT[:, t * P:(t + 1) * P], ident[0:D, 0:D])]).then_inc(z_done, 1)

        @block.scalar
        def _(act):
            act.wait_ge(q_wanted, 1)
            nc.scalar.activation(qkv[:, 0], qkv[:, 0], ACT.Exp).then_inc(q_given, 1)
            act.wait_ge(k_wanted, 1)
            nc.scalar.activation(qkv[:, 1], qkv[:, 1], ACT.Exp).then_inc(k_given, 1)
            for h in range(H):
                act.wait_ge(v_done, h + 1)
                nc.scalar.copy(v_turn[:, h, :], bank(6 + h % 2)[0:S, :]).then_inc(v_copied, 1)
            act.wait_ge(w_done, 1)
            nc.scalar.mul(weights[:].rearrange("p h s -> p (h s)"), bank(0)[0:S, 0:H * S],
                          float(R * HD) ** 0.5).then_inc(w_read, 1)
            for g in range(GROUPS):
                act.wait_ge(t_done, g + 1)
                nc.scalar.copy(mixT[:, g * GCOLS:(g + 1) * GCOLS], bank(4 + g % 2)[0:D, 0:GCOLS]).then_inc(t_copied, 1)

        @block.vector
        def _(dve):
            chain = Chain(dve, dve_done)
            wait_weights(dve, "attn2")
            for pair in range(PAIRS):
                n = min(2, S - 2 * pair)
                dve.wait_ge(p_done, pair + 1)
                for j in range(n):
                    c = 2 * pair + j
                    ins = nc.vector.tensor_tensor(
                        qkv[:, :, c * D:(c + 1) * D], bank(pair % 4)[0:R, j * 192:(j + 1) * 192].rearrange("p (i d) -> p i d", i=3),
                        W["a2b"][:], ALU.add)
                ins.then_inc(p_read, 1)
            dve.wait_ge(p_read, PAIRS)
            nc.vector.tensor_reduce(q_high[:], q3, AX.X, ALU.max).then_inc(qh_done, 1)
            chain.step(nc.vector.tensor_reduce(k_high[:], k4.rearrange("r h n d -> r h d n"), AX.X, ALU.max))
            over_rows = lambda x: x[:].rearrange("r h (a d) -> r h a d", a=1).broadcast_to([R, H, S, HD])
            nc.vector.tensor_tensor(k4, k4, over_rows(k_high), ALU.subtract).then_inc(k_wanted, 1)
            dve.wait_ge(qt_done, 1)
            chain.step(nc.vector.tensor_reduce(q_top[:], bank(4)[0:QUARTER, 0:4 * R].rearrange("p (c r) -> p c r", r=R), AX.X, ALU.max))
            nc.vector.tensor_copy(q_wide[:], q_top[:].rearrange("p (c a) -> p c a", a=1).broadcast_to([QUARTER, 4, R])).then_inc(qw_done, 1)
            dve.wait_ge(qb_done, 1)
            chain.step(nc.vector.tensor_copy(q_sum[:], bank(5)[0:R, 0:ROWS]))
            wide = q_sum[:].rearrange("r (x a) -> r x a", a=1).broadcast_to([R, ROWS, HD])
            nc.vector.tensor_tensor(q3, q3, wide, ALU.subtract).then_inc(q_wanted, 1)
            dve.wait_ge(k_given, 1)
            chain.step(nc.vector.tensor_reduce(k_sum[:], k4.rearrange("r h n d -> r h d n"), AX.X, ALU.add))
            chain.step(nc.vector.reciprocal(k_sum[:], k_sum[:]))
            nc.vector.tensor_tensor(k4, k4, over_rows(k_sum), ALU.mult).then_inc(k_ready, 1)
            dve.wait_ge(q_given, 1)
            nc.vector.tensor_reduce(q_sum[:], q3, AX.X, ALU.add).then_inc(qs_ready, 1)
            dve.wait_ge(qs_done, 1)
            chain.step(nc.vector.reciprocal(q_scale[:], bank(1)[0:S, 0:H]))
            for h in range(H):
                dve.wait_ge(o_done, h + 1)
                nc.vector.tensor_scalar(mixed[:, h * HD:(h + 1) * HD, :].rearrange("p d r -> p (d r)"), bank(2 + h % 2)[0:S, :],
                                        q_scale[:, h:h + 1], None, ALU.mult).then_inc(o_read, 1)

        ctx.close()
        norm("n2a_", z)

    def routed2():
        ctx = ExitStack()
        local = lambda name, shape, dt=F32: sb(name, shape, dt, ctx)
        mark = lambda name: sem(name, ctx)
        h0, h2 = local("h0", [P, TP]), local("h2", [P, TP])
        h1 = [local("h1_%d" % q, [P, S]) for q in range(2)]
        mine = [[local("mine%d%d" % (q, l), [P, P + 1]) for l in range(2)] for q in range(2)]
        (in_done, in_read, dve_done, ready, staged, one_done, one_read, two_done, two_read, pad_set, z_done,
         passed, dve_passed) = (mark(n) for n in (
             "in_done", "in_read", "dve_done", "ready", "staged", "one_done", "one_read", "two_done", "two_read", "pad_set",
             "z_done", "passed", "dve_passed"))
        z = psum[:, 0:TILES * D]
        ww = W["f2w"]
        block = ctx.enter_context(nc.Block())

        @block.gpsimd
        def _(pool):
            nc.gpsimd.memset(h2[:, T:TP], 0.0).then_inc(pad_set, 1)

        @block.vector
        def _(dve):
            chain = Chain(dve, dve_done)
            wait_weights(dve, "ffn2")
            for l in range(2):
                shared_w = W["f2ws"][:, l].rearrange("p (a o) -> p a o", a=1).broadcast_to([P, 16, P])
                eye = ident[:].rearrange("p (a o) -> p a o", a=1).broadcast_to([P, 16, P])
                chain.step(nc.vector.tensor_tensor(ww[:, l, :, 0:P], ww[:, l, :, 0:P], shared_w, ALU.add))
                chain.step(nc.vector.tensor_tensor(ww[:, l, :, 0:P], ww[:, l, :, 0:P], eye, ALU.add))
                chain.step(nc.vector.tensor_scalar(ww[:, l, :, P], W["f2br"][:, l], W["f2bs"][:, l:l + 1], None, ALU.add))
            dve.sem_inc(two_read, 2)
            with dve.Fori(0, IMAGES // 2) as i:
                for q in range(2):
                    e = dve.value_load(route[0:1, ds(i * 2 + q, 1)], min_val=0, max_val=15)
                    dve.wait_ge(two_read, i * 2 + (q + 1))
                    dve.sem_inc(dve_passed, 1)
                    for l in range(2):
                        ins = nc.vector.tensor_copy(mine[q][l][:], ww[:, l, ds(e, 1), :].rearrange("p a o -> p (a o)"))
                    ins.then_inc(staged, 1)

        @block.tensor
        def _(pe):
            wait_weights(pe, "ffn2")
            for c, (start, n) in enumerate(CHUNKS):
                if c >= 2:
                    pe.wait_ge(in_read, c - 1)
                nc.tensor.matmul(bank(c % 2)[:, 0:n], W["f2wi"][:], feat[:, start:start + n],
                                 start=True, stop=True).then_inc(in_done, 1)
            pe.wait_ge(in_read, len(CHUNKS))
            with pe.Fori(0, IMAGES // 2) as i:
                for q in range(2):
                    pe.wait_ge(staged, i * 2 + (q + 1))
                    pe.sem_inc(passed, 1)
                    nc.tensor.matmul(bank(2 + q)[:, 0:S], mine[q][0][:, 0:P], h0[:, ds(i * (2 * S) + q * S, S)],
                                     start=True, stop=True).then_inc(one_done, 1)
                for q in range(2):
                    pe.wait_ge(one_read, i * 2 + (q + 1))
                    nc.tensor.matmul(bank(4 + q)[:, 0:S], mine[q][1][:, 0:P], h1[q][:], start=True, stop=True).then_inc(two_done, 1)
            pe.wait_ge(two_read, IMAGES + 2)
            pe.wait_ge(pad_set, 1)
            close_block(pe, z, lambda t: [(h2[:, t * P:(t + 1) * P], W["f2wo"][:])], W["f2bo"][:]).then_inc(z_done, 1)

        @block.scalar
        def _(act):
            wait_weights(act, "ffn2")
            for c, (start, n) in enumerate(CHUNKS):
                act.wait_ge(in_done, c + 1)
                nc.scalar.activation(h0[:, start:start + n], bank(c % 2)[:, 0:n], ACT.Relu,
                                     bias=W["f2bi"][:, 0:1]).then_inc(in_read, 1)
            with act.Fori(0, IMAGES // 2) as i:
                for q in range(2):
                    act.wait_ge(one_done, i * 2 + (q + 1))
                    nc.scalar.activation(h1[q][:], bank(2 + q)[:, 0:S], ACT.Relu,
                                         bias=mine[q][0][:, P:P + 1]).then_inc(one_read, 1)
                for q in range(2):
                    act.wait_ge(two_done, i * 2 + (q + 1))
                    act.sem_inc(dve_passed, 1)
                    nc.scalar.activation(h2[:, ds(i * (2 * S) + q * S, S)], bank(4 + q)[:, 0:S], ACT.Relu,
                                         bias=mine[q][1][:, P:P + 1]).then_inc(two_read, 1)

        ctx.close()
        norm("n2f_", z)
    def heads3():
        ctx = ExitStack()
        local = lambda name, shape, dt=F32: sb(name, shape, dt, ctx)
        mark = lambda name: sem(name, ctx)
        H, HALF = 8, 64
        wkq, wvo = local("wkq", [D, H, D]), local("wvo", [D, 2, H // 2, D])
        x = [local("x%d" % q, [D, 2, HALF]) for q in range(2)]
        keys = [local("keys%d" % q, [D, H, 2, HALF]) for q in range(2)]
        values = [local("values%d" % q, [P, 2, H // 2 * D]) for q in range(2)]
        prob = [local("prob%d" % q, [P, H, HALF]) for q in range(2)]
        probT = [local("probT%d" % q, [P, H // 2, 2, HALF]) for q in range(2)]
        high, total = [local("high3_%d" % q, [P, H]) for q in range(2)], [local("total3_%d" % q, [P, H]) for q in range(2)]
        mixT = local("mixT3", [D, TP])
        (w_done, w_copied, ready, x_ready, k_done, k_copied, s_done, v_done, v_copied, exp_wanted, exp_given, p_ready,
         pT_done, pT_copied, o_done, o_read, dve_done, z_done, p_used, dve_passed, pe_passed) = (mark(n) for n in (
             "w_done", "w_copied", "ready", "x_ready", "k_done", "k_copied", "s_done", "v_done", "v_copied", "exp_wanted",
             "exp_given", "p_ready", "pT_done", "pT_copied", "o_done", "o_read", "dve_done", "z_done", "p_used", "dve_passed",
             "pe_passed"))
        z = psum[:, 0:TILES * D]
        PAIRS = IMAGES // 2
        block = ctx.enter_context(nc.Block())

        @block.gpsimd
        def _(pool):
            for q in range(2):
                nc.gpsimd.memset(x[q][:], 0.0).then_inc(ready, 1)
                nc.gpsimd.memset(prob[q][:], 0.0).then_inc(ready, 1)
            nc.gpsimd.memset(mixT[:, T:TP], 0.0).then_inc(ready, 1)

        @block.tensor
        def _(pe):
            wait_weights(pe, "attn3")
            for h in range(H):
                nc.tensor.matmul(bank(0)[0:D, h * D:(h + 1) * D], W["a3k"][:, h], W["a3q"][:, h], start=True, stop=True)
                mm = nc.tensor.matmul(bank(1)[0:D, (h % 2 * 4 + h // 2) * D:(h % 2 * 4 + h // 2 + 1) * D], W["a3k"][:, h],
                                      W["a3o"][:, h], start=True, stop=True)
            mm.then_inc(w_done, 1)
            pe.wait_ge(w_copied, 2)
            with pe.Fori(0, PAIRS // 2) as i:
                for q in range(2):
                    n1 = i * 2 + (q + 1)
                    pe.wait_ge(x_ready, n1)
                    pe.sem_inc(pe_passed, 1)
                    for h in range(H):
                        mm = nc.tensor.matmul(bank(h // 4)[0:D, (h % 4) * P:(h % 4 + 1) * P], wkq[:, h],
                                              x[q][:].rearrange("d b s -> d (b s)"), start=True, stop=True)
                    mm.then_inc(k_done, 1)
                    for b in range(2):
                        for s in range(2):
                            mm = nc.tensor.matmul(bank(2)[s * HALF:(s + 1) * HALF, b * 256:(b + 1) * 256], x[q][:, b],
                                                  wvo[:, s].rearrange("d h o -> d (h o)"), start=True, stop=True)
                    mm.then_inc(v_done, 1)
                    pe.wait_ge(k_copied, n1)
                    pe.sem_inc(pe_passed, 1)
                    for b in range(2):
                        mm = nc.tensor.matmul(bank(3 + q)[b * HALF:(b + 1) * HALF, 0:H * S], x[q][:, b], keys[q][:, :, b, 0:S],
                                              start=True, stop=True)
                    mm.then_inc(s_done, 1)
                    pe.wait_ge(p_ready, n1)
                    for k in range(H // 2):
                        mm = nc.tensor.transpose(bank(5)[:, k * P:(k + 1) * P],
                                                 prob[q][:, 2 * k:2 * k + 2].rearrange("p h s -> p (h s)"), ident[:])
                    mm.then_inc(pT_done, 1)
                    pe.wait_ge(pT_copied, n1)
                    pe.wait_ge(v_copied, n1)
                    pe.wait_ge(o_read, n1)
                    pe.sem_inc(pe_passed, 1)
                    for b in range(2):
                        for k in range(H // 2):
                            mm = nc.tensor.matmul(bank(6 + q)[0:D, b * S:(b + 1) * S], values[q][:, b, k * D:(k + 1) * D],
                                                  probT[q][:, k, b, 0:S], start=(k == 0), stop=(k == H // 2 - 1))
                    mm.then_inc(o_done, 1)
            pe.wait_ge(o_read, PAIRS + 2)
            close_block(pe, z, lambda t: [(mixT[:, t * P:(t + 1) * P], ident[0:D, 0:D])]).then_inc(z_done, 1)

        @block.scalar
        def _(act):
            act.wait_ge(w_done, 1)
            nc.scalar.copy(wkq[:].rearrange("d h e -> d (h e)"), bank(0)[0:D, :]).then_inc(w_copied, 1)
            nc.scalar.copy(wvo[:].rearrange("d s h e -> d (s h e)"), bank(1)[0:D, :]).then_inc(w_copied, 1)
            with act.Fori(0, PAIRS // 2) as i:
                for q in range(2):
                    n1 = i * 2 + (q + 1)
                    act.wait_ge(k_done, n1)
                    nc.scalar.copy(keys[q][:].rearrange("d h b s -> d (h b s)"), bank(0, 2)[0:D, :]).then_inc(k_copied, 1)
                    act.wait_ge(v_done, n1)
                    nc.scalar.copy(values[q][:].rearrange("p b o -> p (b o)"), bank(2)).then_inc(v_copied, 1)
                    act.wait_ge(exp_wanted, n1)
                    nc.scalar.activation(prob[q][:, :, 0:S], prob[q][:, :, 0:S], ACT.Exp, scale=D ** -0.5).then_inc(exp_given, 1)
                    act.wait_ge(pT_done, n1)
                    nc.scalar.copy(probT[q][:].rearrange("p k b s -> p (k b s)"), bank(5)).then_inc(pT_copied, 1)

        @block.vector
        def _(dve):
            dve.wait_ge(ready, 5)
            dve.sem_inc(o_read, 2)
            with dve.Fori(0, PAIRS // 2) as i:
                for q in range(2):
                    STEPS = 3
                    count = [0]

                    def step(ins):
                        count[0] += 1
                        ins.then_inc(dve_done, 1)
                        dve.wait_ge(dve_done, i * (2 * STEPS) + (q * STEPS + count[0]))

                    n1 = i * 2 + (q + 1)
                    dve.wait_ge(o_read, n1)
                    dve.sem_inc(dve_passed, 1)
                    nc.vector.tensor_copy(x[q][:, :, 0:S], feat[:, ds(i * (4 * S) + q * 2 * S, 2 * S)].rearrange(
                        "d (b s) -> d b s", s=S)).then_inc(x_ready, 1)
                for q in range(2):
                    n1 = i * 2 + (q + 1)
                    count = [0]

                    def step(ins, q=q, count=count):
                        count[0] += 1
                        ins.then_inc(dve_done, 1)
                        dve.wait_ge(dve_done, i * (2 * STEPS) + (q * STEPS + count[0]))

                    s3 = bank(3 + q)[:, 0:H * S].rearrange("p (h s) -> p h s", s=S)
                    wide = lambda v: v[q][:].rearrange("p (h a) -> p h a", a=1).broadcast_to([P, H, S])
                    p3 = prob[q][:, :, 0:S]
                    dve.wait_ge(s_done, n1)
                    step(nc.vector.tensor_reduce(high[q][:], s3, AX.X, ALU.max))
                    nc.vector.tensor_tensor(p3, s3, wide(high), ALU.subtract).then_inc(exp_wanted, 1)
                    dve.wait_ge(exp_given, n1)
                    step(nc.vector.tensor_reduce(total[q][:], p3, AX.X, ALU.add))
                    step(nc.vector.reciprocal(total[q][:], total[q][:]))
                    nc.vector.tensor_tensor(p3, p3, wide(total), ALU.mult).then_inc(p_ready, 1)
                for q in range(2):
                    n1 = i * 2 + (q + 1)
                    dve.wait_ge(o_done, n1)
                    dve.sem_inc(dve_passed, 1)
                    nc.vector.tensor_copy(mixT[:, ds(i * (4 * S) + q * 2 * S, 2 * S)], bank(6 + q)[0:D, 0:2 * S]).then_inc(o_read, 1)

        ctx.close()
        norm("n3a_", z)

    def experts3():
        ctx = ExitStack()
        z = sb("z3", [P, TILES, D], F32, ctx)
        inner = ExitStack()
        mark1 = lambda name: sem(name, inner)
        score = sb("score3", [P, TILES, 8], F32, inner)
        g_done, exp_wanted, exp_given, dve_done = (mark1(n) for n in ("g_done3", "exp_wanted3", "exp_given3", "dve_done3"))
        shared = {}
        block = inner.enter_context(nc.Block())

        @block.tensor
        def _(pe):
            wait_weights(pe, "ffn3")
            for t in range(TILES):
                g = bank(6)[:, t * 8:(t + 1) * 8]
                nc.tensor.matmul(g, feat[:, t * P:(t + 1) * P], W["f3wg"][:], start=True, stop=False)
                mm = nc.tensor.matmul(g, ones_row[:], W["f3bg"][:], start=False, stop=True)
            mm.then_inc(g_done, 1)

        @block.vector
        def _(dve):
            chain = Chain(dve, dve_done)
            dve.wait_ge(g_done, 1)
            chain.step(nc.vector.tensor_copy(score[:], bank(6)[:, 0:TILES * 8].rearrange("p (t e) -> p t e", e=8)))
            gap, finish = top_two(chain, "g3", inner, score[:], 8, exp_wanted, exp_given)
            shared["gap"] = gap
            chain.step(finish())

        @block.scalar
        def _(act):
            act.wait_ge(exp_wanted, 1)
            nc.scalar.activation(shared["gap"][:], shared["gap"][:], ACT.Exp).then_inc(exp_given, 1)

        inner.close()
        experts("e3_", "ffn3", 8, 2, W["f3w1"], W["f3b1"], W["f3w2"], W["f3b2"], z)
        norm("n3f_", z[:].rearrange("p t f -> p (t f)"))
        ctx.close()

    STAGES = [[tokens_and_keys], [attention0], [graph_gates, experts0], [recurrent1], [single_expert1], [regrouped2], [routed2], [heads3], [experts3]]

    for stages in STAGES[:stop + 1]:
        for stage in stages:
            stage()
            nc.clear_and_free_semaphores(stage_semaphores)
            nc.all_engine_barrier()
            stage_semaphores.clear()

    ctx = ExitStack()
    written = sem("written")
    block = ctx.enter_context(nc.Block())

    @block.sync
    def _(sp):
        rows_out = out.rearrange("b s d -> (b s) d")
        whole = T // P
        sp.dma_start(rows_out[0:whole * P].rearrange("(t p) d -> p t d", p=P), tok[:, 0:whole, :]).then_inc(written, 16)
        sp.dma_start(rows_out[whole * P:T], tok[0:T - whole * P, whole, :]).then_inc(written, 16)
        for part in loads:
            wait_weights(sp, part)
        sp.wait_ge(written, 32)

    ctx.close()
    top.close()


def laid_out(inputs):
    import numpy as np

    A = {k: np.asarray(v) for k, v in inputs.items() if k not in ("L3_attn_wv",)}
    for n in ("L0_attn_Wq", "L0_attn_Wk", "L0_attn_Wv", "L0_attn_Wo", "L2_attn_Wq", "L2_attn_Wk", "L2_attn_Wv",
              "L2_ffn_Wi", "L2_ffn_Wo", "L0_ffn_b1"):
        A[n] = A[n].T
    for n in ("L0_ffn_att_src", "L0_ffn_att_dst"):
        A[n] = A[n].reshape(16)
    A["L1_ffn_b1"] = A["L1_ffn_b1"].reshape(2, 128).T
    A["L3_ffn_b1"] = A["L3_ffn_b1"].reshape(16, 128).T
    A["L2_ffn_Wr"] = A["L2_ffn_Wr"].transpose(0, 1, 3, 2)
    A["L2_ffn_Ws"] = A["L2_ffn_Ws"][:, 0].transpose(0, 2, 1)
    A["L2_ffn_br"] = A["L2_ffn_br"].transpose(2, 0, 1)
    A["L2_ffn_bs"] = A["L2_ffn_bs"][:, 0].T
    A["L3_attn_wq"] = A["L3_attn_wq"].transpose(0, 2, 1)
    A["L3_attn_wk"] = A["L3_attn_wk"].transpose(0, 2, 1)
    return {k: np.ascontiguousarray(v) for k, v in A.items()}


def kernel(**inputs):
    import numpy as np
    import concourse.bacc as bacc
    from concourse import mybir
    from concourse.bass_utils import run_bass_kernel_spmd as run

    nc = bacc.Bacc("TRN2", target_bir_lowering=False, num_devices=1)
    arrays = laid_out(inputs)
    aps = {k: nc.dram_tensor("in_" + k, a.shape, mybir.dt.from_np(a.dtype), kind="ExternalInput").ap()
           for k, a in arrays.items()}
    out = nc.dram_tensor("out", (64, 51, 64), mybir.dt.float32, kind="ExternalOutput").ap()
    vit_tower(nc, aps, out, STOP)
    r = run(nc, [{"in_" + k: a for k, a in arrays.items()}], core_ids=[0])
    return r.results[0]["out"]


STOP = 99
```

```python
class Chain:

    def __init__(self, engine, done):
        self.engine, self.done, self.count = engine, done, 0

    def step(self, instruction):
        self.count += 1
        instruction.then_inc(self.done, 1)
        self.engine.wait_ge(self.done, self.count)


def vit_tower(nc, A, out, stop):
    import concourse.bass as bass
    from concourse import mybir
    from contextlib import ExitStack

    F32, BF16, I32, U32 = mybir.dt.float32, mybir.dt.bfloat16, mybir.dt.int32, mybir.dt.uint32
    ALU, ACT, AX = mybir.AluOpType, mybir.ActivationFunctionType, mybir.AxisListType
    ts, ds = bass.ts, bass.ds

    P = 128
    IMAGES, S, D = 64, 51, 64
    T = IMAGES * S
    TILES = (T + P - 1) // P
    TP = TILES * P
    BANK = 512
    PATCH_COLS, STRIDE_COLS, PATCH_ROWS, NH, NW = 25, 12, 64, 3, 17
    GROUP = 8
    GCOLS = GROUP * S
    GROUPS = IMAGES // GROUP
    CHUNKS = [(c, min(BANK, TP - c)) for c in range(0, TP, BANK)]
    EDGES = A["L0_ffn_edge_index"].shape[1]
    EC = EDGES // P
    LN_EPS = 1e-5

    top = ExitStack()
    sb = lambda name, shape, dt=F32, ctx=top: ctx.enter_context(nc.sbuf_tensor(name, shape, dt))
    stage_semaphores, serial = [], [0]

    def sem(name, ctx=top):
        if ctx is top:
            return ctx.enter_context(nc.semaphore(name))
        serial[0] += 1
        stage_semaphores.append(nc.alloc_semaphore("%s_%d" % (name, serial[0])))
        return stage_semaphores[-1]

    psum = top.enter_context(nc.psum_tensor("psum", [P, 8 * BANK], F32))

    def bank(k, n=1):
        return psum[:, k * BANK:(k + n) * BANK]

    tok = sb("tok", [P, TILES, D])
    feat = sb("feat", [P, TP])
    ident = sb("ident", [P, P])
    ones_col = sb("ones_col", [P, 1])
    table = nc.dram_tensor("node_table", (TP, 20), F32, kind="Internal").ap()

    W, loads = {}, {}

    def weight(part, name, shape, src):
        W[name] = sb("w_" + name, shape)
        loads.setdefault(part, []).append((W[name], src))

    padded = sb("padded", [P, 5200])
    padded_end = [0]

    def take(n):
        padded_end[0] += n
        assert padded_end[0] <= padded.shape[1]
        return padded[:, padded_end[0] - n:padded_end[0]]

    def weight64(part, name, n, src):
        W[name] = take(n)
        loads.setdefault(part, []).append((W[name][0:D], src))

    def bias64(part, name, n, src):
        W[name] = take(n)
        loads.setdefault(part, []).append((W[name][D:D + 1], src))

    def row(ap):
        return ap.rearrange("(a n) -> a n", a=1)

    def column(ap):
        return ap.rearrange("(n a) -> n a", a=1)

    def spread(ap, n):
        return ap.rearrange("(a n) -> a n", a=1).broadcast_to([n, ap.shape[0]])

    tw = A["L0_tok_weight"].rearrange("(r c) o -> r c o", c=PATCH_COLS)
    W["tok"] = sb("w_tok", [P, 13, D])
    loads["tok"] = [(W["tok"][0:64], tw[:, 0::2, :]), (W["tok"][64:128, 0:12], tw[:, 1::2, :])]
    weight("tok", "tok_b", [D, 1], column(A["L0_tok_bias"]))
    for n in "qkv":
        weight64("attn0", "a0" + n, D, A["L0_attn_W" + n])
    for n in "qk":
        weight("attn0", "a0b" + n, [D, 1], column(A["L0_attn_b" + n]))
    W["a0bm"] = sb("w_a0bm", [S, 2])
    W["a0o"] = sb("w_a0o", [D + 1, D])
    loads["attn0"] += [(W["a0bm"][:, 0:1], spread(A["L0_attn_bq"][0:1], S)),
                       (W["a0bm"][:, 1:2], spread(A["L0_attn_bk"][0:1], S)),
                       (W["a0o"][0:D], A["L0_attn_Wo"]), (W["a0o"][D:D + 1], row(A["L0_attn_bo"]))]
    weight("attn0", "a0bv", [S, D], spread(A["L0_attn_bv"], S))
    weight64("gat", "gat", 16, A["L0_ffn_W_gat"])
    for n in ("att_src", "att_dst", "b_gat", "ln_gamma", "ln_beta"):
        weight("gat", n, [P, 16], spread(A["L0_ffn_" + n], P))
    W["f0w1"] = take(4 * P).rearrange("p (e h) -> p e h", h=P)
    loads["ffn0"] = [(W["f0w1"][0:D], A["L0_ffn_W1"].rearrange("e d h -> d e h"))]
    weight("ffn0", "f0b1", [P, 4], A["L0_ffn_b1"])
    weight("ffn0", "f0w2", [P, 4, D], A["L0_ffn_W2"].rearrange("e h d -> h e d"))
    bias64("ffn0", "f0b2", 4 * D, A["L0_ffn_b2"].rearrange("(a e) d -> a (e d)", a=1))
    for n in ("B_re", "B_im"):
        weight64("attn1", n, P, A["L1_attn_" + n])
    for n in ("C_re", "C_im"):
        weight("attn1", n, [P, D], A["L1_attn_" + n])
    weight("attn1", "D", [D, 1], column(A["L1_attn_D"]))
    for n in ("nu", "theta", "gamma_log"):
        weight("attn1", n, [P, 1], column(A["L1_attn_" + n]))
    weight64("ffn1", "f1w1", 256, A["L1_ffn_W1"])
    weight("ffn1", "f1b1", [P, 2], A["L1_ffn_b1"])
    weight("ffn1", "f1wg", [P, 2, 8], A["L1_ffn_Wg"].rearrange("(c p) e -> p c e", p=P))
    bias64("ffn1", "f1bg", 8, row(A["L1_ffn_bg"]))
    W["f1wd"] = sb("w_f1wd", [P, 2, 8, D])
    for c in range(2):
        loads["ffn1"].append((W["f1wd"][:, c], A["L1_ffn_Wd"][:, c * P:(c + 1) * P, :].rearrange("e p d -> p e d")))
    bias64("ffn1", "f1bd", 8 * D, A["L1_ffn_bd"].rearrange("(a e) d -> a (e d)", a=1))
    W["a2"] = take(3 * D).rearrange("p (i d) -> p i d", i=3)
    W["a2b"] = sb("w_a2b", [D, 3, D])
    loads["attn2"] = []
    for i, n in enumerate("qkv"):
        loads["attn2"] += [(W["a2"][0:D, i], A["L2_attn_W" + n]), (W["a2b"][:, i], spread(A["L2_attn_b" + n], D))]
    weight64("ffn2", "f2wi", P, A["L2_ffn_Wi"])
    weight("ffn2", "f2bi", [P, 1], column(A["L2_ffn_bi"]))
    W["f2w"] = sb("w_f2w", [P, 2, 16, P + 1])
    weight("ffn2", "f2ws", [P, 2, P], A["L2_ffn_Ws"].rearrange("l i o -> i l o"))
    weight("ffn2", "f2bs", [P, 2], A["L2_ffn_bs"])
    weight("ffn2", "f2br", [P, 2, 16], A["L2_ffn_br"])
    weight("ffn2", "f2wo", [P, D], A["L2_ffn_Wo"])
    bias64("ffn2", "f2bo", D, row(A["L2_ffn_bo"]))
    for layer in range(2):
        loads["ffn2"].append((W["f2w"][:, layer, :, 0:P], A["L2_ffn_Wr"][layer].rearrange("e i o -> i e o")))
    route = sb("route", [1, IMAGES], I32)
    loads["ffn2"].append((route, row(A["L2_ffn_route_id"])))
    weight("attn3", "a3q", [D, 8, D], A["L3_attn_wq"].rearrange("h e d -> e h d"))
    weight("attn3", "a3k", [D, 8, D], A["L3_attn_wk"].rearrange("h e d -> e h d"))
    weight("attn3", "a3o", [D, 8, D], A["L3_attn_wo"].rearrange("(h e) d -> e h d", e=D))
    weight64("ffn3", "f3wg", 8, A["L3_ffn_Wg"])
    loads["ffn3"].append((W["f3wg"][D:D + 1], row(A["L3_ffn_bg"])))
    W["f3w1"] = take(16 * P).rearrange("p (m h) -> p m h", h=P)
    W["f3w2"] = sb("w_f3w2", [P, 16, D])
    for e in range(8):
        loads["ffn3"] += [(W["f3w1"][0:D, 2 * e:2 * e + 2], A["L3_ffn_W1"][e].rearrange("d (c h) -> d c h", c=2)),
                          (W["f3w2"][:, 2 * e:2 * e + 2], A["L3_ffn_W2"][e].rearrange("(c h) d -> h c d", c=2))]
    weight("ffn3", "f3b1", [P, 16], A["L3_ffn_b1"])
    bias64("ffn3", "f3b2", 8 * D, A["L3_ffn_b2"].rearrange("(a e) d -> a (e d)", a=1))
    loaded = {part: sem("loaded_" + part) for part in loads}

    def load(engine, *parts):
        for part in parts:
            for tile, src in loads[part]:
                engine.dma_start(tile if isinstance(tile, bass.AP) else tile[:], src).then_inc(loaded[part], 16)

    def wait_weights(engine, part):
        engine.wait_ge(loaded[part], 16 * len(loads[part]))

    def ap(x):
        return x if isinstance(x, bass.AP) else x[:]

    SORTS = 2
    SC = EC // SORTS
    SLOTS = 8
    DEPTH = 4
    LEAD = 2
    EP = EC + (LEAD + DEPTH) * SLOTS
    edge_src = sb("edge_src", [P, EP], U32)
    edge_dlo = sb("edge_dlo", [P, EP])
    edge_dhi = sb("edge_dhi", [P, EP])
    eights = sb("eights", [P, SORTS], I32)
    trips = sb("trips", [P, 1], I32)
    MAX_TRIPS = EC // SLOTS // DEPTH

    def tokens_and_keys():
        ctx = ExitStack()
        local = lambda name, shape, dt=F32: sb(name, shape, dt, ctx)
        mark = lambda name: sem(name, ctx)
        rows = local("rows", [P, 2, GROUP * NH, 224])
        e_src, e_dst = local("e_src", [P, EC], I32), local("e_dst", [P, EC], I32)
        key, valid, order = local("key", [P, EC]), local("valid", [P, EC]), local("order", [P, EP])
        field = local("field", [P, EP], I32)
        as_int = local("as_int", [P, EP], I32)
        top8, spare = local("top8", [P, 8]), local("spare", [1, 2])
        count, most = local("count", [P, SORTS]), local("most", [P, SORTS])
        rows_in = [mark("rows_in0"), mark("rows_in1")]
        padded_clear = mark("padded_clear")
        edges_in, patches_done, gelu_done, counted, most_known = (
            mark(n) for n in ("edges_in", "patches_done", "gelu_done", "counted", "most_known"))
        dve_done, consts_done, pool_done = mark("dve_done"), mark("consts_done"), mark("pool_done")
        sort_done = [mark("sort_done") for c in range(SORTS)]

        block = ctx.enter_context(nc.Block())

        @block.sync
        def _(sp):
            load(sp, "tok")
            for h, t in enumerate((e_src, e_dst)):
                sp.dma_start(t[:], A["L0_ffn_edge_index"][h].rearrange("(p c) -> p c", p=P)).then_inc(edges_in, 16)
            for g in range(GROUPS):
                if g >= 2:
                    sp.wait_ge(patches_done, g - 1)
                for half in range(2):
                    img = A["x"][g * GROUP:(g + 1) * GROUP, 0, 0:NH * PATCH_ROWS, half:224]
                    for n in range(NH):
                        sp.dma_start(
                            rows[64 * half:64 * half + 64, g % 2, n::NH, 0:224 - half],
                            img[:, n * PATCH_ROWS:(n + 1) * PATCH_ROWS, :].rearrange("b r c -> r b c"),
                        ).then_inc(rows_in[g % 2], 16)
            sp.wait_ge(padded_clear, 1)
            load(sp, *[p for p in loads if p != "tok"])

        @block.gpsimd
        def _(pool):
            chain = Chain(pool, pool_done)
            nc.gpsimd.memset(padded[:], 0.0).then_inc(padded_clear, 1)
            pool.wait_ge(padded_clear, 1)
            chain.step(nc.gpsimd.memset(feat[D:P, :], 0.0))
            nc.gpsimd.memset(feat[D:D + 1, :], 1.0).then_inc(consts_done, 1)
            pool.wait_ge(consts_done, 1)
            nc.gpsimd.memset(ones_col[:], 1.0).then_inc(consts_done, 1)
            pool.wait_ge(consts_done, 2)
            nc.gpsimd.memset(feat[0:D, T:TP], 0.0).then_inc(consts_done, 1)
            pool.wait_ge(consts_done, 3)
            chain.step(nc.gpsimd.memset(ident[:], 0.0))
            nc.gpsimd.affine_select(out=ident[:], in_=ident[:], compare_op=ALU.not_equal, fill=1.0, base=0,
                                    pattern=[[-1, P]], channel_multiplier=1).then_inc(consts_done, 1)
            pool.wait_ge(counted, 1)
            nc.gpsimd.partition_all_reduce(most[:], count[:], P, bass.bass_isa.ReduceOp.max).then_inc(most_known, 1)

        @block.tensor
        def _(pe):
            wait_weights(pe, "tok")
            for g in range(GROUPS):
                pe.wait_ge(rows_in[g % 2], 16 * 2 * NH * (g // 2 + 1))
                if g >= 2:
                    pe.wait_ge(gelu_done, g - 1)
                for k in range(13):
                    K = P if k < 12 else PATCH_ROWS
                    mm = nc.tensor.matmul(bank(g % 2)[0:D, 0:GCOLS], W["tok"][0:K, k, :],
                                          rows[0:K, g % 2, :, 2 * k:2 * k + STRIDE_COLS * (NW - 1) + 1:STRIDE_COLS],
                                          start=(k == 0), stop=(k == 12))
                mm.then_inc(patches_done, 1)

        @block.scalar
        def _(act):
            wait_weights(act, "tok")
            for g in range(GROUPS):
                act.wait_ge(patches_done, g + 1)
                nc.scalar.activation(feat[0:D, g * GCOLS:(g + 1) * GCOLS], bank(g % 2)[0:D, 0:GCOLS], ACT.Gelu,
                                     bias=W["tok_b"][:, 0:1]).then_inc(gelu_done, 1)
            act.wait_ge(consts_done, 4)

        @block.vector
        def _(dve):
            chain = Chain(dve, dve_done)
            dve.wait_ge(edges_in, 32)
            nc.vector.tensor_scalar(order[:, 0:EC], e_src[:], float(T - 1), None, ALU.min)
            chain.step(nc.vector.tensor_scalar(valid[:], e_dst[:], float(T), None, ALU.is_lt))
            nc.vector.tensor_reduce(count[:], valid[:].rearrange("p (s c) -> p s c", s=SORTS), AX.X, ALU.add).then_inc(counted, 1)
            chain.step(nc.vector.scalar_tensor_tensor(key[:], e_dst[:], 4096.0, order[:, 0:EC], ALU.mult, ALU.add))
            chain.step(nc.vector.scalar_tensor_tensor(key[:], key[:], 1.0, valid[:], ALU.add, ALU.mult))
            chain.step(nc.vector.tensor_scalar(key[:], key[:], -1.0, None, ALU.add))
            chain.step(nc.vector.memset(order[:], -1.0))
            dve.wait_ge(most_known, 1)
            chain.step(nc.vector.tensor_scalar(eights[:], most[:], 7.0, 8.0, ALU.add, ALU.max))
            chain.step(nc.vector.tensor_scalar(eights[:], eights[:], 3, None, ALU.arith_shift_right))
            chain.step(nc.vector.tensor_reduce(count[:, 0:1], eights[:], AX.X, ALU.add))
            chain.step(nc.vector.tensor_scalar(trips[:], count[:, 0:1], float(DEPTH - 1), None, ALU.add))
            chain.step(nc.vector.tensor_scalar(trips[:], trips[:], 2, None, ALU.arith_shift_right))
            base = 0
            for c in range(SORTS):
                part = key[:, c * SC:(c + 1) * SC]
                n_eights = dve.value_load(eights[0:1, c:c + 1], min_val=1, max_val=SC // 8)
                with dve.Fori(0, n_eights) as i:
                    nc.vector.max(top8[:], part).then_inc(sort_done[c], 1)
                    dve.wait_ge(sort_done[c], i * 2 + 1)
                    nc.vector.memset(spare[:, 0:1], 0.0)
                    nc.vector.tensor_copy(order[:, ds((base + i) * 8, 8)], top8[:])
                    nc.vector.match_replace(part, top8[:], part, -1.0).then_inc(sort_done[c], 1)
                    dve.wait_ge(sort_done[c], i * 2 + 2)
                    nc.vector.memset(spare[:, 1:2], 0.0)
                base = base + n_eights
            chain.step(nc.vector.tensor_copy(as_int[:], order[:]))
            chain.step(nc.vector.tensor_scalar(field[:], as_int[:], 4095, None, ALU.bitwise_and))
            chain.step(nc.vector.tensor_scalar(edge_src[:], field[:], float(T - 1), None, ALU.min))
            chain.step(nc.vector.tensor_scalar(field[:], as_int[:], 12, 127, ALU.arith_shift_right, ALU.bitwise_and))
            chain.step(nc.vector.tensor_copy(edge_dlo[:], field[:]))
            chain.step(nc.vector.tensor_scalar(field[:], as_int[:], 19, None, ALU.arith_shift_right))
            chain.step(nc.vector.tensor_copy(edge_dhi[:], field[:]))

        ctx.close()

    def norm(name, z):
        ctx = ExitStack()
        mark = lambda n: sem(name + n, ctx)
        mean = sb(name + "mean", [P, TILES], F32, ctx)
        var = sb(name + "var", [P, TILES], F32, ctx)
        eps = sb(name + "eps", [P, 1], F32, ctx)
        squares = sb(name + "squares", [P, TILES, D], F32, ctx)
        dve_done, var_done, std_done, tok_done, turned, copied = (
            mark(n) for n in ("dve_done", "var_done", "std_done", "tok_done", "turned", "copied"))
        z3 = z.rearrange("p (t f) -> p t f", f=D)
        block = ctx.enter_context(nc.Block())

        def wide(x):
            return x[:].rearrange("p (t a) -> p t a", a=1).broadcast_to([P, TILES, D])

        @block.vector
        def _(dve):
            chain = Chain(dve, dve_done)
            nc.vector.memset(eps[:], LN_EPS)
            chain.step(nc.vector.tensor_reduce(mean[:], z3, AX.X, ALU.add))
            chain.step(nc.vector.tensor_scalar(mean[:], mean[:], 1.0 / D, None, ALU.mult))
            chain.step(nc.vector.tensor_tensor(tok[:], z3, wide(mean), ALU.subtract))
            chain.step(nc.vector.tensor_tensor(squares[:], tok[:], tok[:], ALU.mult))
            nc.vector.tensor_reduce(var[:], squares[:], AX.X, ALU.add).then_inc(var_done, 1)
            dve.wait_ge(std_done, 1)
            chain.step(nc.vector.reciprocal(mean[:], var[:]))
            nc.vector.tensor_tensor(tok[:], tok[:], wide(mean), ALU.mult).then_inc(tok_done, 1)

        @block.scalar
        def _(act):
            act.wait_ge(var_done, 1)
            nc.scalar.activation(var[:], var[:], ACT.Sqrt, bias=eps[:, 0:1], scale=1.0 / D).then_inc(std_done, 1)
            for c, (start, n) in enumerate(CHUNKS):
                act.wait_ge(turned, c + 1)
                nc.scalar.copy(feat[0:D, start:start + n], bank(c)[0:D, 0:n]).then_inc(copied, 1)

        @block.tensor
        def _(pe):
            pe.wait_ge(tok_done, 1)
            for c, (start, n) in enumerate(CHUNKS):
                for j in range(n // P):
                    mm = nc.tensor.transpose(bank(c)[0:D, j * P:(j + 1) * P], tok[:, start // P + j, :], ident[:])
                mm.then_inc(turned, 1)

        ctx.close()

    def close_block(pe, z, branch, bias=None, done=None):
        for t in range(TILES):
            pairs = list(branch(t)) + [(feat[:, t * P:(t + 1) * P], ident[:, 0:D])]
            if bias is not None:
                pairs.append((feat[:, t * P:(t + 1) * P], bias))
            for i, (l, r) in enumerate(pairs):
                mm = nc.tensor.matmul(z[:, t * D:(t + 1) * D], l, r, start=(i == 0), stop=(i == len(pairs) - 1))
        return mm

    def attention0():
        ctx = ExitStack()
        local = lambda name, shape, dt=F32: sb(name, shape, dt, ctx)
        mark = lambda name: sem(name, ctx)
        qT, kT = local("qT", [P, T]), local("kT", [P, T])
        v = local("v", [P, IMAGES, D])
        mask2, mask = local("mask2", [S, IMAGES, 2]), local("mask", [S, IMAGES])
        prob = local("prob", [S, 2, GROUP, S])
        probT = local("probT", [P, 2, GROUP, S])
        high, total = local("high", [S, 2, GROUP]), local("total", [S, 2, GROUP])
        mixT = local("mixT", [D + 1, TP])
        proj_done, proj_copied, v_done, v_copied, m_done = (mark(n) for n in ("proj_done", "proj_copied", "v_done", "v_copied", "m_done"))
        s_done, s_read, exp_in, exp_done, p_done, pT_done, pT_copied, mix_done, mix_copied, dve_done, mixT_set, z_done = (
            mark(n) for n in ("s_done", "s_read", "exp_in", "exp_done", "p_done", "pT_done", "pT_copied", "mix_done",
                              "mix_copied", "dve_done", "mixT_set", "z_done"))
        z = psum[:, 0:TILES * D]
        block = ctx.enter_context(nc.Block())
        PCH = [(c, min(BANK, T - c)) for c in range(0, T, BANK)]

        @block.tensor
        def _(pe):
            wait_weights(pe, "attn0")
            n_proj = 0
            for c, (start, n) in enumerate(PCH):
                for w in ("a0q", "a0k"):
                    if n_proj >= 2:
                        pe.wait_ge(proj_copied, n_proj - 1)
                    nc.tensor.matmul(bank(n_proj % 2)[0:D, 0:n], W[w][:], feat[:, start:start + n],
                                     start=True, stop=True).then_inc(proj_done, 1)
                    n_proj += 1
            pe.wait_ge(mixT_set, 6)
            for g in range(GROUPS):
                if g >= 2:
                    pe.wait_ge(v_copied, g - 1)
                for j in range(GROUP):
                    b = g * GROUP + j
                    x_b = feat[:, b * S:(b + 1) * S]
                    for i, w in enumerate(("a0q", "a0k")):
                        nc.tensor.matmul(bank(4)[0:S, 2 * b + i:2 * b + i + 1], x_b, W[w][:, 0:1], start=True, stop=True)
                    mm = nc.tensor.matmul(bank(2 + g % 2)[0:S, j * D:(j + 1) * D], x_b, W["a0v"][:], start=True, stop=True)
                mm.then_inc(v_done, 1)
            pe.wait_ge(proj_copied, n_proj)

            def scores(g):
                if g >= 2:
                    pe.wait_ge(s_read, g - 1)
                for j in range(GROUP):
                    b = g * GROUP + j
                    mm = nc.tensor.matmul(bank(g % 2)[0:S, j * S:(j + 1) * S], qT[:, b * S:(b + 1) * S],
                                          kT[:, b * S:(b + 1) * S], start=True, stop=True)
                mm.then_inc(s_done, 1)

            def mix(g):
                pe.wait_ge(p_done, g + 1)
                pe.wait_ge(v_copied, g + 1)
                if g >= 1:
                    pe.wait_ge(pT_copied, g)
                for j in range(GROUP):
                    mm = nc.tensor.transpose(bank(5)[0:S, j * S:(j + 1) * S], prob[:, g % 2, j, :], ident[0:S, 0:S])
                mm.then_inc(pT_done, 1)
                pe.wait_ge(pT_copied, g + 1)
                if g >= 2:
                    pe.wait_ge(mix_copied, g - 1)
                for j in range(GROUP):
                    mm = nc.tensor.matmul(bank(6 + g % 2)[0:D, j * S:(j + 1) * S], v[:, g * GROUP + j, :],
                                          probT[:, g % 2, j, :], start=True, stop=True)
                mm.then_inc(mix_done, 1)

            for g in range(GROUPS + 1):
                if g < GROUPS:
                    scores(g)
                if g >= 1:
                    mix(g - 1)
            pe.wait_ge(mix_copied, GROUPS)
            pe.wait_ge(mixT_set, 6)
            close_block(pe, z, lambda t: [(mixT[:, t * P:(t + 1) * P], W["a0o"][:])]).then_inc(z_done, 1)

        @block.scalar
        def _(act):
            wait_weights(act, "attn0")
            n_proj = 0
            for c, (start, n) in enumerate(PCH):
                for dst, b in ((qT, "a0bq"), (kT, "a0bk")):
                    act.wait_ge(proj_done, n_proj + 1)
                    nc.scalar.activation(dst[0:D, start:start + n], bank(n_proj % 2)[0:D, 0:n], ACT.Identity,
                                         bias=W[b][:, 0:1]).then_inc(proj_copied, 1)
                    n_proj += 1
            act.wait_ge(mixT_set, 6)
            for g in range(GROUPS):
                act.wait_ge(exp_in, g + 1)
                nc.scalar.activation(prob[:, g % 2], prob[:, g % 2], ACT.Exp, scale=D ** -0.5).then_inc(exp_done, 1)
                act.wait_ge(pT_done, g + 1)
                nc.scalar.copy(probT[0:S, g % 2].rearrange("p a b -> p (a b)"), bank(5)[0:S, 0:GCOLS]).then_inc(pT_copied, 1)
                act.wait_ge(mix_done, g + 1)
                nc.scalar.copy(mixT[0:D, g * GCOLS:(g + 1) * GCOLS], bank(6 + g % 2)[0:D, 0:GCOLS]).then_inc(mix_copied, 1)

        @block.gpsimd
        def _(pool):
            nc.gpsimd.memset(qT[D:P, :], 0.0).then_inc(mixT_set, 1)
            nc.gpsimd.memset(kT[D:P, :], 0.0).then_inc(mixT_set, 1)
            pool.wait_ge(mixT_set, 2)
            nc.gpsimd.memset(v[:], 0.0).then_inc(mixT_set, 1)
            nc.gpsimd.memset(probT[:], 0.0).then_inc(mixT_set, 1)
            pool.wait_ge(mixT_set, 4)
            nc.gpsimd.memset(mixT[0:D, T:TP], 0.0).then_inc(mixT_set, 1)
            pool.wait_ge(mixT_set, 5)
            nc.gpsimd.memset(mixT[D:D + 1, :], 1.0).then_inc(mixT_set, 1)

        @block.vector
        def _(dve):
            chain = Chain(dve, dve_done)
            wait_weights(dve, "attn0")
            dve.wait_ge(mixT_set, 6)
            for g in range(GROUPS):
                dve.wait_ge(v_done, g + 1)
                nc.vector.tensor_tensor(v[0:S, g * GROUP:(g + 1) * GROUP, :],
                                        bank(2 + g % 2)[0:S].rearrange("p (b f) -> p b f", f=D),
                                        W["a0bv"][:].rearrange("p (a f) -> p a f", a=1).broadcast_to([S, GROUP, D]),
                                        ALU.add).then_inc(v_copied, 1)
            chain.step(nc.vector.tensor_tensor(
                mask2[:], bank(4)[0:S, 0:2 * IMAGES].rearrange("p (b f) -> p b f", f=2),
                W["a0bm"][:].rearrange("p (a f) -> p a f", a=1).broadcast_to([S, IMAGES, 2]), ALU.add))
            chain.step(nc.vector.tensor_scalar(mask2[:], mask2[:], 0.0, None, ALU.not_equal))
            chain.step(nc.vector.tensor_tensor(mask[:], mask2[:, :, 0], mask2[:, :, 1], ALU.mult))
            for g in range(GROUPS):
                s3 = bank(g % 2)[0:S, 0:GCOLS].rearrange("p (b j) -> p b j", j=S)
                wide = lambda x: x[:, g % 2].rearrange("p (b a) -> p b a", a=1).broadcast_to([S, GROUP, S])
                dve.wait_ge(s_done, g + 1)
                if g >= 2:
                    dve.wait_ge(pT_done, g - 1)
                chain.step(nc.vector.tensor_reduce(high[:, g % 2], s3, AX.X, ALU.max))
                ins = nc.vector.tensor_tensor(prob[:, g % 2], s3, wide(high), ALU.subtract)
                ins.then_inc(exp_in, 1)
                dve.wait_ge(exp_in, g + 1)
                nc.vector.memset(total[:, g % 2], 0.0).then_inc(s_read, 1)
                dve.wait_ge(exp_done, g + 1)
                dve.wait_ge(s_read, g + 1)
                chain.step(nc.vector.tensor_reduce(total[:, g % 2], prob[:, g % 2], AX.X, ALU.add))
                chain.step(nc.vector.reciprocal(high[:, g % 2], total[:, g % 2]))
                chain.step(nc.vector.tensor_tensor(total[:, g % 2], high[:, g % 2], mask[:, g * GROUP:(g + 1) * GROUP], ALU.mult))
                nc.vector.tensor_tensor(prob[:, g % 2], prob[:, g % 2], wide(total), ALU.mult).then_inc(p_done, 1)

        ctx.close()
        norm("n0a_", z)

    def per(x, n):
        return x.rearrange("p (t a) -> p t a", a=1).broadcast_to([P, TILES, n])

    def first_largest(chain, chosen, scores, high, index, E):
        lanes = index[:, 0:E].rearrange("p (a e) -> p a e", a=1).broadcast_to([P, TILES, E])
        chain.step(nc.vector.tensor_reduce(high, scores, AX.X, ALU.max))
        chain.step(nc.vector.tensor_tensor(chosen, scores, per(high, E), ALU.is_equal))
        chain.step(nc.vector.scalar_tensor_tensor(chosen, chosen, -float(E), lanes, ALU.mult, ALU.add))
        first = spare_col[:]
        chain.step(nc.vector.tensor_reduce(first, chosen, AX.X, ALU.min))
        chain.step(nc.vector.tensor_tensor(chosen, chosen, per(first, E), ALU.is_equal))

    spare_col = sb("spare_col", [P, TILES])
    lane_index = sb("lane_index", [P, P])
    gates = sb("gates", [P, TILES, 8])

    def top_two(chain, name, ctx, scores, E, exp_wanted, exp_given):
        one, two = sb(name + "one", [P, TILES, E], F32, ctx), sb(name + "two", [P, TILES, E], F32, ctx)
        m1, m2 = sb(name + "m1", [P, TILES], F32, ctx), sb(name + "m2", [P, TILES], F32, ctx)
        first_largest(chain, one[:], scores, m1[:], lane_index, E)
        chain.step(nc.vector.scalar_tensor_tensor(scores, one[:], -1e30, scores, ALU.mult, ALU.add))
        first_largest(chain, two[:], scores, m2[:], lane_index, E)
        nc.vector.tensor_tensor(m2[:], m2[:], m1[:], ALU.subtract).then_inc(exp_wanted, 1)

        def finish():
            chain.engine.wait_ge(exp_given, 1)
            chain.step(nc.vector.tensor_scalar(m1[:], m2[:], 1.0, None, ALU.add))
            chain.step(nc.vector.reciprocal(m1[:], m1[:]))
            chain.step(nc.vector.tensor_tensor(m2[:], m2[:], m1[:], ALU.mult))
            chain.step(nc.vector.tensor_tensor(one[:], one[:], per(m1[:], E), ALU.mult))
            chain.step(nc.vector.tensor_tensor(two[:], two[:], per(m2[:], E), ALU.mult))
            return nc.vector.tensor_tensor(gates[:, :, 0:E], one[:], two[:], ALU.add)

        return m2, finish

    HEADS, FIELDS = 4, 20

    def graph_gates():
        ctx = ExitStack()
        local = lambda name, shape, dt=F32: sb(name, shape, dt, ctx)
        mark = lambda name: sem(name, ctx)
        nodes = local("nodes", [P, TILES, FIELDS])
        a_dst = local("a_dst", [P, TILES, HEADS])
        dst_parts = local("dst_parts", [P, 3, TILES * HEADS], BF16)
        rest = local("rest", [P, TILES * HEADS])
        work = local("work", [P, TILES, 16])
        high, high_all = local("high_src", [P, HEADS]), local("high_all", [P, HEADS])
        zeros = local("zeros", [P, 260])

        inner = ExitStack()
        mark1 = lambda name: sem(name, inner)
        h_done, nodes_ready, table_ready, high_ready, high_known, dve_done1 = (
            mark1(n) for n in ("h_done", "nodes_ready", "table_ready", "high_ready", "high_known", "dve_done1"))
        block = inner.enter_context(nc.Block())

        @block.tensor
        def _(pe):
            wait_weights(pe, "gat")
            for t in range(TILES):
                mm = nc.tensor.matmul(bank(0)[:, 16 * t:16 * t + 16], feat[:, t * P:(t + 1) * P], W["gat"][:],
                                      start=True, stop=True)
            mm.then_inc(h_done, 1)

        @block.vector
        def _(dve):
            chain = Chain(dve, dve_done1)
            wait_weights(dve, "gat")
            nc.vector.memset(zeros[:], 0.0)
            dve.wait_ge(h_done, 1)
            chain.step(nc.vector.tensor_copy(nodes[:, :, 0:16], bank(0)[:, 0:16 * TILES].rearrange("p (t f) -> p t f", f=16)))
            for w, dst in (("att_src", nodes[:, :, 16:20]), ("att_dst", a_dst[:])):
                att = W[w][:].rearrange("p (a f) -> p a f", a=1).broadcast_to([P, TILES, 16])
                chain.step(nc.vector.tensor_tensor(work[:], nodes[:, :, 0:16], att, ALU.mult))
                ins = nc.vector.tensor_reduce(dst, work[:].rearrange("p t (h k) -> p t h k", k=4), AX.X, ALU.add)
                chain.step(ins)
            nc.vector.tensor_reduce(high[:], nodes[:, :, 16:20].rearrange("p t h -> p h t"), AX.X,
                                    ALU.max).then_inc(nodes_ready, 1)
            flat = a_dst[:].rearrange("p t h -> p (t h)")
            chain.step(nc.vector.tensor_copy(dst_parts[:, 0], flat))
            chain.step(nc.vector.tensor_tensor(rest[:], flat, dst_parts[:, 0], ALU.subtract))
            chain.step(nc.vector.tensor_copy(dst_parts[:, 1], rest[:]))
            chain.step(nc.vector.tensor_tensor(rest[:], rest[:], dst_parts[:, 1], ALU.subtract))
            chain.step(nc.vector.tensor_copy(dst_parts[:, 2], rest[:]))

        @block.gpsimd
        def _(pool):
            nc.gpsimd.iota(lane_index[:], [[1, P]], base=0, channel_multiplier=0,
                           allow_small_or_imprecise_dtypes=True).then_inc(high_known, 1)
            pool.wait_ge(nodes_ready, 1)
            nc.gpsimd.partition_all_reduce(high_all[:], high[:], P, bass.bass_isa.ReduceOp.max).then_inc(high_known, 1)
            pool.wait_ge(high_known, 2)

        @block.sync
        def _(sp):
            sp.wait_ge(nodes_ready, 1)
            sp.dma_start(table.rearrange("(t p) f -> p t f", p=P), nodes[:]).then_inc(table_ready, 16)
            sp.wait_ge(table_ready, 16)

        inner.close()

        inner = ExitStack()
        local2 = lambda name, shape, dt=F32: sb(name, shape, dt, inner)
        mark2 = lambda name: sem(name, inner)
        ring = lambda name, n, shape, dt=F32: [local2("%s%d" % (name, q), shape, dt) for q in range(n)]
        idx = ring("idx", DEPTH, [P, SLOTS], U32)
        got = ring("got", DEPTH, [P, SLOTS, FIELDS])
        is_lo = ring("is_lo", DEPTH, [P, SLOTS, P])
        is_hi = ring("is_hi", DEPTH, [P, SLOTS, TILES])
        is_loT = ring("is_loT", 2, [P, SLOTS, P], BF16)
        message = ring("message", 2, [P, SLOTS, FIELDS])
        placed = ring("placed", 2, [P, SLOTS, TILES, FIELDS])
        picked = local2("picked", [P, SLOTS, HEADS, TILES])
        dst_term = local2("dst_term", [P, SLOTS, HEADS])
        logit = local2("logit", [P, 2, SLOTS, HEADS])
        gathered = [mark2("gathered") for q in range(DEPTH)]
        (idx_ready, got_free, hot_ready, turned, turned_copied, picks_done, picks_read, exp_wanted, exp_given,
         placed_ready, summed, pool_passed, dve_done2) = (mark2(n) for n in (
             "idx_ready", "got_free", "hot_ready", "turned", "turned_copied", "picks_done", "picks_read", "exp_wanted",
             "exp_given", "placed_ready", "summed", "pool_passed", "dve_done"))
        HALF = TILES // 2
        PICK_BANK = (2, 6)
        block = inner.enter_context(nc.Block())

        def n_trips(engine):
            return engine.value_load(trips[0:1, 0:1], min_val=1, max_val=MAX_TRIPS)


        @block.gpsimd
        def _(pool):
            n = n_trips(pool)
            with pool.Fori(0, n) as i:
                for q in range(DEPTH):
                    g1 = i * DEPTH + (q + 1)
                    pool.wait_ge(got_free, g1)
                    pool.sem_inc(pool_passed, 1)
                    nc.gpsimd.tensor_copy(idx[q][:], edge_src[:, ds(i * (DEPTH * SLOTS) + SLOTS * q, SLOTS)]).then_inc(idx_ready, 1)
                    pool.wait_ge(idx_ready, g1)
                    pool.sem_inc(pool_passed, 1)
                    for j in range(SLOTS):
                        nc.gpsimd.indirect_dma_start(
                            got[q][:, j, :], None, table,
                            bass.IndirectOffsetOnAxis(ap=idx[q][:, j:j + 1], axis=0)).then_inc(gathered[q], 16)

        @block.tensor
        def _(pe):
            for k in range(2):
                mm = nc.tensor.matmul(bank(4 + k)[:, 0:260], zeros[:, 0:P], zeros[:], start=True, stop=False)
            mm.then_inc(summed, DEPTH)

            def turn(q):
                for j in range(SLOTS):
                    mm = nc.tensor.transpose(bank(j // 4)[:, (j % 4) * P:(j % 4 + 1) * P], is_lo[q % DEPTH][:, j, :], ident[:])
                mm.then_inc(turned, 1)

            def pick(q):
                for j in range(SLOTS):
                    for part in range(3):
                        mm = nc.tensor.matmul(bank(PICK_BANK[q % 2] + j // 4)[:, (j % 4) * P:(j % 4) * P + TILES * HEADS],
                                              is_loT[q % 2][:, j, :], dst_parts[:, part, :], start=(part == 0), stop=(part == 2))
                mm.then_inc(picks_done, 1)

            for g in range(LEAD):
                pe.wait_ge(hot_ready, g + 1)
                if g:
                    pe.wait_ge(turned_copied, g)
                turn(g)
                pe.wait_ge(turned_copied, g + 1)
                pick(g)
            n = n_trips(pe)
            with pe.Fori(0, n) as i:
                for q in range(DEPTH):
                    g1 = i * DEPTH + (q + 1)
                    pe.wait_ge(hot_ready, g1 + LEAD)
                    pe.wait_ge(turned_copied, g1 + (LEAD - 1))
                    turn(q + LEAD)
                    pe.wait_ge(placed_ready, g1)
                    for j in range(SLOTS):
                        for k in range(2):
                            mm = nc.tensor.matmul(
                                bank(4 + k)[:, 0:260], is_lo[q][:, j, :],
                                placed[q % 2][:, j, k * HALF:(k + 1) * HALF, :].rearrange("p t f -> p (t f)"),
                                start=False, stop=False)
                    mm.then_inc(summed, 1)
                    pe.wait_ge(turned_copied, g1 + LEAD)
                    pe.wait_ge(picks_read, g1)
                    pick(q + LEAD)
            for k in range(2):
                nc.tensor.matmul(bank(4 + k)[:, 0:260], zeros[:, 0:P], zeros[:], start=False, stop=True)

        @block.scalar
        def _(act):
            def copy_turned(q):
                nc.scalar.copy(is_loT[q % 2][:].rearrange("p a b -> p (a b)"), bank(0, 2)).then_inc(turned_copied, 1)

            for g in range(LEAD):
                act.wait_ge(turned, g + 1)
                copy_turned(g)
            n = n_trips(act)
            with act.Fori(0, n) as i:
                for q in range(DEPTH):
                    g1 = i * DEPTH + (q + 1)
                    act.wait_ge(exp_wanted, g1)
                    nc.scalar.activation(message[q % 2][:, :, 16:20], logit[:, 0], ACT.Exp).then_inc(exp_given, 1)
                    act.wait_ge(turned, g1 + LEAD)
                    copy_turned(q + LEAD)

        @block.vector
        def _(dve):
            dve.sem_inc(got_free, DEPTH)
            STEPS = 4

            def masks(q, col):
                def slots(x, k):
                    return x[:, ds(col, SLOTS)].rearrange("p (t a) -> p t a", a=1).broadcast_to([P, SLOTS, k])

                lanes = lambda k: lane_index[:, 0:k].rearrange("p (a e) -> p a e", a=1).broadcast_to([P, SLOTS, k])
                nc.vector.tensor_tensor(is_lo[q % DEPTH][:], lanes(P), slots(edge_dlo, P), ALU.is_equal)
                nc.vector.tensor_tensor(is_hi[q % DEPTH][:], lanes(TILES), slots(edge_dhi, TILES), ALU.is_equal).then_inc(hot_ready, 1)

            for g in range(LEAD):
                masks(g, g * SLOTS)
            n = n_trips(dve)
            with dve.Fori(0, n) as i:
                for q in range(DEPTH):
                    g1 = i * DEPTH + (q + 1)

                    def step(ins, k):
                        ins.then_inc(dve_done2, 1)
                        dve.wait_ge(dve_done2, i * (DEPTH * STEPS) + (q * STEPS + k))

                    dve.wait_ge(picks_done, g1)
                    dve.wait_ge(hot_ready, g1)
                    picks = bank(PICK_BANK[q % 2], 2).rearrange("p (j c) -> p j c", c=P)[:, :, 0:TILES * HEADS].rearrange(
                        "p j (t h) -> p j h t", h=HEADS)
                    hi = is_hi[q][:].rearrange("p j (a t) -> p j a t", a=1).broadcast_to([P, SLOTS, HEADS, TILES])
                    nc.vector.tensor_tensor(picked[:], picks, hi, ALU.mult).then_inc(picks_read, 1)
                    dve.wait_ge(picks_read, g1)
                    step(nc.vector.tensor_reduce(dst_term[:], picked[:], AX.X, ALU.add), 1)
                    dve.wait_ge(gathered[q], i * 128 + 128)
                    nc.vector.tensor_tensor(logit[:, 0], got[q][:, :, 16:20], dst_term[:], ALU.add)
                    step(nc.vector.tensor_tensor(
                        logit[:, 1], dst_term[:],
                        high_all[:].rearrange("p (a h) -> p a h", a=1).broadcast_to([P, SLOTS, HEADS]), ALU.add), 2)
                    step(nc.vector.scalar_tensor_tensor(logit[:], logit[:], 0.2, logit[:], ALU.mult, ALU.max), 3)
                    nc.vector.tensor_tensor(logit[:, 0], logit[:, 0], logit[:, 1], ALU.subtract).then_inc(exp_wanted, 1)
                    dve.wait_ge(summed, g1 + 2)
                    masks(q + LEAD, i * (DEPTH * SLOTS) + SLOTS * (q + LEAD))
                    dve.wait_ge(exp_given, g1)
                    weight4 = message[q % 2][:, :, 16:20].rearrange("p j (h a) -> p j h a", a=1).broadcast_to([P, SLOTS, HEADS, 4])
                    step(nc.vector.tensor_tensor(
                        message[q % 2][:, :, 0:16].rearrange("p j (h k) -> p j h k", k=4),
                        got[q][:, :, 0:16].rearrange("p j (h k) -> p j h k", k=4), weight4, ALU.mult), 4)
                    dve.sem_inc(got_free, 1)
                    nc.vector.tensor_tensor(
                        placed[q % 2][:],
                        is_hi[q][:].rearrange("p j (t a) -> p j t a", a=1).broadcast_to([P, SLOTS, TILES, FIELDS]),
                        message[q % 2][:].rearrange("p j (a f) -> p j a f", a=1).broadcast_to([P, SLOTS, TILES, FIELDS]),
                        ALU.mult).then_inc(placed_ready, 1)

        inner.close()

        inner = ExitStack()
        local3 = lambda name, shape, dt=F32: sb(name, shape, dt, inner)
        mark3 = lambda name: sem(name, inner)
        sums = local3("sums", [P, TILES, FIELDS])
        own = local3("own", [P, 2, TILES, HEADS])
        mixed = local3("mixed", [P, TILES, 16])
        mean, var, eps = local3("mean", [P, TILES]), local3("var", [P, TILES]), local3("eps", [P, 1])
        scores = local3("scores", [P, TILES, HEADS])
        dve_done3, own_wanted, own_given, std_wanted, std_given, pair_wanted, pair_given = (mark3(n) for n in (
            "dve_done3", "own_wanted", "own_given", "std_wanted", "std_given", "pair_wanted", "pair_given"))
        block = inner.enter_context(nc.Block())
        shared = {}

        @block.vector
        def _(dve):
            chain = Chain(dve, dve_done3)
            nc.vector.memset(eps[:], LN_EPS)
            high4 = high_all[:].rearrange("p (a h) -> p a h", a=1).broadcast_to([P, TILES, HEADS])
            nc.vector.tensor_tensor(own[:, 0], nodes[:, :, 16:20], a_dst[:], ALU.add)
            chain.step(nc.vector.tensor_tensor(own[:, 1], a_dst[:], high4, ALU.add))
            chain.step(nc.vector.scalar_tensor_tensor(own[:], own[:], 0.2, own[:], ALU.mult, ALU.max))
            nc.vector.tensor_tensor(own[:, 0], own[:, 0], own[:, 1], ALU.subtract).then_inc(own_wanted, 1)
            dve.wait_ge(own_given, 1)
            grouped = lambda x: x.rearrange("p t (h k) -> p t h k", k=4)
            each4 = lambda x: x.rearrange("p t (h a) -> p t h a", a=1).broadcast_to([P, TILES, HEADS, 4])
            chain.step(nc.vector.tensor_tensor(grouped(sums[:, :, 0:16]), grouped(nodes[:, :, 0:16]), each4(own[:, 0]), ALU.mult))
            chain.step(nc.vector.tensor_copy(sums[:, :, 16:20], own[:, 0]))
            for k in range(2):
                part = sums[:, k * HALF:(k + 1) * HALF, :]
                chain.step(nc.vector.tensor_tensor(part, part, bank(4 + k)[:, 0:260].rearrange("p (t f) -> p t f", f=FIELDS), ALU.add))
            chain.step(nc.vector.tensor_scalar(own[:, 0], sums[:, :, 16:20], 1e-16, None, ALU.add))
            chain.step(nc.vector.reciprocal(own[:, 0], own[:, 0]))
            chain.step(nc.vector.tensor_tensor(grouped(mixed[:]), grouped(sums[:, :, 0:16]), each4(own[:, 0]), ALU.mult))
            each = lambda w: W[w][:].rearrange("p (a f) -> p a f", a=1).broadcast_to([P, TILES, 16])
            chain.step(nc.vector.tensor_tensor(mixed[:], mixed[:], each("b_gat"), ALU.add))
            chain.step(nc.vector.tensor_reduce(mean[:], mixed[:], AX.X, ALU.add))
            chain.step(nc.vector.tensor_scalar(mean[:], mean[:], 1.0 / 16, None, ALU.mult))
            chain.step(nc.vector.tensor_tensor(mixed[:], mixed[:], per(mean[:], 16), ALU.subtract))
            chain.step(nc.vector.tensor_tensor(work[:], mixed[:], mixed[:], ALU.mult))
            nc.vector.tensor_reduce(var[:], work[:], AX.X, ALU.add).then_inc(std_wanted, 1)
            dve.wait_ge(std_given, 1)
            chain.step(nc.vector.reciprocal(var[:], var[:]))
            chain.step(nc.vector.tensor_tensor(mixed[:], mixed[:], per(var[:], 16), ALU.mult))
            chain.step(nc.vector.tensor_tensor(mixed[:], mixed[:], each("ln_gamma"), ALU.mult))
            chain.step(nc.vector.tensor_tensor(mixed[:], mixed[:], each("ln_beta"), ALU.add))
            chain.step(nc.vector.tensor_reduce(scores[:], mixed[:].rearrange("p t (h k) -> p t k h", k=4), AX.X, ALU.add))
            chain.step(nc.vector.tensor_scalar(scores[:], scores[:], 1.0 / HEADS, None, ALU.mult))
            gap, finish = top_two(chain, "g0", inner, scores[:], 4, pair_wanted, pair_given)
            shared["gap"] = gap
            chain.step(finish())

        @block.scalar
        def _(act):
            act.wait_ge(own_wanted, 1)
            nc.scalar.activation(own[:, 0], own[:, 0], ACT.Exp).then_inc(own_given, 1)
            act.wait_ge(std_wanted, 1)
            nc.scalar.activation(var[:], var[:], ACT.Sqrt, bias=eps[:, 0:1], scale=1.0 / 16).then_inc(std_given, 1)
            act.wait_ge(pair_wanted, 1)
            nc.scalar.activation(shared["gap"][:], shared["gap"][:], ACT.Exp).then_inc(pair_given, 1)

        inner.close()
        ctx.close()

    def experts(name, part, E, HC, w1, b1, w2, b2, z):
        ctx = ExitStack()
        mark = lambda n: sem(name + n, ctx)
        hidden = sb(name + "hidden", [P, 2, E * HC, BANK], F32, ctx)
        weighed = sb(name + "weighed", [P, 2, E, D], F32, ctx)
        h_done, gelu_done, y_done, y_read, z_part, dve_done = (
            mark(n) for n in ("h_done", "gelu_done", "y_done", "y_read", "z_part", "dve_done"))
        block = ctx.enter_context(nc.Block())
        M = E * HC

        @block.tensor
        def _(pe):
            wait_weights(pe, part)
            done_tiles = 0

            def up(c):
                start, n = CHUNKS[c]
                for m in range(M):
                    k = c * M + m
                    if k >= 4:
                        pe.wait_ge(gelu_done, k - 3)
                    nc.tensor.matmul(bank(k % 4)[:, 0:n], w1[:, m, :], feat[:, start:start + n],
                                     start=True, stop=True).then_inc(h_done, 1)

            def down(c):
                start, n = CHUNKS[c]
                pe.wait_ge(gelu_done, (c + 1) * M)
                for j in range(n // P):
                    t = start // P + j
                    if t >= 2:
                        pe.wait_ge(y_read, t - 1)
                    y = bank(4 + t % 2)
                    nc.tensor.matmul(y[:, 0:E * D], feat[:, t * P:(t + 1) * P], b2, start=True, stop=False)
                    for e in range(E):
                        for h in range(HC):
                            mm = nc.tensor.matmul(y[:, e * D:(e + 1) * D], hidden[:, c % 2, e * HC + h, j * P:(j + 1) * P],
                                                  w2[:, e * HC + h, :], start=False, stop=(e == E - 1 and h == HC - 1))
                    mm.then_inc(y_done, 1)

            up(0)
            for c in range(1, len(CHUNKS)):
                up(c)
                down(c - 1)
            down(len(CHUNKS) - 1)

        @block.scalar
        def _(act):
            wait_weights(act, part)
            for c, (start, n) in enumerate(CHUNKS):
                if c >= 2:
                    act.wait_ge(y_done, CHUNKS[c - 1][0] // P)
                for m in range(M):
                    k = c * M + m
                    act.wait_ge(h_done, k + 1)
                    nc.scalar.activation(hidden[:, c % 2, m, 0:n], bank(k % 4)[:, 0:n], ACT.Gelu,
                                         bias=b1[:, m:m + 1]).then_inc(gelu_done, 1)

        @block.vector
        def _(dve):
            chain = Chain(dve, dve_done)
            for t in range(TILES):
                dve.wait_ge(y_done, t + 1)
                g = gates[:, t, 0:E].rearrange("p (e a) -> p e a", a=1).broadcast_to([P, E, D])
                nc.vector.tensor_tensor(weighed[:, t % 2], bank(4 + t % 2)[:, 0:E * D].rearrange("p (e f) -> p e f", f=D),
                                        g, ALU.mult).then_inc(y_read, 1)
                dve.wait_ge(y_read, t + 1)
                nc.vector.tensor_reduce(z[:, t], weighed[:, t % 2].rearrange("p e f -> p f e"), AX.X,
                                        ALU.add).then_inc(z_part, 1)
            dve.wait_ge(z_part, TILES)
            chain.step(nc.vector.tensor_tensor(z[:], z[:], tok[:], ALU.add))

        ctx.close()

    def experts0():
        ctx = ExitStack()
        z = sb("z0", [P, TILES, D], F32, ctx)
        experts("e0_", "ffn0", 4, 1, W["f0w1"], W["f0b1"], W["f0w2"], W["f0b2"], z)
        norm("n0f_", z[:].rearrange("p t f -> p (t f)"))
        ctx.close()

    def recurrent1():
        ctx = ExitStack()
        local = lambda name, shape, dt=F32: sb(name, shape, dt, ctx)
        mark = lambda name: sem(name, ctx)
        TWO_PI = 6.283185307179586
        step_no = local("step_no", [P, S])
        angle = local("angle", [P, 2, S])
        turns_i, turns = local("turns_i", [P, 2, S], I32), local("turns", [P, 2, S])
        over = local("over", [P, 2, S])
        wave = local("wave", [P, 2, S])
        wave_in = local("wave_in", [P, 2, S])
        decay = local("decay", [P, 1])
        gamma = local("gamma", [P, 1])
        decays = local("decays", [P, GROUP, S])
        c_minus = local("c_minus", [P, D])
        keep = local("keep", [P, D])
        u4 = local("u4", [P, 4, GROUP, S])
        drive = local("drive", [P, 2, GROUP, S])
        state = local("state", [P, 2, GROUP, S])
        x_re, x_im = local("x_re", [P, TP]), local("x_im", [P, TP])
        (bu_done, bu_read, dve_done, pool_done, exps, sines, angles_ready, x_set, z_done, x_done) = (mark(n) for n in (
            "bu_done", "bu_read", "dve_done", "pool_done", "exps", "sines", "angles_ready", "x_set", "z_done", "x_done"))
        z = psum[:, 4 * BANK:4 * BANK + TILES * D]
        block = ctx.enter_context(nc.Block())

        @block.gpsimd
        def _(pool):
            nc.gpsimd.iota(step_no[:], [[1, S]], base=0, channel_multiplier=0,
                           allow_small_or_imprecise_dtypes=True).then_inc(pool_done, 1)
            nc.gpsimd.memset(x_re[:, T:TP], 0.0).then_inc(x_set, 1)
            nc.gpsimd.memset(x_im[:, T:TP], 0.0).then_inc(x_set, 1)

        @block.tensor
        def _(pe):
            wait_weights(pe, "attn1")
            for g in range(GROUPS):
                if g >= 2:
                    pe.wait_ge(bu_read, g - 1)
                for k, w in enumerate(("B_re", "B_im")):
                    mm = nc.tensor.matmul(bank(2 * (g % 2) + k)[:, 0:GCOLS], W[w][:], feat[:, g * GCOLS:(g + 1) * GCOLS],
                                          start=True, stop=True)
                mm.then_inc(bu_done, 1)
            pe.wait_ge(x_done, GROUPS)
            pe.wait_ge(x_set, 2)
            for t in range(TILES):
                cols = slice(t * P, (t + 1) * P)
                nc.tensor.matmul(z[:, t * D:(t + 1) * D], x_re[:, cols], W["C_re"][:], start=True, stop=False)
                nc.tensor.matmul(z[:, t * D:(t + 1) * D], x_im[:, cols], c_minus[:], start=False, stop=False)
                mm = nc.tensor.matmul(z[:, t * D:(t + 1) * D], feat[:, cols], keep[:], start=False, stop=True)
            mm.then_inc(z_done, 1)

        @block.scalar
        def _(act):
            wait_weights(act, "attn1")
            nc.scalar.activation(decay[:], W["nu"][:], ACT.Exp).then_inc(exps, 1)
            nc.scalar.activation(gamma[:], W["gamma_log"][:], ACT.Exp).then_inc(exps, 1)
            act.wait_ge(exps, 2)
            nc.scalar.activation(decay[:], decay[:], ACT.Exp, scale=-1.0).then_inc(exps, 1)
            act.wait_ge(angles_ready, 1)
            nc.scalar.activation(wave[:], angle[:], ACT.Sin).then_inc(sines, 1)

        @block.vector
        def _(dve):
            chain = Chain(dve, dve_done)
            wait_weights(dve, "attn1")
            dve.wait_ge(pool_done, 1)
            chain.step(nc.vector.tensor_scalar(angle[:, 1], step_no[:], W["theta"][:, 0:1], None, ALU.mult))
            chain.step(nc.vector.tensor_scalar(angle[:, 0], angle[:, 1], TWO_PI / 4, None, ALU.add))
            chain.step(nc.vector.tensor_scalar(turns_i[:], angle[:], 1.0 / TWO_PI, None, ALU.mult))
            chain.step(nc.vector.tensor_copy(turns[:], turns_i[:]))
            for piece in (6.28125, TWO_PI - 6.28125):
                chain.step(nc.vector.scalar_tensor_tensor(angle[:], turns[:], -piece, angle[:], ALU.mult, ALU.add))
            for compare, sign in ((ALU.is_gt, 1.0), (ALU.is_lt, -1.0)):
                chain.step(nc.vector.tensor_scalar(over[:], angle[:], sign * TWO_PI / 2, -sign * TWO_PI, compare, ALU.mult))
                chain.step(nc.vector.tensor_tensor(angle[:], angle[:], over[:], ALU.add))
            nc.vector.tensor_scalar(angle[:], angle[:], 3.1415925, -3.1415925, ALU.min, ALU.max).then_inc(angles_ready, 1)
            nc.vector.tensor_scalar(c_minus[:], W["C_im"][:], -1.0, None, ALU.mult)
            chain.step(nc.vector.tensor_scalar(keep[0:D], ident[0:D, 0:D], W["D"][:, 0:1], None, ALU.mult))
            chain.step(nc.vector.tensor_tensor(keep[0:D], keep[0:D], ident[0:D, 0:D], ALU.add))
            dve.wait_ge(exps, 3)
            nc.vector.memset(decays[:], 0.0)
            chain.step(nc.vector.memset(keep[D:P], 0.0))
            chain.step(nc.vector.tensor_scalar(decays[:, :, 1:S], decays[:, :, 1:S], decay[:, 0:1], None, ALU.add))
            dve.wait_ge(sines, 1)
            chain.step(nc.vector.tensor_scalar(wave_in[:], wave[:], gamma[:, 0:1], None, ALU.mult))

            def over_group(x, k):
                return x[:, k].rearrange("p (a s) -> p a s", a=1).broadcast_to([P, GROUP, S])

            for g in range(GROUPS):
                dve.wait_ge(bu_done, g + 1)
                re, im = (bank(2 * (g % 2) + k)[:, 0:GCOLS].rearrange("p (b s) -> p b s", s=S) for k in range(2))
                nc.vector.tensor_tensor(u4[:, 0], re, over_group(wave_in, 0), ALU.mult)
                nc.vector.tensor_tensor(u4[:, 1], im, over_group(wave_in, 1), ALU.mult)
                nc.vector.tensor_tensor(u4[:, 2], im, over_group(wave_in, 0), ALU.mult)
                ins = nc.vector.tensor_tensor(u4[:, 3], re, over_group(wave_in, 1), ALU.mult)
                ins.then_inc(bu_read, 1)
                dve.wait_ge(bu_read, g + 1)
                nc.vector.tensor_tensor(drive[:, 0], u4[:, 0], u4[:, 1], ALU.add)
                chain.step(nc.vector.tensor_tensor(drive[:, 1], u4[:, 2], u4[:, 3], ALU.subtract))
                flat = lambda x: x.rearrange("p b s -> p (b s)")
                nc.vector.tensor_tensor_scan(flat(state[:, 0]), flat(decays[:]), flat(drive[:, 0]), 0.0, ALU.mult, ALU.add)
                chain.step(nc.vector.tensor_tensor_scan(flat(state[:, 1]), flat(decays[:]), flat(drive[:, 1]), 0.0, ALU.mult, ALU.add))
                nc.vector.tensor_tensor(u4[:, 0], state[:, 0], over_group(wave, 0), ALU.mult)
                nc.vector.tensor_tensor(u4[:, 1], state[:, 1], over_group(wave, 1), ALU.mult)
                nc.vector.tensor_tensor(u4[:, 2], state[:, 1], over_group(wave, 0), ALU.mult)
                chain.step(nc.vector.tensor_tensor(u4[:, 3], state[:, 0], over_group(wave, 1), ALU.mult))
                cols = slice(g * GCOLS, (g + 1) * GCOLS)
                nc.vector.tensor_tensor(x_re[:, cols], flat(u4[:, 0]), flat(u4[:, 1]), ALU.subtract)
                nc.vector.tensor_tensor(x_im[:, cols], flat(u4[:, 2]), flat(u4[:, 3]), ALU.add).then_inc(x_done, 1)
                dve.wait_ge(x_done, g + 1)

        ctx.close()
        norm("n1a_", z)

    def single_expert1():
        ctx = ExitStack()
        local = lambda name, shape, dt=F32: sb(name, shape, dt, ctx)
        mark = lambda name: sem(name, ctx)
        E = 8
        z = local("z1", [P, TILES, D])
        inner = ExitStack()
        local1 = lambda name, shape, dt=F32: sb(name, shape, dt, inner)
        mark1 = lambda name: sem(name, inner)
        hidden = local1("hidden1", [P, 2, TP])
        score = local1("score1", [P, TILES, E])
        high, total = local1("high1", [P, TILES]), local1("total1", [P, TILES])
        weighed = local1("weighed1", [P, 2, E, D])
        (h_done, gelu_done, g_done, exp_wanted, exp_given, y_done, y_read, z_part, dve_done) = (mark1(n) for n in (
            "h_done", "gelu_done", "g_done", "exp_wanted", "exp_given", "y_done", "y_read", "z_part", "dve_done"))
        block = inner.enter_context(nc.Block())

        @block.tensor
        def _(pe):
            wait_weights(pe, "ffn1")
            k = 0
            for start, n in CHUNKS:
                for c in range(2):
                    if k >= 4:
                        pe.wait_ge(gelu_done, k - 3)
                    nc.tensor.matmul(bank(k % 4)[:, 0:n], W["f1w1"][:, c * P:(c + 1) * P], feat[:, start:start + n],
                                     start=True, stop=True).then_inc(h_done, 1)
                    k += 1
            pe.wait_ge(gelu_done, k)
            for t in range(TILES):
                cols = slice(t * P, (t + 1) * P)
                g = bank(6)[:, t * E:(t + 1) * E]
                nc.tensor.matmul(g, hidden[:, 0, cols], W["f1wg"][:, 0], start=True, stop=False)
                nc.tensor.matmul(g, hidden[:, 1, cols], W["f1wg"][:, 1], start=False, stop=False)
                mm = nc.tensor.matmul(g, feat[:, cols], W["f1bg"], start=False, stop=True)
            mm.then_inc(g_done, 1)
            for t in range(TILES):
                cols = slice(t * P, (t + 1) * P)
                if t >= 2:
                    pe.wait_ge(y_read, t - 1)
                y = bank(4 + t % 2)
                for c in range(2):
                    nc.tensor.matmul(y, hidden[:, c, cols], W["f1wd"][:, c].rearrange("p e d -> p (e d)"),
                                     start=(c == 0), stop=False)
                nc.tensor.matmul(y, feat[:, cols], W["f1bd"], start=False, stop=True).then_inc(y_done, 1)

        @block.scalar
        def _(act):
            wait_weights(act, "ffn1")
            k = 0
            for start, n in CHUNKS:
                for c in range(2):
                    act.wait_ge(h_done, k + 1)
                    nc.scalar.activation(hidden[:, c, start:start + n], bank(k % 4)[:, 0:n], ACT.Gelu,
                                         bias=W["f1b1"][:, c:c + 1]).then_inc(gelu_done, 1)
                    k += 1
            act.wait_ge(exp_wanted, 1)
            nc.scalar.activation(score[:], score[:], ACT.Exp).then_inc(exp_given, 1)

        @block.vector
        def _(dve):
            chain = Chain(dve, dve_done)
            dve.wait_ge(g_done, 1)
            logits = bank(6)[:, 0:TILES * E].rearrange("p (t e) -> p t e", e=E)
            chain.step(nc.vector.tensor_reduce(high[:], logits, AX.X, ALU.max))
            nc.vector.tensor_tensor(score[:], logits, per(high[:], E), ALU.subtract).then_inc(exp_wanted, 1)
            dve.wait_ge(exp_given, 1)
            chain.step(nc.vector.tensor_reduce(total[:], score[:], AX.X, ALU.add))
            chain.step(nc.vector.reciprocal(total[:], total[:]))
            chain.step(nc.vector.tensor_tensor(score[:], score[:], per(total[:], E), ALU.mult))
            first_largest(chain, gates[:], score[:], high[:], lane_index, E)
            chain.step(nc.vector.tensor_tensor(gates[:], gates[:], score[:], ALU.mult))
            for t in range(TILES):
                dve.wait_ge(y_done, t + 1)
                g = gates[:, t].rearrange("p (e a) -> p e a", a=1).broadcast_to([P, E, D])
                nc.vector.tensor_tensor(weighed[:, t % 2], bank(4 + t % 2).rearrange("p (e f) -> p e f", f=D), g,
                                        ALU.mult).then_inc(y_read, 1)
                dve.wait_ge(y_read, t + 1)
                nc.vector.tensor_reduce(z[:, t], weighed[:, t % 2].rearrange("p e f -> p f e"), AX.X,
                                        ALU.add).then_inc(z_part, 1)
            dve.wait_ge(z_part, TILES)
            chain.step(nc.vector.tensor_tensor(z[:], z[:], tok[:], ALU.add))

        inner.close()
        norm("n1f_", z[:].rearrange("p t f -> p (t f)"))
        ctx.close()

    def regrouped2():
        ctx = ExitStack()
        local = lambda name, shape, dt=F32: sb(name, shape, dt, ctx)
        mark = lambda name: sem(name, ctx)
        H, HD, R = 8, 8, IMAGES
        ROWS = S * H
        QUARTER = ROWS // 4
        qkv_all = local("qkv", [P, 3, S * D])
        qkv = qkv_all[0:R]
        q_high = local("q_high", [R, ROWS])
        q_turn = local("q_turn", [QUARTER, 4, R])
        q_top, q_wide = local("q_top", [QUARTER, 4]), local("q_wide", [QUARTER, 4, R])
        q_sum = local("q_sum", [R, ROWS])
        q_scale = local("q_scale", [S, H])
        k_high, k_sum = local("k_high", [R, H, HD]), local("k_sum", [R, H, HD])
        weights = local("weights", [S, H, S])
        v_turn = local("v_turn", [S, H, HD * R])
        mixed = local("mixed2", [S, D, R])
        mixT = local("mixT2", [P, TP])
        (p_done, p_read, dve_done, qh_done, qt_done, qw_done, qb_done, q_wanted, k_wanted, q_given, k_given, k_ready, qs_ready,
         qs_done, w_done, w_read, v_done, v_copied, o_done, o_read, t_done, t_copied, pad_set, z_done) = (mark(n) for n in (
             "p_done", "p_read", "dve_done", "qh_done", "qt_done", "qw_done", "qb_done", "q_wanted", "k_wanted", "q_given", "k_given",
             "k_ready", "qs_ready", "qs_done", "w_done", "w_read", "v_done", "v_copied", "o_done", "o_read", "t_done", "t_copied",
             "pad_set", "z_done"))
        z = psum[:, 0:TILES * D]
        PAIRS = (S + 1) // 2
        q3 = qkv[:, 0].rearrange("r (x d) -> r x d", d=HD)
        k4 = qkv[:, 1].rearrange("r (h n d) -> r h n d", h=H, d=HD)
        head = lambda i, h, rows=R: qkv_all[0:rows, i].rearrange("r (h n d) -> r h n d", h=H, d=HD)[:, h]
        block = ctx.enter_context(nc.Block())

        @block.gpsimd
        def _(pool):
            nc.gpsimd.memset(qkv_all[R:P, 0:2], 0.0).then_inc(pad_set, 1)
            nc.gpsimd.memset(mixT[D:P, :], 0.0).then_inc(pad_set, 1)
            pool.wait_ge(pad_set, 2)
            nc.gpsimd.memset(mixT[0:D, T:TP], 0.0).then_inc(pad_set, 1)

        @block.tensor
        def _(pe):
            wait_weights(pe, "attn2")
            w = W["a2"].rearrange("p i d -> p (i d)")
            for pair in range(PAIRS):
                if pair >= 4:
                    pe.wait_ge(p_read, pair - 3)
                for j in range(min(2, S - 2 * pair)):
                    mm = nc.tensor.matmul(bank(pair % 4)[0:R, j * 192:(j + 1) * 192],
                                          feat[:, 2 * pair + j:T:S], w, start=True, stop=True)
                mm.then_inc(p_done, 1)
            pe.wait_ge(qh_done, 1)
            for c in range(4):
                mm = nc.tensor.transpose(bank(4)[0:QUARTER, c * R:(c + 1) * R], q_high[:, c * QUARTER:(c + 1) * QUARTER],
                                         ident[0:R, 0:R])
            mm.then_inc(qt_done, 1)
            pe.wait_ge(qw_done, 1)
            for c in range(4):
                mm = nc.tensor.transpose(bank(5)[0:R, c * QUARTER:(c + 1) * QUARTER], q_wide[:, c, :],
                                         ident[0:QUARTER, 0:QUARTER])
            mm.then_inc(qb_done, 1)
            pe.wait_ge(p_read, PAIRS)
            for h in range(H):
                if h >= 2:
                    pe.wait_ge(v_copied, h - 1)
                for d in range(HD):
                    mm = nc.tensor.transpose(bank(6 + h % 2)[0:S, d * R:(d + 1) * R], head(2, h)[:, :, d], ident[0:R, 0:R])
                mm.then_inc(v_done, 1)
            pe.wait_ge(q_given, 1)
            pe.wait_ge(k_ready, 1)
            pe.wait_ge(pad_set, 3)
            for h in range(H):
                for d in range(HD):
                    mm = nc.tensor.matmul(bank(0)[0:S, h * S:(h + 1) * S], head(1, h, P)[:, :, d], head(0, h, P)[:, :, d],
                                          start=(d == 0), stop=(d == HD - 1))
            mm.then_inc(w_done, 1)
            pe.wait_ge(qs_ready, 1)
            for h in range(H):
                mm = nc.tensor.matmul(bank(1)[0:S, h:h + 1], q_sum[:, h * S:(h + 1) * S], ones_col[0:R, 0:1],
                                      start=True, stop=True)
            mm.then_inc(qs_done, 1)
            pe.wait_ge(w_read, 1)
            for h in range(H):
                pe.wait_ge(v_copied, h + 1)
                if h >= 2:
                    pe.wait_ge(o_read, h - 1)
                nc.tensor.matmul(bank(2 + h % 2)[0:S, :], weights[:, h, :], v_turn[:, h, :],
                                 start=True, stop=True).then_inc(o_done, 1)
            pe.wait_ge(o_read, H)
            for g in range(GROUPS):
                if g >= 2:
                    pe.wait_ge(t_copied, g - 1)
                for j in range(GROUP):
                    mm = nc.tensor.transpose(bank(4 + g % 2)[0:D, j * S:(j + 1) * S], mixed[:, :, g * GROUP + j],
                                             ident[0:S, 0:S])
                mm.then_inc(t_done, 1)
            pe.wait_ge(t_copied, GROUPS)
            close_block(pe, z, lambda t: [(mixT[:, t * P:(t + 1) * P], ident[:, 0:D])]).then_inc(z_done, 1)

        @block.scalar
        def _(act):
            act.wait_ge(q_wanted, 1)
            nc.scalar.activation(qkv[:, 0], qkv[:, 0], ACT.Exp).then_inc(q_given, 1)
            act.wait_ge(k_wanted, 1)
            nc.scalar.activation(qkv[:, 1], qkv[:, 1], ACT.Exp).then_inc(k_given, 1)
            for h in range(H):
                act.wait_ge(v_done, h + 1)
                nc.scalar.copy(v_turn[:, h, :], bank(6 + h % 2)[0:S, :]).then_inc(v_copied, 1)
            act.wait_ge(w_done, 1)
            nc.scalar.mul(weights[:].rearrange("p h s -> p (h s)"), bank(0)[0:S, 0:H * S],
                          float(R * HD) ** 0.5).then_inc(w_read, 1)
            for g in range(GROUPS):
                act.wait_ge(t_done, g + 1)
                nc.scalar.copy(mixT[0:D, g * GCOLS:(g + 1) * GCOLS], bank(4 + g % 2)[0:D, 0:GCOLS]).then_inc(t_copied, 1)

        @block.vector
        def _(dve):
            chain = Chain(dve, dve_done)
            wait_weights(dve, "attn2")
            for pair in range(PAIRS):
                n = min(2, S - 2 * pair)
                dve.wait_ge(p_done, pair + 1)
                for j in range(n):
                    c = 2 * pair + j
                    ins = nc.vector.tensor_tensor(
                        qkv[:, :, c * D:(c + 1) * D], bank(pair % 4)[0:R, j * 192:(j + 1) * 192].rearrange("p (i d) -> p i d", i=3),
                        W["a2b"][:], ALU.add)
                ins.then_inc(p_read, 1)
            dve.wait_ge(p_read, PAIRS)
            nc.vector.tensor_reduce(q_high[:], q3, AX.X, ALU.max).then_inc(qh_done, 1)
            chain.step(nc.vector.tensor_reduce(k_high[:], k4.rearrange("r h n d -> r h d n"), AX.X, ALU.max))
            over_rows = lambda x: x[:].rearrange("r h (a d) -> r h a d", a=1).broadcast_to([R, H, S, HD])
            nc.vector.tensor_tensor(k4, k4, over_rows(k_high), ALU.subtract).then_inc(k_wanted, 1)
            dve.wait_ge(qt_done, 1)
            chain.step(nc.vector.tensor_reduce(q_top[:], bank(4)[0:QUARTER, 0:4 * R].rearrange("p (c r) -> p c r", r=R), AX.X, ALU.max))
            nc.vector.tensor_copy(q_wide[:], q_top[:].rearrange("p (c a) -> p c a", a=1).broadcast_to([QUARTER, 4, R])).then_inc(qw_done, 1)
            dve.wait_ge(qb_done, 1)
            chain.step(nc.vector.tensor_copy(q_sum[:], bank(5)[0:R, 0:ROWS]))
            wide = q_sum[:].rearrange("r (x a) -> r x a", a=1).broadcast_to([R, ROWS, HD])
            nc.vector.tensor_tensor(q3, q3, wide, ALU.subtract).then_inc(q_wanted, 1)
            dve.wait_ge(k_given, 1)
            chain.step(nc.vector.tensor_reduce(k_sum[:], k4.rearrange("r h n d -> r h d n"), AX.X, ALU.add))
            chain.step(nc.vector.reciprocal(k_sum[:], k_sum[:]))
            nc.vector.tensor_tensor(k4, k4, over_rows(k_sum), ALU.mult).then_inc(k_ready, 1)
            dve.wait_ge(q_given, 1)
            nc.vector.tensor_reduce(q_sum[:], q3, AX.X, ALU.add).then_inc(qs_ready, 1)
            dve.wait_ge(qs_done, 1)
            chain.step(nc.vector.reciprocal(q_scale[:], bank(1)[0:S, 0:H]))
            for h in range(H):
                dve.wait_ge(o_done, h + 1)
                nc.vector.tensor_scalar(mixed[:, h * HD:(h + 1) * HD, :].rearrange("p d r -> p (d r)"), bank(2 + h % 2)[0:S, :],
                                        q_scale[:, h:h + 1], None, ALU.mult).then_inc(o_read, 1)

        ctx.close()
        norm("n2a_", z)

    def routed2():
        ctx = ExitStack()
        local = lambda name, shape, dt=F32: sb(name, shape, dt, ctx)
        mark = lambda name: sem(name, ctx)
        h0, h2 = local("h0", [P, TP]), local("h2", [P, TP])
        h1 = [local("h1_%d" % q, [P, S]) for q in range(2)]
        mine = [[local("mine%d%d" % (q, l), [P, P + 1]) for l in range(2)] for q in range(2)]
        (in_done, in_read, dve_done, ready, staged, one_done, one_read, two_done, two_read, pad_set, z_done,
         passed, dve_passed) = (mark(n) for n in (
             "in_done", "in_read", "dve_done", "ready", "staged", "one_done", "one_read", "two_done", "two_read", "pad_set",
             "z_done", "passed", "dve_passed"))
        z = psum[:, 0:TILES * D]
        ww = W["f2w"]
        block = ctx.enter_context(nc.Block())

        @block.gpsimd
        def _(pool):
            nc.gpsimd.memset(h2[:, T:TP], 0.0).then_inc(pad_set, 1)

        @block.vector
        def _(dve):
            chain = Chain(dve, dve_done)
            wait_weights(dve, "ffn2")
            for l in range(2):
                shared_w = W["f2ws"][:, l].rearrange("p (a o) -> p a o", a=1).broadcast_to([P, 16, P])
                eye = ident[:].rearrange("p (a o) -> p a o", a=1).broadcast_to([P, 16, P])
                chain.step(nc.vector.tensor_tensor(ww[:, l, :, 0:P], ww[:, l, :, 0:P], shared_w, ALU.add))
                chain.step(nc.vector.tensor_tensor(ww[:, l, :, 0:P], ww[:, l, :, 0:P], eye, ALU.add))
                chain.step(nc.vector.tensor_scalar(ww[:, l, :, P], W["f2br"][:, l], W["f2bs"][:, l:l + 1], None, ALU.add))
            dve.sem_inc(two_read, 2)
            with dve.Fori(0, IMAGES // 2) as i:
                for q in range(2):
                    e = dve.value_load(route[0:1, ds(i * 2 + q, 1)], min_val=0, max_val=15)
                    dve.wait_ge(two_read, i * 2 + (q + 1))
                    dve.sem_inc(dve_passed, 1)
                    for l in range(2):
                        ins = nc.vector.tensor_copy(mine[q][l][:], ww[:, l, ds(e, 1), :].rearrange("p a o -> p (a o)"))
                    ins.then_inc(staged, 1)

        @block.tensor
        def _(pe):
            wait_weights(pe, "ffn2")
            for c, (start, n) in enumerate(CHUNKS):
                if c >= 2:
                    pe.wait_ge(in_read, c - 1)
                nc.tensor.matmul(bank(c % 2)[:, 0:n], W["f2wi"][:], feat[:, start:start + n],
                                 start=True, stop=True).then_inc(in_done, 1)
            pe.wait_ge(in_read, len(CHUNKS))
            with pe.Fori(0, IMAGES // 2) as i:
                for q in range(2):
                    pe.wait_ge(staged, i * 2 + (q + 1))
                    pe.sem_inc(passed, 1)
                    nc.tensor.matmul(bank(2 + q)[:, 0:S], mine[q][0][:, 0:P], h0[:, ds(i * (2 * S) + q * S, S)],
                                     start=True, stop=True).then_inc(one_done, 1)
                for q in range(2):
                    pe.wait_ge(one_read, i * 2 + (q + 1))
                    nc.tensor.matmul(bank(4 + q)[:, 0:S], mine[q][1][:, 0:P], h1[q][:], start=True, stop=True).then_inc(two_done, 1)
            pe.wait_ge(two_read, IMAGES + 2)
            pe.wait_ge(pad_set, 1)
            close_block(pe, z, lambda t: [(h2[:, t * P:(t + 1) * P], W["f2wo"][:])], W["f2bo"][:]).then_inc(z_done, 1)

        @block.scalar
        def _(act):
            wait_weights(act, "ffn2")
            for c, (start, n) in enumerate(CHUNKS):
                act.wait_ge(in_done, c + 1)
                nc.scalar.activation(h0[:, start:start + n], bank(c % 2)[:, 0:n], ACT.Relu,
                                     bias=W["f2bi"][:, 0:1]).then_inc(in_read, 1)
            with act.Fori(0, IMAGES // 2) as i:
                for q in range(2):
                    act.wait_ge(one_done, i * 2 + (q + 1))
                    nc.scalar.activation(h1[q][:], bank(2 + q)[:, 0:S], ACT.Relu,
                                         bias=mine[q][0][:, P:P + 1]).then_inc(one_read, 1)
                for q in range(2):
                    act.wait_ge(two_done, i * 2 + (q + 1))
                    act.sem_inc(dve_passed, 1)
                    nc.scalar.activation(h2[:, ds(i * (2 * S) + q * S, S)], bank(4 + q)[:, 0:S], ACT.Relu,
                                         bias=mine[q][1][:, P:P + 1]).then_inc(two_read, 1)

        ctx.close()
        norm("n2f_", z)
    def heads3():
        ctx = ExitStack()
        local = lambda name, shape, dt=F32: sb(name, shape, dt, ctx)
        mark = lambda name: sem(name, ctx)
        H, HALF = 8, 64
        wkq, wvo = local("wkq", [P, H, D]), local("wvo", [P, 2, H // 2, D])
        x = [local("x%d" % q, [P, 2, HALF]) for q in range(2)]
        keys = [local("keys%d" % q, [P, H, 2, HALF]) for q in range(2)]
        values = [local("values%d" % q, [P, 2, H // 2 * D]) for q in range(2)]
        prob = [local("prob%d" % q, [P, H, HALF]) for q in range(2)]
        probT = [local("probT%d" % q, [P, H // 2, 2, HALF]) for q in range(2)]
        high, total = [local("high3_%d" % q, [P, H]) for q in range(2)], [local("total3_%d" % q, [P, H]) for q in range(2)]
        mixT = local("mixT3", [P, TP])
        (w_done, w_copied, ready, x_ready, k_done, k_copied, s_done, v_done, v_copied, exp_wanted, exp_given, p_ready,
         pT_done, pT_copied, o_done, o_read, dve_done, z_done, p_used, dve_passed, pe_passed) = (mark(n) for n in (
             "w_done", "w_copied", "ready", "x_ready", "k_done", "k_copied", "s_done", "v_done", "v_copied", "exp_wanted",
             "exp_given", "p_ready", "pT_done", "pT_copied", "o_done", "o_read", "dve_done", "z_done", "p_used", "dve_passed",
             "pe_passed"))
        z = psum[:, 0:TILES * D]
        PAIRS = IMAGES // 2
        LOOPS = (PAIRS - 4) // 2
        block = ctx.enter_context(nc.Block())

        @block.gpsimd
        def _(pool):
            for q in range(2):
                nc.gpsimd.memset(x[q][:], 0.0).then_inc(ready, 1)
                nc.gpsimd.memset(prob[q][:], 0.0).then_inc(ready, 1)
            pool.wait_ge(ready, 4)
            for half in (keys[0], keys[1], wkq, wvo, mixT):
                nc.gpsimd.memset(half[D:P], 0.0).then_inc(ready, 1)
            pool.wait_ge(ready, 9)
            nc.gpsimd.memset(mixT[0:D, T:TP], 0.0).then_inc(ready, 1)

        @block.tensor
        def _(pe):
            wait_weights(pe, "attn3")
            for h in range(H):
                nc.tensor.matmul(bank(0)[0:D, h * D:(h + 1) * D], W["a3k"][:, h], W["a3q"][:, h], start=True, stop=True)
                mm = nc.tensor.matmul(bank(1)[0:D, (h % 2 * 4 + h // 2) * D:(h % 2 * 4 + h // 2 + 1) * D], W["a3k"][:, h],
                                      W["a3o"][:, h], start=True, stop=True)
            mm.then_inc(w_done, 1)
            pe.wait_ge(w_copied, 2)
            pe.wait_ge(ready, 10)

            def keys_of(q, n1):
                pe.wait_ge(x_ready, n1)
                pe.sem_inc(pe_passed, 1)
                for h in range(H):
                    mm = nc.tensor.matmul(bank(h // 4)[0:D, (h % 4) * P:(h % 4 + 1) * P], wkq[:, h],
                                          x[q][:].rearrange("d b s -> d (b s)"), start=True, stop=True)
                mm.then_inc(k_done, 1)

            def values_and_scores(q, n1):
                for b in range(2):
                    for s in range(2):
                        mm = nc.tensor.matmul(bank(2)[s * HALF:(s + 1) * HALF, b * 256:(b + 1) * 256], x[q][:, b],
                                              wvo[:, s].rearrange("d h o -> d (h o)"), start=True, stop=True)
                mm.then_inc(v_done, 1)
                pe.wait_ge(k_copied, n1)
                pe.sem_inc(pe_passed, 1)
                for b in range(2):
                    mm = nc.tensor.matmul(bank(3 + q)[b * HALF:(b + 1) * HALF, 0:H * S], x[q][:, b], keys[q][:, :, b, 0:S],
                                          start=True, stop=True)
                mm.then_inc(s_done, 1)

            def turn_probs(q, n1):
                pe.wait_ge(p_ready, n1)
                for k in range(H // 2):
                    mm = nc.tensor.transpose(bank(5)[:, k * P:(k + 1) * P],
                                             prob[q][:, 2 * k:2 * k + 2].rearrange("p h s -> p (h s)"), ident[:])
                mm.then_inc(pT_done, 1)

            def mix(q, n1):
                pe.wait_ge(pT_copied, n1)
                pe.wait_ge(v_copied, n1)
                pe.wait_ge(o_read, n1)
                pe.sem_inc(pe_passed, 1)
                for b in range(2):
                    for k in range(H // 2):
                        mm = nc.tensor.matmul(bank(6 + q)[0:D, b * S:(b + 1) * S], values[q][:, b, k * D:(k + 1) * D],
                                              probT[q][:, k, b, 0:S], start=(k == 0), stop=(k == H // 2 - 1))
                mm.then_inc(o_done, 1)

            def pair(q, n1, more=True):
                if more:
                    keys_of(1 - q, n1 + 1)
                turn_probs(q, n1)
                if more:
                    values_and_scores(1 - q, n1 + 1)
                mix(q, n1)

            keys_of(0, 1)
            values_and_scores(0, 1)
            pair(0, 1)
            with pe.Fori(0, LOOPS) as i:
                for q in (1, 0):
                    pair(q, i * 2 + (3 - q))
            for n in range(1 + 2 * LOOPS, PAIRS):
                pair(n % 2, n + 1, n < PAIRS - 1)
            pe.wait_ge(o_read, PAIRS + 2)
            close_block(pe, z, lambda t: [(mixT[:, t * P:(t + 1) * P], ident[:, 0:D])]).then_inc(z_done, 1)

        @block.scalar
        def _(act):
            act.wait_ge(w_done, 1)
            nc.scalar.copy(wkq[0:D].rearrange("d h e -> d (h e)"), bank(0)[0:D, :]).then_inc(w_copied, 1)
            nc.scalar.copy(wvo[0:D].rearrange("d s h e -> d (s h e)"), bank(1)[0:D, :]).then_inc(w_copied, 1)

            def keys_of(q, n1):
                act.wait_ge(k_done, n1)
                nc.scalar.copy(keys[q][0:D].rearrange("d h b s -> d (h b s)"), bank(0, 2)[0:D, :]).then_inc(k_copied, 1)

            def values_of(q, n1):
                act.wait_ge(v_done, n1)
                nc.scalar.copy(values[q][:].rearrange("p b o -> p (b o)"), bank(2)).then_inc(v_copied, 1)

            def pair(q, n1, more=True):
                act.wait_ge(exp_wanted, n1)
                nc.scalar.activation(prob[q][:, :, 0:S], prob[q][:, :, 0:S], ACT.Exp, scale=D ** -0.5).then_inc(exp_given, 1)
                if more:
                    keys_of(1 - q, n1 + 1)
                act.wait_ge(pT_done, n1)
                nc.scalar.copy(probT[q][:].rearrange("p k b s -> p (k b s)"), bank(5)).then_inc(pT_copied, 1)
                if more:
                    values_of(1 - q, n1 + 1)

            keys_of(0, 1)
            values_of(0, 1)
            pair(0, 1)
            with act.Fori(0, LOOPS) as i:
                for q in (1, 0):
                    pair(q, i * 2 + (3 - q))
            for n in range(1 + 2 * LOOPS, PAIRS):
                pair(n % 2, n + 1, n < PAIRS - 1)

        @block.vector
        def _(dve):
            STEPS = 3
            dve.wait_ge(ready, 10)
            dve.sem_inc(o_read, 2)

            def stage(q, col):
                nc.vector.tensor_copy(x[q][0:D, :, 0:S], feat[0:D, ds(col, 2 * S)].rearrange(
                    "d (b s) -> d b s", s=S)).then_inc(x_ready, 1)

            def copy_mix(q, n1, col):
                dve.wait_ge(o_done, n1)
                dve.sem_inc(dve_passed, 1)
                nc.vector.tensor_copy(mixT[0:D, ds(col, 2 * S)], bank(6 + q)[0:D, 0:2 * S]).then_inc(o_read, 1)

            def pair(q, n1, steps_before, col, stages=True, copies=True):
                def step(ins, k):
                    ins.then_inc(dve_done, 1)
                    dve.wait_ge(dve_done, steps_before + k)

                s3 = bank(3 + q)[:, 0:H * S].rearrange("p (h s) -> p h s", s=S)
                wide = lambda v: v[q][:].rearrange("p (h a) -> p h a", a=1).broadcast_to([P, H, S])
                p3 = prob[q][:, :, 0:S]
                dve.wait_ge(s_done, n1)
                step(nc.vector.tensor_reduce(high[q][:], s3, AX.X, ALU.max), 1)
                nc.vector.tensor_tensor(p3, s3, wide(high), ALU.subtract).then_inc(exp_wanted, 1)
                if stages:
                    stage(q, col + 4 * S)
                if copies:
                    copy_mix(1 - q, n1 - 1, col - 2 * S)
                dve.wait_ge(exp_given, n1)
                step(nc.vector.tensor_reduce(total[q][:], p3, AX.X, ALU.add), 2)
                step(nc.vector.reciprocal(total[q][:], total[q][:]), 3)
                nc.vector.tensor_tensor(p3, p3, wide(total), ALU.mult).then_inc(p_ready, 1)

            stage(0, 0)
            stage(1, 2 * S)
            pair(0, 1, 0, 0, copies=False)
            with dve.Fori(0, LOOPS) as i:
                for q in (1, 0):
                    k = 2 - q
                    pair(q, i * 2 + (k + 1), i * (2 * STEPS) + k * STEPS, i * (4 * S) + k * 2 * S)
            for n in range(1 + 2 * LOOPS, PAIRS):
                pair(n % 2, n + 1, n * STEPS, n * 2 * S, stages=n + 2 < PAIRS)
            copy_mix((PAIRS - 1) % 2, PAIRS, (PAIRS - 1) * 2 * S)

        ctx.close()
        norm("n3a_", z)

    def experts3():
        ctx = ExitStack()
        z = sb("z3", [P, TILES, D], F32, ctx)
        inner = ExitStack()
        mark1 = lambda name: sem(name, inner)
        score = sb("score3", [P, TILES, 8], F32, inner)
        g_done, exp_wanted, exp_given, dve_done = (mark1(n) for n in ("g_done3", "exp_wanted3", "exp_given3", "dve_done3"))
        shared = {}
        block = inner.enter_context(nc.Block())

        @block.tensor
        def _(pe):
            wait_weights(pe, "ffn3")
            for t in range(TILES):
                g = bank(6)[:, t * 8:(t + 1) * 8]
                mm = nc.tensor.matmul(g, feat[:, t * P:(t + 1) * P], W["f3wg"], start=True, stop=True)
            mm.then_inc(g_done, 1)

        @block.vector
        def _(dve):
            chain = Chain(dve, dve_done)
            dve.wait_ge(g_done, 1)
            chain.step(nc.vector.tensor_copy(score[:], bank(6)[:, 0:TILES * 8].rearrange("p (t e) -> p t e", e=8)))
            gap, finish = top_two(chain, "g3", inner, score[:], 8, exp_wanted, exp_given)
            shared["gap"] = gap
            chain.step(finish())

        @block.scalar
        def _(act):
            act.wait_ge(exp_wanted, 1)
            nc.scalar.activation(shared["gap"][:], shared["gap"][:], ACT.Exp).then_inc(exp_given, 1)

        inner.close()
        experts("e3_", "ffn3", 8, 2, W["f3w1"], W["f3b1"], W["f3w2"], W["f3b2"], z)
        norm("n3f_", z[:].rearrange("p t f -> p (t f)"))
        ctx.close()

    STAGES = [[tokens_and_keys], [attention0], [graph_gates, experts0], [recurrent1], [single_expert1], [regrouped2], [routed2], [heads3], [experts3]]

    for stages in STAGES[:stop + 1]:
        for stage in stages:
            stage()
            nc.clear_and_free_semaphores(stage_semaphores)
            nc.all_engine_barrier()
            stage_semaphores.clear()

    ctx = ExitStack()
    written = sem("written")
    block = ctx.enter_context(nc.Block())

    @block.sync
    def _(sp):
        rows_out = out.rearrange("b s d -> (b s) d")
        whole = T // P
        sp.dma_start(rows_out[0:whole * P].rearrange("(t p) d -> p t d", p=P), tok[:, 0:whole, :]).then_inc(written, 16)
        sp.dma_start(rows_out[whole * P:T], tok[0:T - whole * P, whole, :]).then_inc(written, 16)
        for part in loads:
            wait_weights(sp, part)
        sp.wait_ge(written, 32)

    ctx.close()
    top.close()


def laid_out(inputs):
    import numpy as np

    A = {k: np.asarray(v) for k, v in inputs.items() if k not in ("L3_attn_wv",)}
    for n in ("L0_attn_Wq", "L0_attn_Wk", "L0_attn_Wv", "L0_attn_Wo", "L2_attn_Wq", "L2_attn_Wk", "L2_attn_Wv",
              "L2_ffn_Wi", "L2_ffn_Wo", "L0_ffn_b1"):
        A[n] = A[n].T
    for n in ("L0_ffn_att_src", "L0_ffn_att_dst"):
        A[n] = A[n].reshape(16)
    A["L1_ffn_b1"] = A["L1_ffn_b1"].reshape(2, 128).T
    A["L3_ffn_b1"] = A["L3_ffn_b1"].reshape(16, 128).T
    A["L2_ffn_Wr"] = A["L2_ffn_Wr"].transpose(0, 1, 3, 2)
    A["L2_ffn_Ws"] = A["L2_ffn_Ws"][:, 0].transpose(0, 2, 1)
    A["L2_ffn_br"] = A["L2_ffn_br"].transpose(2, 0, 1)
    A["L2_ffn_bs"] = A["L2_ffn_bs"][:, 0].T
    A["L3_attn_wq"] = A["L3_attn_wq"].transpose(0, 2, 1)
    A["L3_attn_wk"] = A["L3_attn_wk"].transpose(0, 2, 1)
    return {k: np.ascontiguousarray(v) for k, v in A.items()}


def kernel(**inputs):
    import numpy as np
    import concourse.bacc as bacc
    from concourse import mybir
    from concourse.bass_utils import run_bass_kernel_spmd as run

    nc = bacc.Bacc("TRN2", target_bir_lowering=False, num_devices=1)
    arrays = laid_out(inputs)
    aps = {k: nc.dram_tensor("in_" + k, a.shape, mybir.dt.from_np(a.dtype), kind="ExternalInput").ap()
           for k, a in arrays.items()}
    out = nc.dram_tensor("out", (64, 51, 64), mybir.dt.float32, kind="ExternalOutput").ap()
    vit_tower(nc, aps, out, STOP)
    r = run(nc, [{"in_" + k: a for k, a in arrays.items()}], core_ids=[0])
    return r.results[0]["out"]


STOP = 99
```
